# Optimizing a Trainium2 kernel written in Bass

```python
import numpy as np
import jax
import jax.numpy as jnp

def _softmax(x, axis=-1):
    return jax.nn.softmax(x, axis=axis)

def _gelu(x):
    return jax.nn.gelu(x, approximate=True)

def _silu(x):
    return jax.nn.silu(x)

def _sigmoid(x):
    return jax.nn.sigmoid(x)

def _layernorm(x, axis=-1, eps=1e-05):
    m = jnp.mean(x, axis=axis, keepdims=True)
    v = jnp.var(x, axis=axis, keepdims=True)
    return (x - m) / jnp.sqrt(v + eps)

def _scatter_add(tgt, idx, src, axis=0):
    return tgt.at[idx].add(src)

def _segment_sum(src, seg, n):
    return jax.ops.segment_sum(src, seg, n)
kernel_name = 'mk_lm_tower_d1_tok_ids768_r4_a6b71e'

def setup_inputs(seed: int=0):
    np.random.seed(seed)
    _w = jnp.asarray

    def _rec_inputs():
        import jax
        import jax.numpy as jnp
        _rk = jax.random.key(seed)
        x = jax.random.randint(jax.random.fold_in(_rk, 1), (8, 256), 0, 8000, jnp.int32)
        return x
    x = _rec_inputs()

    def _L0_tok_setup():
        import jax, jax.numpy as jnp
        import numpy as np
        V, S, D, H = (8000, 256, 192, 768)
        EPS = 1e-05

        def pos_encoding(seq_len, dim, dtype=jnp.float32):
            pos = jnp.arange(seq_len, dtype=dtype)[:, None]
            i = jnp.arange(dim, dtype=dtype)[None, :]
            ang = pos / jnp.power(jnp.asarray(10000.0, dtype), i / dim)
            even = (jnp.arange(dim) % 2 == 0)[None, :]
            return jnp.where(even, jnp.sin(ang), jnp.cos(ang))

        def layernorm2d(x, w, b):
            m = jnp.mean(x, axis=(-2, -1), keepdims=True)
            v = jnp.mean((x - m) ** 2, axis=(-2, -1), keepdims=True)
            return (x - m) / jnp.sqrt(v + EPS) * w + b
        key = jax.random.key(seed)
        ks = jax.random.split(key, 16)
        sc = 0.02
        emb = jax.random.normal(ks[0], (V, D), jnp.float32) * sc
        emb = emb.at[0].set(0.0)
        inp = {'x': jax.random.randint(ks[1], (8, S), 0, V), 'emb': emb, 'Wq': jax.random.normal(ks[2], (D, H), jnp.float32) * sc, 'bq': jnp.zeros((H,), jnp.float32), 'Wk': jax.random.normal(ks[3], (D, H), jnp.float32) * sc, 'bk': jnp.zeros((H,), jnp.float32), 'Wv': jax.random.normal(ks[4], (D, H), jnp.float32) * sc, 'bv': jnp.zeros((H,), jnp.float32), 'Wo': jax.random.normal(ks[5], (H, D), jnp.float32) * sc, 'bo': jnp.zeros((D,), jnp.float32), 'W1': jax.random.normal(ks[6], (D, H), jnp.float32) * sc, 'b1': jnp.zeros((H,), jnp.float32), 'W2': jax.random.normal(ks[7], (H, D), jnp.float32) * sc, 'b2': jnp.zeros((D,), jnp.float32), 'ln1_w': jnp.ones((S, D), jnp.float32), 'ln1_b': jnp.zeros((S, D), jnp.float32), 'ln2_w': jnp.ones((S, D), jnp.float32), 'ln2_b': jnp.zeros((S, D), jnp.float32)}
        return inp
    _L0_tok_all = _L0_tok_setup()
    _L0_tok_in = {k: v for k, v in _L0_tok_all.items() if k in ('emb', 'Wq', 'bq', 'Wk', 'bk', 'Wv', 'bv', 'Wo', 'bo', 'W1', 'b1', 'W2', 'b2', 'ln1_w', 'ln1_b', 'ln2_w', 'ln2_b')}
    del _L0_tok_all

    def _L0_attn_setup():
        import jax, jax.numpy as jnp
        import numpy as np
        import math
        D_MODEL = 192
        N_HEADS = 12
        HEAD_DIM = D_MODEL // N_HEADS
        B, T = (2, 512)
        key = jax.random.key(seed)
        k1, k2, k3 = jax.random.split(key, 3)
        x = jax.random.normal(k1, (B, T, D_MODEL), dtype=jnp.float32)
        W_qkv = jax.random.normal(k2, (3 * D_MODEL, D_MODEL), dtype=jnp.float32) * (1.0 / math.sqrt(D_MODEL))
        W_proj = jax.random.normal(k3, (D_MODEL, D_MODEL), dtype=jnp.float32) * (1.0 / math.sqrt(D_MODEL))
        return {'x': x, 'W_qkv': W_qkv, 'W_proj': W_proj}
    _L0_attn_all = _L0_attn_setup()
    _L0_attn_in = {k: v for k, v in _L0_attn_all.items() if k in ('W_qkv', 'W_proj')}
    del _L0_attn_all

    def _L0_ffn_setup():
        import jax, jax.numpy as jnp
        import numpy as np
        DIM = 192
        NUM_EXPERTS = 4
        NUM_HEADS = 12
        HEAD_DIM = DIM // NUM_HEADS
        MLP_HID = 4 * DIM
        FC1_OUT = MLP_HID + 3 * DIM
        FC2_IN = MLP_HID + DIM
        FC2_OUT = 2 * DIM
        CAP_FACTOR = 0.5
        LN_EPS = 1e-06
        key = jax.random.key(seed)
        ks = jax.random.split(key, 4)
        B, N = (8, 256)
        return {'x': jax.random.normal(ks[0], (B, N, DIM), jnp.float32), 'w_router': jax.random.normal(ks[1], (NUM_EXPERTS, DIM), jnp.float32) * 0.02, 'gamma1': jnp.ones((DIM,), jnp.float32), 'beta1': jnp.zeros((DIM,), jnp.float32), 'w1': jax.random.normal(ks[2], (FC1_OUT, DIM), jnp.float32) * 0.02, 'b1': jnp.zeros((FC1_OUT,), jnp.float32), 'w2': jax.random.normal(ks[3], (FC2_OUT, FC2_IN), jnp.float32) * 0.02, 'b2': jnp.zeros((FC2_OUT,), jnp.float32)}
    _L0_ffn_all = _L0_ffn_setup()
    _L0_ffn_in = {k: v for k, v in _L0_ffn_all.items() if k in ('w_router', 'gamma1', 'beta1', 'w1', 'b1', 'w2', 'b2')}
    del _L0_ffn_all
    return {'x': x, 'L0_tok_emb': _L0_tok_in['emb'], 'L0_tok_Wq': _L0_tok_in['Wq'], 'L0_tok_bq': _L0_tok_in['bq'], 'L0_tok_Wk': _L0_tok_in['Wk'], 'L0_tok_bk': _L0_tok_in['bk'], 'L0_tok_Wv': _L0_tok_in['Wv'], 'L0_tok_bv': _L0_tok_in['bv'], 'L0_tok_Wo': _L0_tok_in['Wo'], 'L0_tok_bo': _L0_tok_in['bo'], 'L0_tok_W1': _L0_tok_in['W1'], 'L0_tok_b1': _L0_tok_in['b1'], 'L0_tok_W2': _L0_tok_in['W2'], 'L0_tok_b2': _L0_tok_in['b2'], 'L0_tok_ln1_w': _L0_tok_in['ln1_w'], 'L0_tok_ln1_b': _L0_tok_in['ln1_b'], 'L0_tok_ln2_w': _L0_tok_in['ln2_w'], 'L0_tok_ln2_b': _L0_tok_in['ln2_b'], 'L0_attn_W_qkv': _L0_attn_in['W_qkv'], 'L0_attn_W_proj': _L0_attn_in['W_proj'], 'L0_ffn_w_router': _L0_ffn_in['w_router'], 'L0_ffn_gamma1': _L0_ffn_in['gamma1'], 'L0_ffn_beta1': _L0_ffn_in['beta1'], 'L0_ffn_w1': _L0_ffn_in['w1'], 'L0_ffn_b1': _L0_ffn_in['b1'], 'L0_ffn_w2': _L0_ffn_in['w2'], 'L0_ffn_b2': _L0_ffn_in['b2']}

def reference(x, L0_tok_emb, L0_tok_Wq, L0_tok_bq, L0_tok_Wk, L0_tok_bk, L0_tok_Wv, L0_tok_bv, L0_tok_Wo, L0_tok_bo, L0_tok_W1, L0_tok_b1, L0_tok_W2, L0_tok_b2, L0_tok_ln1_w, L0_tok_ln1_b, L0_tok_ln2_w, L0_tok_ln2_b, L0_attn_W_qkv, L0_attn_W_proj, L0_ffn_w_router, L0_ffn_gamma1, L0_ffn_beta1, L0_ffn_w1, L0_ffn_b1, L0_ffn_w2, L0_ffn_b2):
    import jax
    import jax.numpy as jnp

    def _L0_tok_ref(x, emb, Wq, bq, Wk, bk, Wv, bv, Wo, bo, W1, b1, W2, b2, ln1_w, ln1_b, ln2_w, ln2_b):
        import jax, jax.numpy as jnp
        import numpy as np
        V, S, D, H = (8000, 256, 192, 768)
        EPS = 1e-05

        def pos_encoding(seq_len, dim, dtype=jnp.float32):
            pos = jnp.arange(seq_len, dtype=dtype)[:, None]
            i = jnp.arange(dim, dtype=dtype)[None, :]
            ang = pos / jnp.power(jnp.asarray(10000.0, dtype), i / dim)
            even = (jnp.arange(dim) % 2 == 0)[None, :]
            return jnp.where(even, jnp.sin(ang), jnp.cos(ang))

        def layernorm2d(x, w, b):
            m = jnp.mean(x, axis=(-2, -1), keepdims=True)
            v = jnp.mean((x - m) ** 2, axis=(-2, -1), keepdims=True)
            return (x - m) / jnp.sqrt(v + EPS) * w + b
        y = emb[x]
        y = y + pos_encoding(y.shape[1], y.shape[2], y.dtype)
        q = y @ Wq + bq
        k = y @ Wk + bk
        v = y @ Wv + bv
        attn = jax.nn.softmax(jnp.einsum('bsh,bth->bst', q, k), axis=-1)
        a = jnp.einsum('bst,bth->bsh', attn, v) @ Wo + bo
        y = layernorm2d(y + a, ln1_w, ln1_b)
        f = jax.nn.gelu((y @ W1 + b1) @ W2 + b2, approximate=False)
        y = layernorm2d(y + f, ln2_w, ln2_b)
        return y

    def _L0_attn_ref(x, W_qkv, W_proj):
        import jax, jax.numpy as jnp
        import numpy as np
        import math
        D_MODEL = 192
        N_HEADS = 12
        HEAD_DIM = D_MODEL // N_HEADS
        B, T = (2, 512)
        Bx, Tx, C = x.shape
        qkv = x @ W_qkv.T
        q, k, v = jnp.split(qkv, 3, axis=-1)
        q = q.reshape(Bx, Tx, N_HEADS, HEAD_DIM).transpose(0, 2, 1, 3)
        k = k.reshape(Bx, Tx, N_HEADS, HEAD_DIM).transpose(0, 2, 1, 3)
        v = v.reshape(Bx, Tx, N_HEADS, HEAD_DIM).transpose(0, 2, 1, 3)
        scale = 1.0 / math.sqrt(HEAD_DIM)
        att = jnp.einsum('bhqd,bhkd->bhqk', q, k) * scale
        causal = jnp.tril(jnp.ones((Tx, Tx), dtype=bool))
        att = jnp.where(causal[None, None, :, :], att, -jnp.inf)
        att_probs = jax.nn.softmax(att, axis=-1)
        out = jnp.einsum('bhqk,bhkd->bhqd', att_probs, v)
        out = out.transpose(0, 2, 1, 3).reshape(Bx, Tx, C)
        return out @ W_proj.T

    def _L0_ffn_ref(x, w_router, gamma1, beta1, w1, b1, w2, b2):
        import jax, jax.numpy as jnp
        import numpy as np
        DIM = 192
        NUM_EXPERTS = 4
        NUM_HEADS = 12
        HEAD_DIM = DIM // NUM_HEADS
        MLP_HID = 4 * DIM
        FC1_OUT = MLP_HID + 3 * DIM
        FC2_IN = MLP_HID + DIM
        FC2_OUT = 2 * DIM
        CAP_FACTOR = 0.5
        LN_EPS = 1e-06
        B, N, C = x.shape
        E = NUM_EXPERTS
        cap = int(CAP_FACTOR * N)
        m = np.array([C // 2 ** (E - 1 - e) for e in range(E)])
        in_mask = (np.arange(C)[None, :] < m[:, None]).astype(np.float32)
        in_mask = jnp.asarray(in_mask)
        out_mask = jnp.concatenate([in_mask, in_mask], axis=-1)
        logits = jnp.einsum('bnc,ec->bne', x, w_router)
        probs = jax.nn.softmax(logits, axis=-1)
        gate, idx = jax.lax.top_k(jnp.swapaxes(probs, 1, 2), cap)
        dispatch = jax.nn.one_hot(idx, N, dtype=x.dtype)
        combine = dispatch * gate[..., None]
        mu = jnp.mean(x, -1, keepdims=True)
        var = jnp.var(x, -1, keepdims=True)
        y = (x - mu) * jax.lax.rsqrt(var + LN_EPS) * gamma1 + beta1
        xg = jnp.einsum('becn,bnd->becd', dispatch, y)
        xg = xg * in_mask[None, :, None, :]
        h = jnp.einsum('becd,fd->becf', xg, w1) + b1
        h = jnp.einsum('becn,becf->bnf', dispatch, h)
        x_mlp, x_qkv = (h[..., :MLP_HID], h[..., MLP_HID:])
        qkv = x_qkv.reshape(B, N, 3, NUM_HEADS, HEAD_DIM).transpose(2, 0, 3, 1, 4)
        q, k, v = (qkv[0], qkv[1], qkv[2])
        scale = HEAD_DIM ** (-0.5)
        attn = jax.nn.softmax(jnp.einsum('bhqd,bhkd->bhqk', q, k) * scale, axis=-1)
        x_attn = jnp.einsum('bhqk,bhkd->bhqd', attn, v)
        x_attn = x_attn.transpose(0, 2, 1, 3).reshape(B, N, C)
        x_mlp = jax.nn.gelu(x_mlp, approximate=False)
        y2 = jnp.concatenate([x_mlp, x_attn], axis=-1)
        yg = jnp.einsum('becn,bnf->becf', dispatch, y2)
        o = jnp.einsum('becf,of->beco', yg, w2) + b2
        o = o * out_mask[None, :, None, :]
        z = jnp.einsum('becn,beco->bno', combine, o)
        x_mlp2, x_attn2 = (z[..., :C], z[..., C:])
        return x + x_mlp2 + x_attn2
    h = _L0_tok_ref(x, L0_tok_emb, L0_tok_Wq, L0_tok_bq, L0_tok_Wk, L0_tok_bk, L0_tok_Wv, L0_tok_bv, L0_tok_Wo, L0_tok_bo, L0_tok_W1, L0_tok_b1, L0_tok_W2, L0_tok_b2, L0_tok_ln1_w, L0_tok_ln1_b, L0_tok_ln2_w, L0_tok_ln2_b)
    h = h + _L0_attn_ref(_layernorm(h, axis=-1), L0_attn_W_qkv, L0_attn_W_proj)
    h = h + _L0_ffn_ref(_layernorm(h, axis=-1), L0_ffn_w_router, L0_ffn_gamma1, L0_ffn_beta1, L0_ffn_w1, L0_ffn_b1, L0_ffn_w2, L0_ffn_b2)
    return h

_drawn_inputs = setup_inputs


def setup_inputs(seed=0):
    import zlib

    import numpy as np

    out = dict(_drawn_inputs(seed))
    spreads = {'L0_tok_bq': (0.0, 0.8),
     'L0_tok_bk': (0.0, 2.0),
     'L0_tok_bv': (0.0, 0.1),
     'L0_tok_bo': (0.0, 0.1),
     'L0_tok_b1': (0.0, 0.28),
     'L0_tok_b2': (0.0, 0.1),
     'L0_tok_ln1_w': (1.0, 0.2),
     'L0_tok_ln1_b': (0.0, 0.1),
     'L0_tok_ln2_w': (1.0, 0.2),
     'L0_tok_ln2_b': (0.0, 0.1),
     'L0_ffn_gamma1': (1.0, 0.6),
     'L0_ffn_beta1': (0.0, 2.0),
     'L0_ffn_b1': (0.0, 0.425),
     'L0_ffn_b2': (0.0, 0.43)}
    factors = {'L0_tok_Wq': 2.891}
    for name, (base, spread) in spreads.items():
        noise = np.random.default_rng([zlib.crc32(name.encode()), seed]).standard_normal(out[name].shape)
        drawn = base * np.exp(spread * noise) if base else spread * noise
        out[name] = jnp.asarray(drawn.astype(out[name].dtype))
    for name, factor in factors.items():
        out[name] = (out[name] * factor).astype(out[name].dtype)
    return out
```

```python
from contextlib import ExitStack

import concourse.bass as bass
from concourse import mybir

F32 = mybir.dt.float32
F16 = mybir.dt.float16
BF16 = mybir.dt.bfloat16
U32 = mybir.dt.uint32
I32 = mybir.dt.int32
ALU = mybir.AluOpType
ACT = mybir.ActivationFunctionType
AX = mybir.AxisListType

P = 128
SEQS, TOKENS, DIM, HIDDEN = 8, 256, 192, 768
HALVES = TOKENS // P
VOCAB = 8000
CH = DIM // 2
HT = HIDDEN // P
HEADS, HD = 12, 16
GROUPS = HEADS // 4
SLOT = 64
EXPERTS = 4
CAP = TOKENS // 2
REGIONS = [(0, DIM // 8), (DIM // 8, DIM // 4), (DIM // 4, DIM // 2), (DIM // 2, DIM)]
BANK = 512
QKV = 3 * DIM
FC1 = HIDDEN + QKV
SCALE = HD ** -0.5
EPS_TOK, EPS_ROW, EPS_FFN = 1e-5, 1e-5, 1e-6
MASKED = -1e30
AHEAD = 2


class Signal:

    def __init__(self, sem, per_seq):
        self.sem, self.per_seq = sem, per_seq

    def done(self, seq, count=None):
        return seq * self.per_seq + (AHEAD * self.per_seq + (self.per_seq if count is None else count))

    def freed(self, seq, count=None):
        return seq * self.per_seq + (self.per_seq if count is None else count)


def build(nc, d):
    with ExitStack() as ctx:
        def sb(name, shape, dt=F32):
            return ctx.enter_context(nc.sbuf_tensor(name, shape, dt))

        signals = []

        def sig(name, per_seq=1):
            s = Signal(ctx.enter_context(nc.semaphore(name)), per_seq)
            signals.append(s)
            return s

        def sem(name):
            return ctx.enter_context(nc.semaphore(name))

        PS = ctx.enter_context(nc.psum_tensor("PS", [P, 8 * BANK], F32))

        def bank(b, n=1):
            return PS[:, b * BANK:(b + n) * BANK]

        idx = sb("idx", [P, SEQS * HALVES], I32)
        pos = sb("pos", [P, HALVES, DIM])
        ident = sb("ident", [P, P])
        ident16 = sb("ident16", [P, P], F16)
        identb = sb("identb", [P, P], BF16)
        maskf = sb("maskf", [P, P])
        maskb = sb("maskb", [P, 4, P], BF16)
        mean_of = sb("mean_of", [P, P])
        half_neg = sb("half_neg", [P, 2])
        fold = sb("fold", [P, 4 * HT * (DIM + 1) + 2 * HT * DIM])
        fold_l = fold[:, 0:4 * HT * (DIM + 1)].rearrange("p (a k c) -> p a k c", a=4, k=HT)
        fold_r = fold[:, 4 * HT * (DIM + 1):].rearrange("p (a k c) -> p a k c", a=2, k=HT)
        bias_r = sb("bias_r", [1, 2, DIM])
        e_last = sb("e_last", [1, DIM + 1])
        Aw = sb("Aw", [CH + 1, 2, DIM + 1])
        VO = sb("VO", [CH + 1, 2, DIM])
        W12 = sb("W12", [CH + 1, 2, DIM])
        ln1w = sb("ln1w", [P, HALVES, DIM])
        ln1b = sb("ln1b", [P, HALVES, DIM])
        ln2w = sb("ln2w", [P, HALVES, DIM])
        ln2b = sb("ln2b", [P, HALVES, DIM])
        wqkv = sb("wqkv", [CH, 2, QKV])
        wproj = sb("wproj", [P, GROUPS, DIM])
        wrout = sb("wrout", [CH, 2, EXPERTS])
        w1 = sb("w1", [CH + 1, 2, FC1])
        free_at = SEQS * HALVES * DIM
        w2ab = fold[:, free_at:free_at + 2 * (HT + GROUPS) * DIM].rearrange("p (a k c) -> p a k c", a=2, k=HT + GROUPS)
        w2 = sb("w2", [P, HT + GROUPS, DIM])
        b2ab = sb("b2ab", [P, 2, DIM])
        b2 = sb("b2", [P, HALVES, DIM])
        gamma = sb("gamma", [P, 1, DIM])
        beta = sb("beta", [P, 1, DIM])

        EMB = sb("EMB", [P, SEQS * HALVES, DIM])
        H = sb("H", [P, SEQS * HALVES, DIM])
        X3 = EMB
        BASE = fold[:, 0:SEQS * HALVES * DIM].rearrange("p (t c) -> p t c", c=DIM)
        LG = sb("LG", [P, HALVES, SEQS, EXPERTS])

        def two(name, shape, dt=F32):
            return [sb(f"{name}{s}", shape, dt) for s in range(2)]

        PTf = two("PT", [P, HEADS * 2 * TOKENS])
        at = [0, 0]

        def carve(shape):
            size = shape[1] * shape[2]
            out = []
            for s in range(2):
                out.append(PTf[s][0:shape[0], at[s]:at[s] + size].rearrange("p (a b) -> p a b", a=shape[1]))
                at[s] += size
            return out

        ys = carve([P, HALVES, DIM + 1])
        yT = carve([CH + 1, 2, TOKENS])
        q2 = carve([CH + 1, 2, TOKENS])
        vp = carve([P, HALVES, DIM])
        nm = two("nm", [P, HALVES])
        pr = carve([P, HALVES, TOKENS])
        rs = two("rs", [P, HALVES])
        ri = two("ri", [P, HALVES])
        pT = carve([P, HALVES, TOKENS])
        r1 = carve([P, HALVES, DIM])
        y1 = carve([P, HALVES, DIM + 1])
        y1T = carve([CH + 1, 2, TOKENS])
        g1 = carve([P, HALVES, DIM])
        r2 = carve([P, HALVES, DIM])
        bs = two("bs", [P, 2, 6])
        mv = two("mv", [P, 2])
        st = two("st", [P, 4])
        bs2 = two("bs2", [P, 2, 6])
        mv2 = two("mv2", [P, 2])
        st2 = two("st2", [P, 4])

        xs = two("xs", [P, HALVES, DIM + 1])
        rv = two("rv", [P, HALVES, 2])
        rstd = two("rstd", [P, HALVES])
        bsr = two("bsr", [P, HALVES, 6])
        xT = two("xT", [CH + 1, 2, TOKENS])
        QS = two("QS", [P, HALVES, 2 * HEADS, SLOT], F16)
        VA = two("VA", [P, HALVES, HEADS, 2 * HD])
        QT = two("QT", [P, HEADS, TOKENS], F16)
        PT = [t[:].rearrange("p (h c) -> p h c", h=HEADS) for t in PTf]
        SM = two("SM", [P, GROUPS, TOKENS])
        OT = two("OT", [P, GROUPS, TOKENS])
        h2 = two("h2", [P, HALVES, DIM])
        x3 = two("x3", [P, HALVES, DIM])
        x3T = two("x3T", [CH, 2, TOKENS])
        rv3 = two("rv3", [P, HALVES, 2])
        rstd3 = two("rstd3", [P, HALVES])
        bsr3 = two("bsr3", [P, HALVES, 6])
        hid = [fold[:, free_at + s * HT * TOKENS:free_at + (s + 1) * HT * TOKENS].rearrange("p (k t) -> p k t", k=HT) for s in range(2)]
        z = h2

        lmax = sb("lmax", [P, HALVES, SEQS])
        lsum = sb("lsum", [P, HALVES, SEQS])
        lsub = sb("lsub", [P, HALVES, SEQS, EXPERTS])
        lexp = sb("lexp", [P, HALVES, SEQS, EXPERTS])
        PR = sb("PR", [P, HALVES, SEQS, EXPERTS])
        tops = [x3T[i][0:SEQS * EXPERTS, 0, :] for i in range(2)]
        top8 = [sb(f"top8{i}", [SEQS * EXPERTS, 8]) for i in range(2)]
        chosen = x3T[0][0:SEQS * EXPERTS, 1, :]
        MS = sb("MS", [P, HALVES, SEQS, EXPERTS])
        GS = sb("GS", [P, HALVES, SEQS, EXPERTS])

        ld_idx, ld_pos, ld_const, ld_fold = sem("ld_idx"), sem("ld_pos"), sem("ld_const"), sem("ld_fold")
        ld_ln, ld_attn, ld_ffn = sem("ld_ln"), sem("ld_attn"), sem("ld_ffn")
        rows_in = sem("rows_in")
        consts_set, dve_consts = sem("consts_set"), sem("dve_consts")
        set_by_act = sem("set_by_act")
        fold_mm, fold_set = sem("fold_mm"), sem("fold_set")
        pre_ffn = sem("pre_ffn")
        out_dma = sem("out_dma")

        a_y, a_yT, a_yTs = sig("a_y"), sig("a_yT"), sig("a_yTs")
        a_q2, a_q2s, a_vp, a_vps = sig("a_q2"), sig("a_q2s"), sig("a_vp"), sig("a_vps")
        a_sc, a_max, a_exp, a_pT, a_pTs = sig("a_sc"), sig("a_max"), sig("a_exp", 2), sig("a_pT"), sig("a_pTs")
        a_ri, a_o, a_res, a_bn, a_ag, a_sq = sig("a_ri"), sig("a_o"), sig("a_res"), sig("a_bn"), sig("a_ag"), sig("a_sq")
        a_st, a_ss, a_nv, a_ve, a_rs, a_n, a_w, a_y1 = (sig(f"a_{x}") for x in ("st", "ss", "nv", "ve", "rs", "n", "w", "y1"))
        a_y1T, a_y1Ts, a_f, a_g, a_r2 = sig("a_y1T"), sig("a_y1Ts"), sig("a_f"), sig("a_g"), sig("a_r2")
        a_bn2, a_ag2, a_sq2, a_st2, a_ss2 = (sig(f"a_{x}") for x in ("bn2", "ag2", "sq2", "st2", "ss2"))
        a_nv2, a_ve2, a_rs2, a_n2, a_w2, a_h = (sig(f"a_{x}") for x in ("nv2", "ve2", "rs2", "n2", "w2", "h"))

        def head_signals(loop, chunks1, chunks2, own):
            names = {
                "bn": 1, "ag": 1, "ve": 1, "rs": 1, "x": 1, "xT": 1, "xTs": 1,
                "qk": 1, "v": 1, "hi": 1, "lo": 1, "dup": 1, "vs": 1,
                "qkT": 1, "qTs": 1, "kTs": 1, "s1": chunks1, "max": chunks1,
                "rT": 1, "rTs": 1, "s2": chunks2, "exp": chunks2,
                "o": 1, "shuf": 1, "rec": 1, "on": 1,
            } | own
            return {name: sig(f"{loop}_{name}", per) for name, per in names.items()}

        CAUSAL1 = [(1, 0, 4, 256), (1, 4, 4, 256), (1, 8, 4, 256), (0, 0, 8, 128), (0, 8, 4, 128)]
        CAUSAL2 = [(0, 0, 4, 256), (0, 4, 4, 256), (0, 8, 4, 256), (1, 0, 8, 128), (1, 8, 4, 128)]
        FULL = [(k, h, 4, 256) for k in (0, 1) for h in (0, 4, 8)]
        B_ = head_signals("b", len(CAUSAL1), len(CAUSAL2), {
            "cut": 2, "pj": 1, "h2": 1, "bn3": 1, "ag3": 1, "ve3": 1, "rs3": 1, "x3": 1, "x3c": 1, "base": 1,
            "x3T": 1, "x3Ts": 1, "lg": 1, "lgs": 1})
        C_ = head_signals("c", len(FULL), len(FULL), {
            "gm": 1, "bt": 1, "mk": 1, "hm": 3, "hg": 3, "z": 1, "zb": 1, "zg": 1, "za": 1})
        stored = [sig(f"stored{s}", 8) for s in range(2)]
        cut_waits = sem("cut_waits")
        t_sig = sem("t_sig")
        t_pe, t_act = sem("t_pe"), sem("t_act")

        def pipeline(eng, step):
            step((0, 0), None, None)
            step((1, 1), (0, 0), None)
            with eng.Fori(1, SEQS // 2) as pair:
                step((2 * pair, 0), (2 * pair - 1, 1), (2 * pair - 2, 0))
                step((2 * pair + 1, 1), (2 * pair, 0), (2 * pair - 1, 1))
            step(None, (SEQS - 1, 1), (SEQS - 2, 0))
            step(None, None, (SEQS - 1, 1))

        def settle(eng):
            eng.wait_ge(ld_const, 32)

        def tiles(T, n):
            return T[:, bass.ds(2 * n, 2), :] if not isinstance(n, int) else T[:, 2 * n:2 * n + 2, :]

        def pair_view(pair, slots, width, lo=0, hi=None):
            v = bank(pair, 2).rearrange("p (b c) -> p b c", b=2)[:, :, 0:slots * width]
            return v.rearrange("p b (i w) -> p b i w", w=width)

        with nc.Block() as start:
            def start_values(share):
                def program(eng):
                    for s in signals[share::5]:
                        eng.sem_inc(s.sem, AHEAD * s.per_seq)
                return program

            for share, on in enumerate((start.sync, start.gpsimd, start.scalar, start.vector, start.tensor)):
                on(start_values(share))

        block = ctx.enter_context(nc.Block())

        @block.sync
        def _(sp):
            sp.dma_start(idx[:], d["idx"]).then_inc(ld_idx, 16)
            sp.dma_start(ident[:], d["ident"]).then_inc(ld_const, 16)
            sp.dma_start(maskf[:], d["mask"]).then_inc(ld_const, 16)
            sp.dma_start(fold_l[:, 0:2], d["fold_l"][:, 0:2]).then_inc(ld_fold, 16)
            sp.dma_start(pos[:], d["pos"]).then_inc(ld_pos, 16)
            sp.dma_start(fold_l[:, 2:4], d["fold_l"][:, 2:4]).then_inc(ld_fold, 16)
            sp.dma_start(fold_r[:], d["fold_r"]).then_inc(ld_fold, 16)
            sp.dma_start(bias_r[:], d["bias_r"]).then_inc(ld_fold, 16)
            sp.dma_start(e_last[:], d["e_last"]).then_inc(ld_fold, 16)
            for t, name in ((ln1w, "ln1_w"), (ln1b, "ln1_b"), (ln2w, "ln2_w"), (ln2b, "ln2_b")):
                sp.dma_start(t[:], d[name].rearrange("(h p) c -> p h c", p=P)).then_inc(ld_ln, 16)
            sp.dma_start(wqkv[:], d["wqkv"]).then_inc(ld_attn, 16)
            sp.dma_start(wproj[:], d["wproj"]).then_inc(ld_attn, 16)
            sp.dma_start(wrout[:], d["wrout"]).then_inc(ld_attn, 16)
            sp.dma_start(w1[:], d["w1"]).then_inc(ld_ffn, 16)
            sp.dma_start(b2ab[:], d["b2"].partition_broadcast(P)).then_inc(ld_ffn, 16)
            sp.dma_start(gamma[:, 0, :], d["gamma"].partition_broadcast(P)).then_inc(ld_ffn, 16)
            sp.dma_start(beta[:, 0, :], d["beta"].partition_broadcast(P)).then_inc(ld_ffn, 16)
            sp.wait_ge(fold_mm, 3)
            sp.dma_start(w2ab[:], d["w2"]).then_inc(ld_ffn, 16)

            def store(n, s):
                sp.wait_ge(C_["za"].sem, C_["za"].done(n))
                dst = d["out"][bass.ds(n, 1)] if not isinstance(n, int) else d["out"][n:n + 1]
                sp.dma_start(dst.rearrange("a (h p) c -> p (a h) c", p=P), z[s][:]).then_inc(stored[s].sem, 16)

            with sp.Fori(0, SEQS // 2) as pair:
                store(2 * pair, 0)
                store(2 * pair + 1, 1)
            for s in range(2):
                sp.wait_ge(stored[s].sem, stored[s].done(SEQS - 2, 16))

        @block.gpsimd
        def _(pool):
            pool.wait_ge(ld_idx, 16)
            for t in range(SEQS * HALVES):
                pool.indirect_dma_start(EMB[:, t, :], None, d["emb"],
                                        bass.IndirectOffsetOnAxis(ap=idx[:, t:t + 1], axis=0)).then_inc(rows_in, 16)
            pool.memset(half_neg[:], -0.5).then_inc(consts_set, 1)
            pool.memset(mean_of[:], 1.0 / P).then_inc(consts_set, 1)
            for s in range(2):
                pool.memset(ys[s][:, :, DIM:DIM + 1], 1.0).then_inc(consts_set, 1)
                pool.memset(y1[s][:, :, DIM:DIM + 1], 1.0).then_inc(consts_set, 1)
                pool.memset(QS[s][:], 0.0).then_inc(consts_set, 1)
                pool.memset(VA[s][:], 1.0).then_inc(consts_set, 1)
            pool.wait_ge(consts_set, 10)
            for s in range(2):
                pool.memset(QS[s][:, :, HEADS:, 3 * HD:3 * HD + 1], 1.0).then_inc(consts_set, 1)
            pool.wait_ge(consts_set, 12)

            def power(out, var, s, have, freed, sig_out, n):
                pool.wait_ge(have.sem, have.done(n))
                pool.wait_ge(freed.sem, freed.freed(n))
                nc.gpsimd.tensor_tensor(out, var, half_neg[:, 0:var.shape[1]], ALU.pow).then_inc(sig_out.sem, 1)

            def tok_step(new, mid, back):
                if mid:
                    n, s = mid
                    power(st[s][:, 3:4], st[s][:, 2:3], s, a_ve, a_n, a_rs, n)
                    pool.wait_ge(a_n.sem, a_n.done(n))
                    pool.wait_ge(ld_ln, 64)
                    nc.gpsimd.tensor_tensor(r1[s][:], r1[s][:], ln1w[:], ALU.mult).then_inc(a_w.sem, 1)
                if back:
                    n, s = back
                    power(st2[s][:, 3:4], st2[s][:, 2:3], s, a_ve2, a_n2, a_rs2, n)
                    pool.wait_ge(a_n2.sem, a_n2.done(n))
                    nc.gpsimd.tensor_tensor(r2[s][:], r2[s][:], ln2w[:], ALU.mult).then_inc(a_w2.sem, 1)
                    pool.wait_ge(a_w2.sem, a_w2.done(n))
                    nc.gpsimd.tensor_tensor(tiles(H, n), r2[s][:], ln2b[:], ALU.add).then_inc(a_h.sem, 1)

            pipeline(pool, tok_step)

            def dup(S, n, s):
                settle(pool)
                pool.wait_ge(S["hi"].sem, S["hi"].done(n))
                pool.wait_ge(S["qkT"].sem, S["qkT"].freed(n))
                nc.gpsimd.tensor_copy(QS[s][:, :, 0:HEADS, HD:2 * HD], QS[s][:, :, 0:HEADS, 0:HD])
                nc.gpsimd.tensor_copy(QS[s][:, :, HEADS:, 2 * HD:3 * HD], QS[s][:, :, HEADS:, 0:HD]).then_inc(S["dup"].sem, 1)

            zero = pool.to_reg(0.0)

            def causal_step(new, mid, back):
                S = B_
                if new:
                    n, s = new
                    power(rstd[s][:], rv[s][:, :, 1], s, S["ve"], S["x"], S["rs"], n)
                    dup(S, n, s)
                if mid:
                    n, s = mid
                    for k, (col, last) in enumerate(((0, 3), (TOKENS, 5))):
                        pool.wait_ge(S["exp"].sem, S["exp"].done(n, last))
                        pool.sem_inc(cut_waits, 1)
                        v = PT[s][:, :, col:col + P]
                        nc.gpsimd.affine_select(out=v, in_=v, compare_op=ALU.is_ge, fill=zero, base=0,
                                                pattern=[[0, HEADS], [1, P]], channel_multiplier=-1).then_inc(S["cut"].sem, 1)
                    power(rstd3[s][:], rv3[s][:, :, 1], s, S["ve3"], S["x3"], S["rs3"], n)
                    pool.wait_ge(S["x3"].sem, S["x3"].done(n))
                    nc.gpsimd.tensor_tensor(tiles(BASE, n), h2[s][:], x3[s][:], ALU.add).then_inc(S["base"].sem, 1)
                    nc.gpsimd.tensor_copy(tiles(X3, n), x3[s][:]).then_inc(S["x3c"].sem, 1)

            pipeline(pool, causal_step)

            pool.wait_ge(ld_ffn, 5 * 16)
            nc.gpsimd.tensor_tensor(w2[:], w2ab[:, 0], w2ab[:, 1], ALU.add).then_inc(pre_ffn, 1)
            for h in range(HALVES):
                nc.gpsimd.tensor_tensor(b2[:, h], b2ab[:, 0], b2ab[:, 1], ALU.add).then_inc(pre_ffn, 1)

            def ffn_step(new, mid, back):
                S = C_
                if new:
                    n, s = new
                    power(rstd[s][:], rv[s][:, :, 1], s, S["ve"], S["x"], S["rs"], n)
                    pool.wait_ge(S["x"].sem, S["x"].done(n))
                    nc.gpsimd.tensor_tensor(xs[s][:, :, 0:DIM], xs[s][:, :, 0:DIM], gamma[:].to_broadcast([P, HALVES, DIM]), ALU.mult).then_inc(S["gm"].sem, 1)
                    pool.wait_ge(S["gm"].sem, S["gm"].done(n))
                    nc.gpsimd.tensor_tensor(xs[s][:, :, 0:DIM], xs[s][:, :, 0:DIM], beta[:].to_broadcast([P, HALVES, DIM]), ALU.add).then_inc(S["bt"].sem, 1)
                    dup(S, n, s)
                if back:
                    n, s = back
                    pool.wait_ge(S["zg"].sem, S["zg"].done(n))
                    nc.gpsimd.tensor_tensor(z[s][:], z[s][:], tiles(BASE, n), ALU.add).then_inc(S["za"].sem, 1)

            pool.wait_ge(t_sig, 1)
            pipeline(pool, ffn_step)

        @block.scalar
        def _(act):
            def evac(dst, src, ready, freed, made, n, extra=()):
                act.wait_ge(ready.sem, ready.done(n))
                act.wait_ge(freed.sem, freed.freed(n))
                nc.scalar.copy(dst, src).then_inc(made.sem, 1)

            for k, (w, width) in enumerate(((Aw, DIM + 1), (VO, DIM), (W12, DIM))):
                act.wait_ge(fold_mm, k + 1)
                nc.scalar.copy(w[:].rearrange("p a b -> p (a b)"), bank(k)[0:CH + 1, 0:2 * width]).then_inc(fold_set, 1)

            def tok_step(new, mid, back):
                if new:
                    n, s = new
                    evac(yT[s][:].rearrange("p a b -> p (a b)"), bank(4 * s)[0:CH + 1, :], a_yT, a_sc, a_yTs, n)
                if back:
                    n, s = back
                    evac(y1T[s][:].rearrange("p a b -> p (a b)"), bank(4 * s + 3)[0:CH + 1, :], a_y1T, a_f, a_y1Ts, n)
                if new:
                    n, s = new
                    evac(q2[s][:].rearrange("p a b -> p (a b)"), bank(4 * s + 1)[0:CH + 1, :], a_q2, a_sc, a_q2s, n)
                if back:
                    n, s = back
                    act.wait_ge(a_f.sem, a_f.done(n))
                    act.wait_ge(a_r2.sem, a_r2.freed(n))
                    nc.scalar.activation(g1[s][:].rearrange("p a b -> p (a b)"), bank(4 * s + 3)[:, 0:2 * DIM], ACT.Gelu).then_inc(a_g.sem, 1)
                if new:
                    n, s = new
                    act.wait_ge(a_max.sem, a_max.done(n))
                    act.wait_ge(a_pT.sem, a_pT.freed(n))
                    act.wait_ge(a_ri.sem, a_ri.freed(n))
                    for h in range(HALVES):
                        nc.scalar.activation(pr[s][:, h, :], bank(4 * s)[:, h * TOKENS:(h + 1) * TOKENS], ACT.Exp,
                                             bias=nm[s][:, h:h + 1], accum_out=rs[s][:, h:h + 1]).then_inc(a_exp.sem, 1)

            pipeline(act, tok_step)

            def front_x(S, n, s, rows):
                evac(xT[s][0:rows].rearrange("p a b -> p (a b)"), bank(0)[0:rows, :], S["xT"], S["v"], S["xTs"], n)

            def front_qkv(S, n, s):
                act.wait_ge(S["qk"].sem, S["qk"].done(n))
                act.wait_ge(S["qkT"].sem, S["qkT"].freed(n))
                act.wait_ge(S["rT"].sem, S["rT"].freed(n))
                v = bank(1, 2).rearrange("p (b c) -> p b c", b=2)[:, :, 0:2 * DIM].rearrange("p b (h e) -> p b h e", e=HD)
                nc.scalar.copy(QS[s][:, :, :, 0:HD], v).then_inc(S["hi"].sem, 1)
                act.wait_ge(S["v"].sem, S["v"].done(n))
                act.wait_ge(S["o"].sem, S["o"].freed(n))
                v = bank(3)[:, 0:2 * DIM].rearrange("p (b h e) -> p b h e", b=2, e=HD)
                nc.scalar.copy(VA[s][:, :, :, 0:HD], v).then_inc(S["vs"].sem, 1)

            def front_keys(S, n, s):
                act.wait_ge(S["qkT"].sem, S["qkT"].done(n))
                act.wait_ge(S["s2"].sem, S["s2"].freed(n))
                nc.scalar.copy(QT[s][:, HEADS // 2:, :].rearrange("p a b -> p (a b)"),
                               bank(2, 2).bitcast(F16)[:, 0:HEADS // 2 * TOKENS]).then_inc(S["kTs"].sem, 1)

            def exps(S, chunks, n, s, ks):
                for k in ks:
                    kt, h0, nh, w = chunks[k]
                    act.wait_ge(S["s2"].sem, S["s2"].done(n, k + 1))
                    if k == 0:
                        act.wait_ge(S["o"].sem, S["o"].freed(n))
                    dst = PT[s][:, h0:h0 + nh, kt * TOKENS:kt * TOKENS + w].rearrange("p (i b) w -> p b i w", b=2)
                    nc.scalar.activation(dst, pair_view(6 - 2 * (k % 2), nh // 2, w), ACT.Exp, scale=SCALE).then_inc(S["exp"].sem, 1)

            def causal_step(new, mid, back):
                S = B_
                if mid:
                    exps(S, CAUSAL2, *mid, (0, 1))
                if new:
                    front_x(S, *new, CH)
                if mid:
                    exps(S, CAUSAL2, *mid, (2,))
                if new:
                    front_qkv(S, *new)
                if mid:
                    exps(S, CAUSAL2, *mid, (3, 4))
                if new:
                    front_keys(S, *new)
                if back:
                    n, s = back
                    evac(x3T[s][:].rearrange("p a b -> p (a b)"), bank(7)[0:CH, :], S["x3T"], S["lg"], S["x3Ts"], n)

            pipeline(act, causal_step)

            act.wait_ge(t_sig, 2)
            nc.scalar.activation(lexp[:], lsub[:], ACT.Exp).then_inc(t_act, 1)

            def ffn_step(new, mid, back):
                S = C_
                if mid:
                    exps(S, FULL, *mid, (0, 1))
                if new:
                    front_x(S, *new, CH + 1)
                if mid:
                    exps(S, FULL, *mid, (2,))
                if new:
                    front_qkv(S, *new)
                if mid:
                    exps(S, FULL, *mid, (3, 4, 5))
                if new:
                    front_keys(S, *new)
                if mid:
                    n, s = mid
                    for k in range(3):
                        act.wait_ge(S["hm"].sem, S["hm"].done(n, k + 1))
                        if k == 0:
                            act.wait_ge(S["z"].sem, S["z"].freed(n))
                        nc.scalar.activation(hid[s][:, 2 * k:2 * k + 2, :].rearrange("p a b -> p (a b)"), bank(6 + k % 2), ACT.Gelu).then_inc(S["hg"].sem, 1)

            pipeline(act, ffn_step)

        @block.vector
        def _(dve):
            dve.wait_ge(ld_const, 32)
            nc.vector.tensor_copy(ident16[:], ident[:]).then_inc(dve_consts, 1)
            nc.vector.tensor_copy(identb[:], ident[:]).then_inc(dve_consts, 1)
            for i in range(4):
                nc.vector.tensor_copy(maskb[:, i], maskf[:]).then_inc(dve_consts, 1)
            dve.wait_ge(ld_pos, 16)
            dve.wait_ge(rows_in, 16 * SEQS * HALVES)
            dve.wait_ge(consts_set, 12)

            def whole_norm_stats(x, BS, MV, ready, bn, ag, sq, n):
                dve.wait_ge(ready.sem, ready.done(n))
                dve.wait_ge(sq.sem, sq.freed(n))
                nc.vector.bn_stats(BS[:, 0, :], x.rearrange("p a b -> p (a b)")).then_inc(bn.sem, 1)
                settle(dve)
                dve.wait_ge(bn.sem, bn.done(n))
                nc.vector.bn_aggr(MV[:], BS[:, 0:1, :]).then_inc(ag.sem, 1)
                dve.wait_ge(ag.sem, ag.done(n))
                nc.vector.scalar_tensor_tensor(MV[:, 1:2], MV[:, 0:1], MV[:, 0:1], MV[:, 1:2], ALU.mult, ALU.add).then_inc(sq.sem, 1)

            def whole_norm(x, ST, src, mm, ss, nv, ve, rs_, out_sig, n):
                dve.wait_ge(mm.sem, mm.done(n))
                nc.vector.tensor_copy(ST[:, 0:2], src).then_inc(ss.sem, 1)
                dve.wait_ge(ss.sem, ss.done(n))
                nc.vector.scalar_tensor_tensor(ST[:, 2:3], ST[:, 0:1], ST[:, 0:1], ST[:, 1:2], ALU.mult, ALU.subtract).then_inc(nv.sem, 1)
                dve.wait_ge(nv.sem, nv.done(n))
                nc.vector.tensor_scalar(ST[:, 2:3], ST[:, 2:3], -1.0, EPS_TOK, ALU.mult, ALU.add).then_inc(ve.sem, 1)
                dve.wait_ge(rs_.sem, rs_.done(n))
                nc.vector.tensor_scalar(x, x, ST[:, 0:1], ST[:, 3:4], ALU.subtract, ALU.mult).then_inc(out_sig.sem, 1)

            def tok_step(new, mid, back):
                if new:
                    n, s = new
                    dve.wait_ge(a_yT.sem, a_yT.freed(n))
                    dve.wait_ge(a_res.sem, a_res.freed(n))
                    nc.vector.tensor_tensor(ys[s][:, :, 0:DIM], tiles(EMB, n), pos[:], ALU.add).then_inc(a_y.sem, 1)
                if mid:
                    n, s = mid
                    dve.wait_ge(a_pT.sem, a_pT.done(n))
                    dve.wait_ge(a_o.sem, a_o.freed(n))
                    nc.vector.tensor_copy(pT[s][:].rearrange("p a b -> p (a b)"), bank(4 * s + 1)).then_inc(a_pTs.sem, 1)
                    dve.wait_ge(a_exp.sem, a_exp.done(n))
                    nc.vector.reciprocal(ri[s][:], rs[s][:]).then_inc(a_ri.sem, 1)
                    dve.wait_ge(a_ri.sem, a_ri.done(n))
                    dve.wait_ge(a_o.sem, a_o.done(n))
                    dve.wait_ge(a_y1.sem, a_y1.freed(n))
                    for h in range(HALVES):
                        i = nc.vector.scalar_tensor_tensor(r1[s][:, h], bank(4 * s + 2)[:, h * DIM:(h + 1) * DIM], ri[s][:, h:h + 1],
                                                           ys[s][:, h, 0:DIM], ALU.mult, ALU.add)
                    i.then_inc(a_res.sem, 1)
                    whole_norm_stats(r1[s][:], bs[s], mv[s], a_res, a_bn, a_ag, a_sq, n)
                if new:
                    n, s = new
                    dve.wait_ge(a_vp.sem, a_vp.done(n))
                    dve.wait_ge(a_o.sem, a_o.freed(n))
                    nc.vector.tensor_copy(vp[s][:].rearrange("p a b -> p (a b)"), bank(4 * s + 2)[:, 0:2 * DIM]).then_inc(a_vps.sem, 1)
                if back:
                    n, s = back
                    dve.wait_ge(a_g.sem, a_g.done(n))
                    dve.wait_ge(a_h.sem, a_h.freed(n))
                    nc.vector.tensor_tensor(r2[s][:], y1[s][:, :, 0:DIM], g1[s][:], ALU.add).then_inc(a_r2.sem, 1)
                    whole_norm_stats(r2[s][:], bs2[s], mv2[s], a_r2, a_bn2, a_ag2, a_sq2, n)
                if mid:
                    n, s = mid
                    whole_norm(r1[s][:], st[s], bank(4 * s + 1)[:, 0:2], a_st, a_ss, a_nv, a_ve, a_rs, a_n, n)
                if new:
                    n, s = new
                    dve.wait_ge(a_sc.sem, a_sc.done(n))
                    dve.wait_ge(a_exp.sem, a_exp.freed(n))
                    nc.vector.tensor_reduce(nm[s][:], bank(4 * s).rearrange("p (h t) -> p h t", h=HALVES), AX.X, ALU.max,
                                            negate=True).then_inc(a_max.sem, 1)
                if mid:
                    n, s = mid
                    dve.wait_ge(a_w.sem, a_w.done(n))
                    dve.wait_ge(a_r2.sem, a_r2.freed(n))
                    dve.wait_ge(a_y1T.sem, a_y1T.freed(n))
                    nc.vector.tensor_tensor(y1[s][:, :, 0:DIM], r1[s][:], ln1b[:], ALU.add).then_inc(a_y1.sem, 1)
                if back:
                    n, s = back
                    whole_norm(r2[s][:], st2[s], bank(4 * s + 3)[:, 0:2], a_st2, a_ss2, a_nv2, a_ve2, a_rs2, a_n2, n)

            pipeline(dve, tok_step)

            def row_norm(S, src, dst, BS, RV, RSTD, eps, bn, ag, ve, rs_, out_sig, freed, n):
                for h in range(HALVES):
                    i = nc.vector.bn_stats(BS[:, h, :], src(h))
                i.then_inc(bn.sem, 1)
                settle(dve)
                dve.wait_ge(bn.sem, bn.done(n))
                for h in range(HALVES):
                    i = nc.vector.bn_aggr(RV[:, h, :], BS[:, h:h + 1, :])
                i.then_inc(ag.sem, 1)
                dve.wait_ge(ag.sem, ag.done(n))
                nc.vector.tensor_scalar(RV[:, :, 1], RV[:, :, 1], eps, None, ALU.add).then_inc(ve.sem, 1)
                dve.wait_ge(rs_.sem, rs_.done(n))
                for f in freed:
                    dve.wait_ge(f.sem, f.freed(n))
                for h in range(HALVES):
                    i = nc.vector.tensor_scalar(dst(h), src(h), RV[:, h, 0:1], RSTD[:, h:h + 1], ALU.subtract, ALU.mult)
                i.then_inc(out_sig.sem, 1)

            def tile_of(T, n):
                return lambda h: T[:, bass.ds(2 * n + h, 1), :].rearrange("p a b -> p (a b)") if not isinstance(n, int) else T[:, 2 * n + h, :]

            def split(S, n, s):
                dve.wait_ge(S["hi"].sem, S["hi"].done(n))
                v = bank(1, 2).rearrange("p (b c) -> p b c", b=2)[:, :, 0:2 * DIM].rearrange("p b (h e) -> p b h e", e=HD)
                nc.vector.tensor_tensor(QS[s][:, :, 0:HEADS, 2 * HD:3 * HD], v[:, :, 0:HEADS], QS[s][:, :, 0:HEADS, 0:HD], ALU.subtract)
                nc.vector.tensor_tensor(QS[s][:, :, HEADS:, HD:2 * HD], v[:, :, HEADS:], QS[s][:, :, HEADS:, 0:HD], ALU.subtract).then_inc(S["lo"].sem, 1)

            def queries(S, n, s):
                dve.wait_ge(S["qkT"].sem, S["qkT"].done(n))
                dve.wait_ge(S["s2"].sem, S["s2"].freed(n))
                nc.vector.tensor_copy(QT[s][:, 0:HEADS // 2, :].rearrange("p a b -> p (a b)"),
                                      bank(0, 2).bitcast(F16)[:, 0:HEADS // 2 * TOKENS]).then_inc(S["qTs"].sem, 1)

            def maxima(S, chunks, n, s):
                for k, (h, h0, nh, w) in enumerate(chunks):
                    dve.wait_ge(S["s1"].sem, S["s1"].done(n, k + 1))
                    dst = QS[s][:, h, h0:h0 + nh, 3 * HD].rearrange("p (i b) -> p b i", b=2)
                    nc.vector.tensor_reduce(dst, pair_view(2 * (k % 2), nh // 2, w), AX.X, ALU.max, negate=True).then_inc(S["max"].sem, 1)

            def requeries(S, n, s):
                dve.wait_ge(S["rT"].sem, S["rT"].done(n))
                nc.vector.tensor_copy(QT[s][:, 0:HEADS // 2, :].rearrange("p a b -> p (a b)"),
                                      bank(4, 2).bitcast(F16)[:, 0:HEADS // 2 * TOKENS]).then_inc(S["rTs"].sem, 1)

            def normalise(S, n, s):
                o = bank(4, 2)[:, 0:GROUPS * TOKENS]
                flat = "p a b -> p (a b)"
                settle(dve)
                dve.wait_ge(S["o"].sem, S["o"].done(n))
                nc.vector.stream_shuffle(SM[s][:].rearrange(flat), o, [HD + i % HD for i in range(32)]).then_inc(S["shuf"].sem, 1)
                dve.wait_ge(S["shuf"].sem, S["shuf"].done(n))
                nc.vector.reciprocal(SM[s][:], SM[s][:]).then_inc(S["rec"].sem, 1)
                dve.wait_ge(S["rec"].sem, S["rec"].done(n))
                used = S["pj"] if S is B_ else S["z"]
                dve.wait_ge(used.sem, used.freed(n))
                nc.vector.tensor_tensor(OT[s][:].rearrange(flat), o, SM[s][:].rearrange(flat), ALU.mult).then_inc(S["on"].sem, 1)

            def causal_step(new, mid, back):
                S = B_
                if mid:
                    requeries(S, *mid)
                if new:
                    n, s = new
                    dve.wait_ge(a_h.sem, a_h.done(n))
                    row_norm(S, tile_of(H, n), lambda h: xs[s][:, h, 0:DIM], bsr[s], rv[s], rstd[s], EPS_ROW, S["bn"], S["ag"], S["ve"], S["rs"], S["x"], [S["xT"]], n)
                    split(S, n, s)
                    queries(S, n, s)
                if mid:
                    normalise(S, *mid)
                if new:
                    maxima(S, CAUSAL1, *new)
                if mid:
                    n, s = mid
                    dve.wait_ge(S["pj"].sem, S["pj"].done(n))
                    dve.wait_ge(S["base"].sem, S["base"].freed(n))
                    nc.vector.tensor_tensor(h2[s][:], bank(6)[:, 0:2 * DIM].rearrange("p (a b) -> p a b", a=2), tiles(H, n), ALU.add).then_inc(S["h2"].sem, 1)
                    dve.wait_ge(S["h2"].sem, S["h2"].done(n))
                    row_norm(S, lambda h: h2[s][:, h], lambda h: x3[s][:, h], bsr3[s], rv3[s], rstd3[s], EPS_ROW, S["bn3"], S["ag3"], S["ve3"], S["rs3"], S["x3"], [S["x3T"], S["x3c"]], n)
                if back:
                    n, s = back
                    dve.wait_ge(S["lg"].sem, S["lg"].done(n))
                    dst = LG[:, :, bass.ds(n, 1), :] if not isinstance(n, int) else LG[:, :, n:n + 1, :]
                    nc.vector.tensor_copy(dst, bank(7)[:, 0:2 * EXPERTS].rearrange("p (a o b) -> p a o b", a=2, o=1)).then_inc(S["lgs"].sem, 1)

            pipeline(dve, causal_step)

            count = [0]

            def link(i):
                count[0] += 1
                i.then_inc(t_sig, 1)
                dve.wait_ge(t_sig, count[0])

            dve.wait_ge(B_["lgs"].sem, B_["lgs"].done(SEQS - 1))
            wide = [P, HALVES, SEQS, EXPERTS]
            link(nc.vector.tensor_reduce(lmax[:], LG[:], AX.X, ALU.max))
            link(nc.vector.tensor_tensor(lsub[:], LG[:], lmax[:].unsqueeze(3).to_broadcast(wide), ALU.subtract))
            dve.wait_ge(t_act, 1)
            link(nc.vector.tensor_reduce(lsum[:], lexp[:], AX.X, ALU.add))
            link(nc.vector.reciprocal(lsum[:], lsum[:]))
            link(nc.vector.tensor_tensor(PR[:], lexp[:], lsum[:].unsqueeze(3).to_broadcast(wide), ALU.mult))
            dve.wait_ge(t_pe, 1)
            link(nc.vector.tensor_copy(tops[0], bank(0)[0:SEQS * EXPERTS, 0:TOKENS]))
            for r in range(CAP // 8):
                link(nc.vector.max(top8[r % 2][:], tops[r % 2]))
                link(nc.vector.match_replace(tops[1 - r % 2], top8[r % 2][:], tops[r % 2], -1.0))
            link(nc.vector.tensor_scalar(chosen, tops[CAP // 8 % 2], -1.0, None, ALU.is_equal))
            dve.wait_ge(t_pe, 2)
            link(nc.vector.tensor_copy(MS[:].rearrange("p a b c -> p (a b c)"), bank(1)[:, 0:HALVES * SEQS * EXPERTS]))
            link(nc.vector.tensor_tensor(GS[:], MS[:], PR[:], ALU.mult))
            for e in range(EXPERTS - 2, -1, -1):
                nc.vector.tensor_tensor(MS[:, :, :, e], MS[:, :, :, e], MS[:, :, :, e + 1], ALU.add)
                link(nc.vector.tensor_tensor(GS[:, :, :, e], GS[:, :, :, e], GS[:, :, :, e + 1], ALU.add))

            def region(dst, src, W, n):
                for e, (lo, hi) in enumerate(REGIONS):
                    w = (W[:, :, bass.ds(n, 1), e:e + 1] if not isinstance(n, int) else W[:, :, n:n + 1, e:e + 1])
                    w = w.rearrange("p a b c -> p a (b c)").to_broadcast([P, HALVES, hi - lo])
                    i = nc.vector.tensor_tensor(dst[:, :, lo:hi], src[:, :, lo:hi], w, ALU.mult)
                return i

            def ffn_step(new, mid, back):
                S = C_
                if mid:
                    requeries(S, *mid)
                if new:
                    n, s = new
                    dve.wait_ge(B_["x3c"].sem, B_["x3c"].done(n))
                    row_norm(S, tile_of(X3, n), lambda h: xs[s][:, h, 0:DIM], bsr[s], rv[s], rstd[s], EPS_FFN, S["bn"], S["ag"], S["ve"], S["rs"], S["x"], [S["xT"]], n)
                    w = MS[:, :, bass.ds(n, 1), 0:1] if not isinstance(n, int) else MS[:, :, n:n + 1, 0:1]
                    nc.vector.tensor_copy(xs[s][:, :, DIM:DIM + 1], w.rearrange("p a b c -> p a (b c)"))
                    dve.wait_ge(S["bt"].sem, S["bt"].done(n))
                    region(xs[s], xs[s], MS, n).then_inc(S["mk"].sem, 1)
                    split(S, n, s)
                    queries(S, n, s)
                if mid:
                    normalise(S, *mid)
                if new:
                    maxima(S, FULL, *new)
                if back:
                    n, s = back
                    dve.wait_ge(S["z"].sem, S["z"].done(n))
                    dve.wait_ge(stored[s].sem, stored[s].freed(n - s, 16))
                    nc.vector.tensor_tensor(z[s][:], bank(7)[:, 0:2 * DIM].rearrange("p (a b) -> p a b", a=2), b2[:], ALU.add).then_inc(S["zb"].sem, 1)
                    dve.wait_ge(S["zb"].sem, S["zb"].done(n))
                    region(z[s], z[s], GS, n).then_inc(S["zg"].sem, 1)

            dve.wait_ge(pre_ffn, 3)
            pipeline(dve, ffn_step)

        @block.tensor
        def _(pe):
            def mm(out, l, r, start=True, stop=True, free=False):
                return nc.tensor.matmul(out, l, r, start=start, stop=stop, skip_group_check=free)

            def rows(c):
                return CH + c

            pe.wait_ge(ld_fold, 80)
            pe.wait_ge(ld_const, 32)
            pe.wait_ge(consts_set, 12)
            pe.wait_ge(dve_consts, 6)
            for b, (left, right, width, bias) in enumerate((((0), None, DIM + 1, None), (2, 0, DIM, 0), (3, 1, DIM, 1))):
                for c in range(2):
                    lo = c * CH
                    out = bank(b)[0:CH + 1, c * width:(c + 1) * width]
                    for k in range(HT):
                        r = fold_l[:, 1, k, :] if right is None else fold_r[:, right, k, :]
                        i = mm(out, fold_l[:, left, k, lo:lo + CH + 1], r, start=(k == 0), stop=(k == HT - 1 and bias is None))
                    if bias is not None:
                        i = mm(out, e_last[0:1, lo:lo + CH + 1], bias_r[0:1, bias, :], start=False, stop=True)
                i.then_inc(fold_mm, 1)
            pe.wait_ge(fold_set, 3)

            def transposes(dst, src, width, ready, n, made):
                pe.wait_ge(ready.sem, ready.done(n))
                for c in range(2):
                    for h in range(HALVES):
                        i = nc.tensor.transpose(dst[0:width, c * TOKENS + h * P:c * TOKENS + (h + 1) * P],
                                                src[:, h, c * CH:c * CH + width], ident[:])
                i.then_inc(made.sem, 1)

            def tok_front1(n, s):
                pe.wait_ge(a_exp.sem, a_exp.freed(n))
                transposes(bank(4 * s), ys[s], CH + 1, a_y, n, a_yT)

            def tok_front2(n, s):
                pe.wait_ge(a_yTs.sem, a_yTs.done(n))
                pe.wait_ge(a_ss.sem, a_ss.freed(n))
                for m in range(2):
                    for c in range(2):
                        i = mm(bank(4 * s + 1)[0:CH + 1, m * TOKENS:(m + 1) * TOKENS], Aw[0:rows(c), c, m * CH:m * CH + CH + 1],
                               yT[s][0:rows(c), c, :], start=(c == 0), stop=(c == 1))
                i.then_inc(a_q2.sem, 1)
                pe.wait_ge(a_res.sem, a_res.freed(n))
                for h in range(HALVES):
                    for c in range(2):
                        i = mm(bank(4 * s + 2)[:, h * DIM:(h + 1) * DIM], yT[s][0:rows(c), c, h * P:(h + 1) * P], VO[0:rows(c), c, :],
                               start=(c == 0), stop=(c == 1))
                i.then_inc(a_vp.sem, 1)

            def tok_scores(n, s):
                pe.wait_ge(a_q2s.sem, a_q2s.done(n))
                for h in range(HALVES):
                    for c in range(2):
                        i = mm(bank(4 * s)[:, h * TOKENS:(h + 1) * TOKENS], q2[s][0:rows(c), c, h * P:(h + 1) * P], yT[s][0:rows(c), c, :],
                               start=(c == 0), stop=(c == 1))
                i.then_inc(a_sc.sem, 1)

            def tok_pT(n, s):
                pe.wait_ge(a_exp.sem, a_exp.done(n))
                for k in range(HALVES):
                    for h in range(HALVES):
                        i = nc.tensor.transpose(bank(4 * s + 1)[:, k * TOKENS + h * P:k * TOKENS + (h + 1) * P],
                                                pr[s][:, h, k * P:(k + 1) * P], ident[:])
                i.then_inc(a_pT.sem, 1)

            def tok_out(n, s):
                pe.wait_ge(a_pTs.sem, a_pTs.done(n))
                pe.wait_ge(a_vps.sem, a_vps.done(n))
                for h in range(HALVES):
                    for k in range(HALVES):
                        i = mm(bank(4 * s + 2)[:, h * DIM:(h + 1) * DIM], pT[s][:, k, h * P:(h + 1) * P], vp[s][:, k, :],
                               start=(k == 0), stop=(k == 1))
                i.then_inc(a_o.sem, 1)

            def tok_step(new, mid, back):
                if mid:
                    tok_pT(*mid)
                if new:
                    tok_front1(*new)
                if back:
                    n, s = back
                    pe.wait_ge(a_ss2.sem, a_ss2.freed(n))
                    transposes(bank(4 * s + 3), y1[s], CH + 1, a_y1, n, a_y1T)
                if mid:
                    tok_out(*mid)
                if new:
                    tok_front2(*new)
                if back:
                    n, s = back
                    pe.wait_ge(a_y1Ts.sem, a_y1Ts.done(n))
                    for h in range(HALVES):
                        for c in range(2):
                            i = mm(bank(4 * s + 3)[:, h * DIM:(h + 1) * DIM], y1T[s][0:rows(c), c, h * P:(h + 1) * P], W12[0:rows(c), c, :],
                                   start=(c == 0), stop=(c == 1))
                    i.then_inc(a_f.sem, 1)
                if mid:
                    n, s = mid
                    pe.wait_ge(a_sq.sem, a_sq.done(n))
                    mm(bank(4 * s + 1)[:, 0:2], mean_of[:], mv[s][:]).then_inc(a_st.sem, 1)
                if new:
                    tok_scores(*new)
                if back:
                    n, s = back
                    pe.wait_ge(a_sq2.sem, a_sq2.done(n))
                    mm(bank(4 * s + 3)[:, 0:2], mean_of[:], mv2[s][:]).then_inc(a_st2.sem, 1)

            pipeline(pe, tok_step)

            def front_x(S, n, s, rows_, ready):
                pe.wait_ge(S["max"].sem, S["max"].done(n - 1))
                transposes(bank(0), xs[s], rows_, ready, n, S["xT"])

            def front_qkv(S, n, s, W, col, K):
                pe.wait_ge(S["xTs"].sem, S["xTs"].done(n))
                for h in range(HALVES):
                    for c in range(2):
                        i = mm(bank(1 + h)[:, 0:2 * DIM], xT[s][0:K[c], c, h * P:(h + 1) * P], W[0:K[c], c, col:col + 2 * DIM],
                               start=(c == 0), stop=(c == 1))
                i.then_inc(S["qk"].sem, 1)
                for h in range(HALVES):
                    for c in range(2):
                        i = mm(bank(3)[:, h * DIM:(h + 1) * DIM], xT[s][0:K[c], c, h * P:(h + 1) * P], W[0:K[c], c, col + 2 * DIM:col + 3 * DIM],
                               start=(c == 0), stop=(c == 1))
                i.then_inc(S["v"].sem, 1)

            def slots_T(dst, s, blocks):
                for j, b in enumerate(blocks):
                    for h in range(HALVES):
                        i = nc.tensor.transpose(dst[:, j * TOKENS + h * P:j * TOKENS + (h + 1) * P],
                                                QS[s][:, h, 2 * b:2 * b + 2, :].rearrange("p a b -> p (a b)"), ident16[:])
                return i

            def front_T(S, n, s):
                pe.wait_ge(S["hi"].sem, S["hi"].done(n))
                pe.wait_ge(S["lo"].sem, S["lo"].done(n))
                pe.wait_ge(S["dup"].sem, S["dup"].done(n))
                pe.wait_ge(S["vs"].sem, S["vs"].done(n))
                slots_T(bank(0, 2).bitcast(F16), s, range(HEADS // 2))
                slots_T(bank(2, 2).bitcast(F16), s, range(HEADS // 2, HEADS)).then_inc(S["qkT"].sem, 1)

            def head_rows(t, h):
                return t[SLOT * (h % 2):SLOT * (h % 2) + SLOT]

            def front_s1(S, chunks, n, s, causal):
                for k, (half, h0, nh, w) in enumerate(chunks):
                    if k == 0:
                        pe.wait_ge(S["qTs"].sem, S["qTs"].done(n))
                    if k == 0:
                        pe.wait_ge(S["kTs"].sem, S["kTs"].done(n))
                    if k >= 2:
                        pe.wait_ge(S["max"].sem, S["max"].done(n, k - 1))
                    pair = 2 * (k % 2)
                    if causal:
                        for b in range(2):
                            v = bank(pair + b)[:, 0:nh // 2 * w].rearrange("p (i w) -> p i w", w=w)[:, :, w - P:w]
                            mm(v, identb[:], maskb[:, 0:nh // 2, :], start=True, stop=False, free=True)
                    for j in range(nh):
                        h = h0 + j
                        i = mm(bank(pair + j % 2)[:, j // 2 * w:(j // 2 + 1) * w], head_rows(QT[s], h)[:, h // 2, half * P:(half + 1) * P],
                               head_rows(QT[s], h)[:, HEADS // 2 + h // 2, 0:w], start=(not causal and j < 2), stop=(j >= nh - 2), free=True)
                    i.then_inc(S["s1"].sem, 1)

            def mid_rT(S, n, s, free):
                pe.wait_ge(S["max"].sem, S["max"].done(n))
                pe.wait_ge(free.sem, free.done(n - 1))
                slots_T(bank(4, 2).bitcast(F16), s, range(HEADS // 2)).then_inc(S["rT"].sem, 1)

            def mid_s2(S, chunks, n, s, ks, free):
                for k in ks:
                    kt, h0, nh, w = chunks[k]
                    if k == 0:
                        pe.wait_ge(free[0].sem, free[0].done(n - 1))
                        pe.wait_ge(free[1].sem, free[1].freed(n))
                    if k == 0:
                        pe.wait_ge(S["rTs"].sem, S["rTs"].done(n))
                    if k >= 2:
                        pe.wait_ge(S["exp"].sem, S["exp"].done(n, k - 1))
                    pair = 6 - 2 * (k % 2)
                    for j in range(nh):
                        h = h0 + j
                        i = mm(bank(pair + j % 2)[:, j // 2 * w:(j // 2 + 1) * w], head_rows(QT[s], h)[:, HEADS // 2 + h // 2, kt * P:(kt + 1) * P],
                               head_rows(QT[s], h)[:, h // 2, TOKENS - w:TOKENS], start=(j < 2), stop=(j >= nh - 2), free=True)
                    i.then_inc(S["s2"].sem, 1)

            def mid_pv(S, n, s, w1_):
                for g in range(GROUPS):
                    for kt, w in ((0, TOKENS), (1, w1_)):
                        for j in range(4):
                            i = mm(bank(4, 2)[32 * j:32 * j + 32, g * TOKENS + TOKENS - w:(g + 1) * TOKENS], VA[s][:, kt, 4 * g + j, :],
                                   PT[s][:, 4 * g + j, kt * TOKENS:kt * TOKENS + w], start=(kt == 0), stop=(kt == 1), free=True)
                i.then_inc(S["o"].sem, 1)

            def causal_step(new, mid, back):
                S = B_
                if mid:
                    mid_rT(S, *mid, S["on"])
                    mid_s2(S, CAUSAL2, *mid, (0, 1), [S["h2"], S["lgs"]])
                if new:
                    front_x(S, *new, CH, S["x"])
                if mid:
                    mid_s2(S, CAUSAL2, *mid, (2,), [])
                if new:
                    front_qkv(S, *new, wqkv, 0, (CH, CH))
                if mid:
                    mid_s2(S, CAUSAL2, *mid, (3, 4), [])
                if new:
                    front_T(S, *new)
                if mid:
                    n, s = mid
                    pe.wait_ge(S["cut"].sem, S["cut"].done(n))
                    pe.wait_ge(S["exp"].sem, S["exp"].done(n))
                    mid_pv(S, n, s, P)
                if new:
                    front_s1(S, CAUSAL1, *new, True)
                if back:
                    n, s = back
                    if mid:
                        pe.wait_ge(S["exp"].sem, S["exp"].done(n + 1))
                    pe.wait_ge(S["lgs"].sem, S["lgs"].done(n - 1))
                    transposes(bank(7), x3[s], CH, S["x3"], n, S["x3T"])
                if mid:
                    n, s = mid
                    pe.wait_ge(S["on"].sem, S["on"].done(n))
                    for h in range(HALVES):
                        for g in range(GROUPS):
                            i = mm(bank(6)[:, h * DIM:(h + 1) * DIM], OT[s][:, g, h * P:(h + 1) * P], wproj[:, g, :],
                                   start=(g == 0), stop=(g == GROUPS - 1))
                    i.then_inc(S["pj"].sem, 1)
                if back:
                    n, s = back
                    pe.wait_ge(S["x3Ts"].sem, S["x3Ts"].done(n))
                    for h in range(HALVES):
                        for c in range(2):
                            i = mm(bank(7)[:, h * EXPERTS:(h + 1) * EXPERTS], x3T[s][:, c, h * P:(h + 1) * P], wrout[:, c, :],
                                   start=(c == 0), stop=(c == 1))
                    i.then_inc(S["lg"].sem, 1)

            pe.wait_ge(ld_attn, 48)
            pipeline(pe, causal_step)

            pe.wait_ge(t_sig, 5)
            for h in range(HALVES):
                i = nc.tensor.transpose(bank(0)[0:SEQS * EXPERTS, h * P:(h + 1) * P], PR[:, h].rearrange("p a b -> p (a b)"), ident[:])
            i.then_inc(t_pe, 1)
            pe.wait_ge(t_sig, 6 + 2 * (CAP // 8) + 1)
            for h in range(HALVES):
                i = nc.tensor.transpose(bank(1)[:, h * SEQS * EXPERTS:(h + 1) * SEQS * EXPERTS], chosen[:, h * P:(h + 1) * P],
                                        ident[0:SEQS * EXPERTS, 0:SEQS * EXPERTS])
            i.then_inc(t_pe, 1)
            pe.wait_ge(t_sig, 6 + 2 * (CAP // 8) + 2)

            def ffn_step(new, mid, back):
                S = C_
                if mid:
                    mid_rT(S, *mid, S["on"])
                    mid_s2(S, FULL, *mid, (0, 1), [S["hg"], S["zb"]])
                if new:
                    front_x(S, *new, CH + 1, S["mk"])
                if mid:
                    mid_s2(S, FULL, *mid, (2,), [])
                if new:
                    front_qkv(S, *new, w1, HIDDEN, (CH, CH + 1))
                if mid:
                    mid_s2(S, FULL, *mid, (3, 4, 5), [])
                if new:
                    front_T(S, *new)
                if mid:
                    n, s = mid
                    for k in range(3):
                        if k == 0:
                            pe.wait_ge(S["exp"].sem, S["exp"].done(n))
                        if k == 2:
                            pe.wait_ge(S["hg"].sem, S["hg"].done(n, 1))
                        for m in (2 * k, 2 * k + 1):
                            for c in range(2):
                                i = mm(bank(6 + k % 2)[:, m % 2 * TOKENS:(m % 2 + 1) * TOKENS], w1[0:rows(c), c, m * P:(m + 1) * P],
                                       xT[s][0:rows(c), c, :], start=(c == 0), stop=(c == 1))
                        i.then_inc(S["hm"].sem, 1)
                    mid_pv(S, n, s, TOKENS)
                if new:
                    front_s1(S, FULL, *new, False)
                if back:
                    n, s = back
                    if mid:
                        pe.wait_ge(S["hg"].sem, S["hg"].done(n + 1))
                    pe.wait_ge(S["zb"].sem, S["zb"].done(n - 1))
                    pe.wait_ge(S["hg"].sem, S["hg"].done(n))
                    pe.wait_ge(S["on"].sem, S["on"].done(n))
                    for h in range(HALVES):
                        for k in range(HT + GROUPS):
                            l = hid[s][:, k, h * P:(h + 1) * P] if k < HT else OT[s][:, k - HT, h * P:(h + 1) * P]
                            i = mm(bank(7)[:, h * DIM:(h + 1) * DIM], l, w2[:, k, :], start=(k == 0), stop=(k == HT + GROUPS - 1))
                    i.then_inc(S["z"].sem, 1)

            pe.wait_ge(ld_ffn, 5 * 16)
            pe.wait_ge(pre_ffn, 3)
            pipeline(pe, ffn_step)


def kernel(**inputs):
    import numpy as np
    import concourse.bacc as bacc
    from concourse.bass_utils import run_bass_kernel_spmd

    a = {k: np.asarray(v) for k, v in inputs.items()}
    tok = lambda k: a["L0_tok_" + k]

    def rows(w):
        return np.ascontiguousarray(w.reshape(-1, P, w.shape[-1]).transpose(1, 0, 2))

    def aug(w, b):
        return rows(np.concatenate([w, b[None]], 0).T)

    def halves(w):
        out = np.zeros((w.shape[0] - CH, 2, w.shape[1]), w.dtype)
        out[:CH, 0] = w[:CH]
        out[:, 1] = w[CH:]
        return out

    def head_rows_of(w):
        out = np.zeros((HEADS, 2 * HD, w.shape[1]), w.dtype)
        out[:, :HD] = w.reshape(HEADS, HD, -1)
        return rows(out.reshape(HEADS * 2 * HD, -1))

    f = np.float32
    ang = np.arange(TOKENS, dtype=f)[:, None] / np.power(f(10000.0), np.arange(DIM, dtype=f)[None] / f(DIM)).astype(f)
    pos = np.where((np.arange(DIM) % 2 == 0)[None], np.sin(ang), np.cos(ang)).astype(f)
    causal = np.where(np.arange(P)[None, :] <= np.arange(P)[:, None], f(0), f(MASKED)).astype(f)
    w2 = a["L0_ffn_w2"]
    split2 = [np.concatenate([rows(w.T[:HIDDEN]), head_rows_of(w.T[HIDDEN:])], 1) for w in (w2[:DIM], w2[DIM:])]
    arrays = {
        "idx": np.ascontiguousarray(a["x"].reshape(SEQS * HALVES, P).T),
        "emb": tok("emb"),
        "pos": np.ascontiguousarray(pos.reshape(HALVES, P, DIM).transpose(1, 0, 2)),
        "ident": np.eye(P, dtype=f),
        "mask": causal,
        "fold_l": np.stack([aug(tok("W" + k), tok("b" + k)) for k in ("q", "k", "v", "1")], 1),
        "fold_r": np.stack([rows(tok("Wo")), rows(tok("W2"))], 1),
        "bias_r": np.stack([tok("bo"), tok("b2")])[None],
        "e_last": np.eye(DIM + 1, dtype=f)[DIM:],
        "ln1_w": tok("ln1_w"), "ln1_b": tok("ln1_b"), "ln2_w": tok("ln2_w"), "ln2_b": tok("ln2_b"),
        "wqkv": halves(a["L0_attn_W_qkv"].T),
        "wproj": head_rows_of(a["L0_attn_W_proj"].T),
        "wrout": halves(a["L0_ffn_w_router"].T),
        "w1": halves(np.concatenate([a["L0_ffn_w1"].T, a["L0_ffn_b1"][None]], 0)),
        "w2": np.stack(split2, 1),
        "b2": a["L0_ffn_b2"].reshape(2, DIM),
        "gamma": a["L0_ffn_gamma1"], "beta": a["L0_ffn_beta1"],
    }
    arrays = {k: np.ascontiguousarray(v) for k, v in arrays.items()}
    nc = bacc.Bacc("TRN2", target_bir_lowering=False, num_devices=1)
    d = {k: nc.dram_tensor("in_" + k, v.shape, mybir.dt.from_np(v.dtype), kind="ExternalInput").ap() for k, v in arrays.items()}
    d["out"] = nc.dram_tensor("out", (SEQS, TOKENS, DIM), F32, kind="ExternalOutput").ap()
    build(nc, d)
    r = run_bass_kernel_spmd(nc, [{"in_" + k: v for k, v in arrays.items()}], core_ids=[0])
    return r.results[0]["out"]
```

```python
from contextlib import ExitStack

import concourse.bass as bass
from concourse import mybir

F32 = mybir.dt.float32
F16 = mybir.dt.float16
BF16 = mybir.dt.bfloat16
U32 = mybir.dt.uint32
I32 = mybir.dt.int32
ALU = mybir.AluOpType
ACT = mybir.ActivationFunctionType
AX = mybir.AxisListType

P = 128
SEQS, TOKENS, DIM, HIDDEN = 8, 256, 192, 768
HALVES = TOKENS // P
VOCAB = 8000
CH = DIM // 2
HT = HIDDEN // P
HEADS, HD = 12, 16
GROUPS = HEADS // 4
SLOT = 64
EXPERTS = 4
CAP = TOKENS // 2
REGIONS = [(0, DIM // 8), (DIM // 8, DIM // 4), (DIM // 4, DIM // 2), (DIM // 2, DIM)]
BANK = 512
QKV = 3 * DIM
FC1 = HIDDEN + QKV
SCALE = HD ** -0.5
EPS_TOK, EPS_ROW, EPS_FFN = 1e-5, 1e-5, 1e-6
MASKED = -1e30
AHEAD = 2


class Signal:

    def __init__(self, sem, per_seq):
        self.sem, self.per_seq = sem, per_seq

    def done(self, seq, count=None):
        return seq * self.per_seq + (AHEAD * self.per_seq + (self.per_seq if count is None else count))

    def freed(self, seq, count=None):
        return seq * self.per_seq + (self.per_seq if count is None else count)


def build(nc, d):
    with ExitStack() as ctx:
        def sb(name, shape, dt=F32):
            return ctx.enter_context(nc.sbuf_tensor(name, shape, dt))

        signals = []

        def sig(name, per_seq=1):
            s = Signal(ctx.enter_context(nc.semaphore(name)), per_seq)
            signals.append(s)
            return s

        def sem(name):
            return ctx.enter_context(nc.semaphore(name))

        PS = ctx.enter_context(nc.psum_tensor("PS", [P, 8 * BANK], F32))

        def bank(b, n=1):
            return PS[:, b * BANK:(b + n) * BANK]

        idx = sb("idx", [P, SEQS * HALVES], I32)
        pos = sb("pos", [P, HALVES, DIM])
        ident = sb("ident", [P, P])
        ident16 = sb("ident16", [P, P], F16)
        identb = sb("identb", [P, P], BF16)
        maskf = sb("maskf", [P, P])
        maskb = sb("maskb", [P, 4, P], BF16)
        mean_of = sb("mean_of", [P, P])
        half_neg = sb("half_neg", [P, 2])
        fold = sb("fold", [P, 4 * HT * (DIM + 1) + 2 * HT * DIM])
        fold_l = fold[:, 0:4 * HT * (DIM + 1)].rearrange("p (a k c) -> p a k c", a=4, k=HT)
        fold_r = fold[:, 4 * HT * (DIM + 1):].rearrange("p (a k c) -> p a k c", a=2, k=HT)
        bias_r = sb("bias_r", [1, 2, DIM])
        e_last = sb("e_last", [1, DIM + 1])
        Aw = sb("Aw", [CH + 1, 2, DIM + 1])
        VO = sb("VO", [CH + 1, 2, DIM])
        W12 = sb("W12", [CH + 1, 2, DIM])
        ln1w = sb("ln1w", [P, HALVES, DIM])
        ln1b = sb("ln1b", [P, HALVES, DIM])
        ln2w = sb("ln2w", [P, HALVES, DIM])
        ln2b = sb("ln2b", [P, HALVES, DIM])
        wqkv = sb("wqkv", [CH, 2, QKV])
        wproj = sb("wproj", [CH, 2, DIM])
        wrout = sb("wrout", [CH, 2, EXPERTS])
        w1 = sb("w1", [CH + 1, 2, FC1])
        free_at = SEQS * HALVES * DIM
        w2ab = fold[:, free_at:free_at + 2 * (HT + 2) * DIM].rearrange("p (a k c) -> p a k c", a=2, k=HT + 2)
        w2 = sb("w2", [P, HT + 2, DIM])
        b2ab = sb("b2ab", [P, 2, DIM])
        b2 = sb("b2", [P, HALVES, DIM])
        gamma = sb("gamma", [P, 1, DIM])
        beta = sb("beta", [P, 1, DIM])

        X = sb("X", [P, SEQS * HALVES, DIM])
        H = sb("H", [P, SEQS * HALVES, DIM])
        BASE = fold[:, 0:SEQS * HALVES * DIM].rearrange("p (t c) -> p t c", c=DIM)
        LG = sb("LG", [P, HALVES, SEQS, EXPERTS])

        def two(name, shape, dt=F32):
            return [sb(f"{name}{s}", shape, dt) for s in range(2)]

        PTf = two("PT", [P, HEADS * 2 * TOKENS])
        at = [0, 0]

        def carve(shape):
            size = shape[1] * shape[2]
            out = []
            for s in range(2):
                out.append(PTf[s][0:shape[0], at[s]:at[s] + size].rearrange("p (a b) -> p a b", a=shape[1]))
                at[s] += size
            return out

        ys = carve([P, HALVES, DIM + 1])
        yT = carve([CH + 1, 2, TOKENS])
        q2 = carve([CH + 1, 2, TOKENS])
        vp = carve([P, HALVES, DIM])
        nm = two("nm", [P, HALVES])
        pr = carve([P, HALVES, TOKENS])
        rs = two("rs", [P, HALVES])
        ri = two("ri", [P, HALVES])
        pT = carve([P, HALVES, TOKENS])
        r1 = carve([P, HALVES, DIM])
        y1 = carve([P, HALVES, DIM + 1])
        y1T = carve([CH + 1, 2, TOKENS])
        g1 = carve([P, HALVES, DIM])
        r2 = carve([P, HALVES, DIM])
        bs = two("bs", [P, 2, 6])
        mv = two("mv", [P, 2])
        st = two("st", [P, 4])
        bs2 = two("bs2", [P, 2, 6])
        mv2 = two("mv2", [P, 2])
        st2 = two("st2", [P, 4])

        xs = two("xs", [P, HALVES, DIM + 1])
        rv = two("rv", [P, HALVES, 2])
        rstd = two("rstd", [P, HALVES])
        bsr = two("bsr", [P, HALVES, 6])
        xT = two("xT", [CH + 1, 2, TOKENS])
        QS = two("QS", [P, HALVES, 2 * HEADS, SLOT], F16)
        VA = two("VA", [P, HALVES, HEADS, 2 * HD])
        QT = two("QT", [P, HEADS, TOKENS], F16)
        PT = [t[:].rearrange("p (h c) -> p h c", h=HEADS) for t in PTf]
        OR = two("OR", [P, GROUPS, TOKENS])
        ON = two("ON", [P, HALVES, DIM])
        rsum = two("rsum", [P, HALVES, HEADS])
        OT = two("OT", [CH, 2, TOKENS])
        h2 = two("h2", [P, HALVES, DIM])
        x3 = two("x3", [P, HALVES, DIM])
        x3T = two("x3T", [CH, 2, TOKENS])
        rv3 = two("rv3", [P, HALVES, 2])
        rstd3 = two("rstd3", [P, HALVES])
        rv4 = two("rv4", [P, HALVES, 2])
        rstd4 = two("rstd4", [P, HALVES])
        bsr4 = two("bsr4", [P, HALVES, 6])
        bsr3 = two("bsr3", [P, HALVES, 6])
        hid = [fold[:, free_at + s * HT * TOKENS:free_at + (s + 1) * HT * TOKENS].rearrange("p (k t) -> p k t", k=HT) for s in range(2)]
        z = h2

        lmax = sb("lmax", [P, HALVES, SEQS])
        lsum = sb("lsum", [P, HALVES, SEQS])
        lsub = sb("lsub", [P, HALVES, SEQS, EXPERTS])
        lexp = sb("lexp", [P, HALVES, SEQS, EXPERTS])
        PR = sb("PR", [P, HALVES, SEQS, EXPERTS])
        tops = [x3T[i][0:SEQS * EXPERTS, 0, :] for i in range(2)]
        top8 = [sb(f"top8{i}", [SEQS * EXPERTS, 8]) for i in range(2)]
        chosen = x3T[0][0:SEQS * EXPERTS, 1, :]
        MS = sb("MS", [P, HALVES, SEQS, EXPERTS])
        GS = sb("GS", [P, HALVES, SEQS, EXPERTS])

        ld_idx, ld_pos, ld_const, ld_fold = sem("ld_idx"), sem("ld_pos"), sem("ld_const"), sem("ld_fold")
        ld_ln, ld_attn, ld_ffn, ld_w2 = sem("ld_ln"), sem("ld_attn"), sem("ld_ffn"), sem("ld_w2")
        rows_in = sem("rows_in")
        consts_set, dve_consts = sem("consts_set"), sem("dve_consts")
        set_by_act = sem("set_by_act")
        fold_mm, fold_set = sem("fold_mm"), sem("fold_set")
        pre_ffn = sem("pre_ffn")
        out_dma = sem("out_dma")

        a_y, a_yT, a_yTs = sig("a_y"), sig("a_yT"), sig("a_yTs")
        a_q2, a_q2s, a_vp, a_vps = sig("a_q2"), sig("a_q2s"), sig("a_vp"), sig("a_vps")
        a_sc, a_max, a_exp, a_pT, a_pTs = sig("a_sc"), sig("a_max"), sig("a_exp", 2), sig("a_pT"), sig("a_pTs")
        a_ri, a_o, a_res, a_bn, a_ag, a_sq = sig("a_ri"), sig("a_o"), sig("a_res"), sig("a_bn"), sig("a_ag"), sig("a_sq")
        a_st, a_ss, a_nv, a_ve, a_rs, a_n, a_w, a_y1 = (sig(f"a_{x}") for x in ("st", "ss", "nv", "ve", "rs", "n", "w", "y1"))
        a_y1T, a_y1Ts, a_f, a_g, a_r2 = sig("a_y1T"), sig("a_y1Ts"), sig("a_f"), sig("a_g"), sig("a_r2")
        a_bn2, a_ag2, a_sq2, a_st2, a_ss2 = (sig(f"a_{x}") for x in ("bn2", "ag2", "sq2", "st2", "ss2"))
        a_nv2, a_ve2, a_rs2, a_n2, a_w2, a_h = (sig(f"a_{x}") for x in ("nv2", "ve2", "rs2", "n2", "w2", "h"))

        def head_signals(loop, chunks1, chunks2, own):
            names = {
                "bn": 1, "ag": 1, "ve": 1, "rs": 1, "x": 1, "xc": 1, "xT": 1, "xTs": 1,
                "qq": 1, "hq": 1, "qk": 1, "v": 1, "hi": 1, "lo": 1, "dup": 1, "vs": 1,
                "qkT": 1, "qTs": 1, "kTs": 1, "s1": chunks1, "max": chunks1,
                "rT": 1, "rTs": 1, "s2": chunks2, "exp": chunks2,
                "o": 1, "or": 1, "ot": 1, "rec": 1, "on": 1, "o2": 1, "o2s": 1,
            } | own
            return {name: sig(f"{loop}_{name}", per) for name, per in names.items()}

        CAUSAL1 = [(1, 0, 4, 256), (1, 4, 4, 256), (1, 8, 4, 256), (0, 0, 8, 128), (0, 8, 4, 128)]
        CAUSAL2 = [(0, 0, 4, 256), (0, 4, 4, 256), (0, 8, 4, 256), (1, 0, 8, 128), (1, 8, 4, 128)]
        FULL = [(k, h, 4, 256) for k in (0, 1) for h in (0, 4, 8)]
        B_ = head_signals("b", len(CAUSAL1), len(CAUSAL2), {
            "cut": 2, "pj": 1, "h2": 1, "bn3": 1, "ag3": 1, "ve3": 1, "rs3": 1, "x3": 1, "base": 1,
            "x3T": 1, "x3Ts": 1, "lg": 1, "lgs": 1})
        C_ = head_signals("c", len(FULL), len(FULL), {
            "gm": 1, "bt": 1, "hm": 3, "hg": 3, "z": 1, "zb": 1, "zg": 1, "za": 1})
        stored = [sig(f"stored{s}", 8) for s in range(2)]
        cut_waits = sem("cut_waits")
        t_sig = sem("t_sig")
        routed = 6 + 2 * (CAP // 8) + 3 + EXPERTS - 1
        t_pe, t_act = sem("t_pe"), sem("t_act")

        def pipeline(eng, step, stages=3):
            def peeled(i):
                step(*[(i - k, (i - k) % 2) if 0 <= i - k < SEQS else None for k in range(stages)])

            first = stages // 2 * 2
            for i in range(first):
                peeled(i)
            with eng.Fori(first // 2, SEQS // 2) as pair:
                for i in range(2):
                    step(*[(2 * pair + (i - k), (i - k) % 2) for k in range(stages)])
            for i in range(SEQS, SEQS + stages - 1):
                peeled(i)

        def settle(eng):
            eng.wait_ge(ld_const, 32)

        def tiles(T, n):
            return T[:, bass.ds(2 * n, 2), :] if not isinstance(n, int) else T[:, 2 * n:2 * n + 2, :]

        def pair_view(pair, slots, width, lo=0, hi=None):
            v = bank(pair, 2).rearrange("p (b c) -> p b c", b=2)[:, :, 0:slots * width]
            return v.rearrange("p b (i w) -> p b i w", w=width)

        with nc.Block() as start:
            def start_values(share):
                def program(eng):
                    for s in signals[share::5]:
                        eng.sem_inc(s.sem, AHEAD * s.per_seq)
                return program

            for share, on in enumerate((start.sync, start.gpsimd, start.scalar, start.vector, start.tensor)):
                on(start_values(share))

        block = ctx.enter_context(nc.Block())

        @block.sync
        def _(sp):
            sp.dma_start(idx[:], d["idx"]).then_inc(ld_idx, 16)
            sp.dma_start(ident[:], d["ident"]).then_inc(ld_const, 16)
            sp.dma_start(maskf[:], d["mask"]).then_inc(ld_const, 16)
            sp.dma_start(fold_l[:, 0:2], d["fold_l"][:, 0:2]).then_inc(ld_fold, 16)
            sp.dma_start(pos[:], d["pos"]).then_inc(ld_pos, 16)
            sp.dma_start(fold_l[:, 2:4], d["fold_l"][:, 2:4]).then_inc(ld_fold, 16)
            sp.dma_start(fold_r[:], d["fold_r"]).then_inc(ld_fold, 16)
            sp.dma_start(bias_r[:], d["bias_r"]).then_inc(ld_fold, 16)
            sp.dma_start(e_last[:], d["e_last"]).then_inc(ld_fold, 16)
            for t, name in ((ln1w, "ln1_w"), (ln1b, "ln1_b"), (ln2w, "ln2_w"), (ln2b, "ln2_b")):
                sp.dma_start(t[:], d[name].rearrange("(h p) c -> p h c", p=P)).then_inc(ld_ln, 16)
            sp.dma_start(wqkv[:], d["wqkv"]).then_inc(ld_attn, 16)
            sp.dma_start(wproj[:], d["wproj"]).then_inc(ld_attn, 16)
            sp.dma_start(wrout[:], d["wrout"]).then_inc(ld_attn, 16)
            sp.dma_start(w1[:], d["w1"]).then_inc(ld_ffn, 16)
            sp.dma_start(b2ab[:], d["b2"].partition_broadcast(P)).then_inc(ld_ffn, 16)
            sp.dma_start(gamma[:, 0, :], d["gamma"].partition_broadcast(P)).then_inc(ld_ffn, 16)
            sp.dma_start(beta[:, 0, :], d["beta"].partition_broadcast(P)).then_inc(ld_ffn, 16)
            sp.wait_ge(fold_mm, 3)
            sp.dma_start(w2ab[:], d["w2"]).then_inc(ld_w2, 16)

            def store(n, s):
                sp.wait_ge(C_["za"].sem, C_["za"].done(n))
                dst = d["out"][bass.ds(n, 1)] if not isinstance(n, int) else d["out"][n:n + 1]
                sp.dma_start(dst.rearrange("a (h p) c -> p (a h) c", p=P), z[s][:]).then_inc(stored[s].sem, 16)

            with sp.Fori(0, SEQS // 2) as pair:
                store(2 * pair, 0)
                store(2 * pair + 1, 1)
            for s in range(2):
                sp.wait_ge(stored[s].sem, stored[s].done(SEQS - 2, 16))

        @block.gpsimd
        def _(pool):
            pool.wait_ge(ld_idx, 16)
            for t in range(SEQS * HALVES):
                pool.indirect_dma_start(X[:, t, 0:DIM], None, d["emb"],
                                        bass.IndirectOffsetOnAxis(ap=idx[:, t:t + 1], axis=0)).then_inc(rows_in, 16)
            pool.memset(half_neg[:], -0.5).then_inc(consts_set, 1)
            pool.memset(mean_of[:], 1.0 / P).then_inc(consts_set, 1)
            for s in range(2):
                pool.memset(ys[s][:, :, DIM:DIM + 1], 1.0).then_inc(consts_set, 1)
                pool.memset(y1[s][:, :, DIM:DIM + 1], 1.0).then_inc(consts_set, 1)
                pool.memset(QS[s][:], 0.0).then_inc(consts_set, 1)
                pool.memset(VA[s][:], 1.0).then_inc(consts_set, 1)
            pool.wait_ge(consts_set, 10)
            for s in range(2):
                pool.memset(QS[s][:, :, HEADS:, 3 * HD:3 * HD + 1], 1.0).then_inc(consts_set, 1)
            pool.wait_ge(consts_set, 12)

            def power(out, var, s, have, freed, sig_out, n):
                pool.wait_ge(have.sem, have.done(n))
                pool.wait_ge(freed.sem, freed.freed(n))
                nc.gpsimd.tensor_tensor(out, var, half_neg[:, 0:var.shape[1]], ALU.pow).then_inc(sig_out.sem, 1)

            def tok_step(new, mid, back, last):
                if mid:
                    n, s = mid
                    power(st[s][:, 3:4], st[s][:, 2:3], s, a_ve, a_n, a_rs, n)
                    pool.wait_ge(a_n.sem, a_n.done(n))
                    pool.wait_ge(ld_ln, 64)
                    nc.gpsimd.tensor_tensor(r1[s][:], r1[s][:], ln1w[:], ALU.mult).then_inc(a_w.sem, 1)
                if back:
                    n, s = back
                    power(st2[s][:, 3:4], st2[s][:, 2:3], s, a_ve2, a_n2, a_rs2, n)
                    pool.wait_ge(a_n2.sem, a_n2.done(n))
                    nc.gpsimd.tensor_tensor(r2[s][:], r2[s][:], ln2w[:], ALU.mult).then_inc(a_w2.sem, 1)
                    pool.wait_ge(a_w2.sem, a_w2.done(n))
                    nc.gpsimd.tensor_tensor(tiles(H, n), r2[s][:], ln2b[:], ALU.add).then_inc(a_h.sem, 1)
                if last:
                    n, s = last
                    S = B_
                    power(rstd[s][:], rv[s][:, :, 1], s, S["ve"], S["x"], S["rs"], n)

            pipeline(pool, tok_step, 4)

            zero = pool.to_reg(0.0)

            def causal_step(new, mid, back):
                S = B_
                if new:
                    n, s = new
                    settle(pool)
                    pool.wait_ge(S["x"].sem, S["x"].done(n))
                    pool.wait_ge(S["xT"].sem, S["xT"].freed(n))
                    nc.gpsimd.tensor_copy(xs[s][:, :, 0:DIM], tiles(X, n)[:, :, 0:DIM]).then_inc(S["xc"].sem, 1)
                if back:
                    n, s = back
                    power(rstd3[s][:], rv3[s][:, :, 1], s, S["ve3"], S["x3"], S["rs3"], n)
                    pool.wait_ge(S["x3"].sem, S["x3"].done(n))
                    power(rstd4[s][:], rv4[s][:, :, 1], s, C_["ve"], C_["x"], C_["rs"], n)
                    nc.gpsimd.tensor_tensor(tiles(BASE, n), h2[s][:], x3[s][:], ALU.add).then_inc(S["base"].sem, 1)
                if mid:
                    n, s = mid
                    for k, (col, last) in enumerate(((0, 3), (TOKENS, 5))):
                        pool.wait_ge(S["exp"].sem, S["exp"].done(n, last))
                        pool.sem_inc(cut_waits, 1)
                        v = PT[s][:, :, col:col + P]
                        nc.gpsimd.affine_select(out=v, in_=v, compare_op=ALU.is_ge, fill=zero, base=0,
                                                pattern=[[0, HEADS], [1, P]], channel_multiplier=-1).then_inc(S["cut"].sem, 1)
                if back:
                    n, s = back
                    xn = tiles(X, n)[:, :, 0:DIM]
                    settle(pool)
                    pool.wait_ge(C_["x"].sem, C_["x"].done(n))
                    nc.gpsimd.tensor_tensor(xn, xn, gamma[:].to_broadcast([P, HALVES, DIM]), ALU.mult).then_inc(C_["gm"].sem, 1)
                    settle(pool)
                    pool.wait_ge(C_["gm"].sem, C_["gm"].done(n))
                    nc.gpsimd.tensor_tensor(xn, xn, beta[:].to_broadcast([P, HALVES, DIM]), ALU.add).then_inc(C_["bt"].sem, 1)

            pool.wait_ge(ld_ffn, 4 * 16)
            pipeline(pool, causal_step)

            pool.wait_ge(ld_w2, 16)
            nc.gpsimd.tensor_tensor(w2[:], w2ab[:, 0], w2ab[:, 1], ALU.add).then_inc(pre_ffn, 1)
            for h in range(HALVES):
                nc.gpsimd.tensor_tensor(b2[:, h], b2ab[:, 0], b2ab[:, 1], ALU.add).then_inc(pre_ffn, 1)

            def region(dst, src, W, n):
                for e, (lo, hi) in enumerate(REGIONS):
                    w = (W[:, :, bass.ds(n, 1), e:e + 1] if not isinstance(n, int) else W[:, :, n:n + 1, e:e + 1])
                    w = w.rearrange("p a b c -> p a (b c)").to_broadcast([P, HALVES, hi - lo])
                    i = nc.gpsimd.tensor_tensor(dst[:, :, lo:hi], src[:, :, lo:hi], w, ALU.mult)
                return i

            pool.wait_ge(B_["xT"].sem, B_["xT"].done(SEQS - 1))
            pool.wait_ge(C_["bt"].sem, C_["bt"].done(SEQS - 1))
            pool.wait_ge(t_sig, routed)

            def stage(n, s):
                S = C_
                w = MS[:, :, bass.ds(n, 1), 0:1] if not isinstance(n, int) else MS[:, :, n:n + 1, 0:1]
                settle(pool)
                pool.wait_ge(S["xT"].sem, S["xT"].freed(n))
                nc.gpsimd.tensor_copy(xs[s][:, :, DIM:DIM + 1], w.rearrange("p a b c -> p a (b c)"))
                region(xs[s], tiles(X, n), MS, n).then_inc(S["xc"].sem, 1)

            def ffn_step(new, mid, back, last):
                S = C_
                if new:
                    stage(*new)
                if last:
                    n, s = last
                    settle(pool)
                    pool.wait_ge(S["zb"].sem, S["zb"].done(n))
                    region(z[s], z[s], GS, n).then_inc(S["zg"].sem, 1)
                    pool.wait_ge(S["zg"].sem, S["zg"].done(n))
                    nc.gpsimd.tensor_tensor(z[s][:], z[s][:], tiles(BASE, n), ALU.add).then_inc(S["za"].sem, 1)

            pipeline(pool, ffn_step, 4)

        @block.scalar
        def _(act):
            def evac(dst, src, ready, freed, made, n, extra=()):
                act.wait_ge(ready.sem, ready.done(n))
                act.wait_ge(freed.sem, freed.freed(n))
                nc.scalar.copy(dst, src).then_inc(made.sem, 1)

            for k, (w, width) in enumerate(((Aw, DIM + 1), (VO, DIM), (W12, DIM))):
                act.wait_ge(fold_mm, k + 1)
                nc.scalar.copy(w[:].rearrange("p a b -> p (a b)"), bank(k)[0:CH + 1, 0:2 * width]).then_inc(fold_set, 1)

            def tok_step(new, mid, back):
                if new:
                    n, s = new
                    evac(yT[s][:].rearrange("p a b -> p (a b)"), bank(4 * s)[0:CH + 1, :], a_yT, a_sc, a_yTs, n)
                if back:
                    n, s = back
                    evac(y1T[s][:].rearrange("p a b -> p (a b)"), bank(4 * s + 3)[0:CH + 1, :], a_y1T, a_f, a_y1Ts, n)
                if new:
                    n, s = new
                    evac(q2[s][:].rearrange("p a b -> p (a b)"), bank(4 * s + 1)[0:CH + 1, :], a_q2, a_sc, a_q2s, n)
                if back:
                    n, s = back
                    act.wait_ge(a_f.sem, a_f.done(n))
                    act.wait_ge(a_r2.sem, a_r2.freed(n))
                    nc.scalar.activation(g1[s][:].rearrange("p a b -> p (a b)"), bank(4 * s + 3)[:, 0:2 * DIM], ACT.Gelu).then_inc(a_g.sem, 1)
                if new:
                    n, s = new
                    act.wait_ge(a_max.sem, a_max.done(n))
                    act.wait_ge(a_pT.sem, a_pT.freed(n))
                    act.wait_ge(a_ri.sem, a_ri.freed(n))
                    for h in range(HALVES):
                        nc.scalar.activation(pr[s][:, h, :], bank(4 * s)[:, h * TOKENS:(h + 1) * TOKENS], ACT.Exp,
                                             bias=nm[s][:, h:h + 1], accum_out=rs[s][:, h:h + 1]).then_inc(a_exp.sem, 1)

            pipeline(act, tok_step)

            def front_x(S, n, s, rows):
                evac(xT[s][0:rows].rearrange("p a b -> p (a b)"), bank(0)[0:rows, :], S["xT"], S["v"], S["xTs"], n)

            def front_qk(S, n, s):
                act.wait_ge(S["qk"].sem, S["qk"].done(n))
                act.wait_ge(S["qkT"].sem, S["qkT"].freed(n))
                for h in range(HALVES):
                    dst = QS[s][:, h, HEADS:, :].rearrange("p h (a b e) -> p h a b e", a=2, e=HD)[:, :, :, 0, :]
                    src = bank(2)[:, h * DIM:(h + 1) * DIM].rearrange("p (h o e) -> p h o e", o=1, e=HD)
                    i = nc.scalar.copy(dst, src.to_broadcast([P, HEADS, 2, HD]))
                i.then_inc(S["hi"].sem, 1)

            def front_v(S, n, s):
                act.wait_ge(S["v"].sem, S["v"].done(n))
                act.wait_ge(S["o"].sem, S["o"].freed(n))
                v = bank(3)[:, 0:2 * DIM].rearrange("p (b h e) -> p b h e", b=2, e=HD)
                nc.scalar.copy(VA[s][:, :, :, 0:HD], v).then_inc(S["vs"].sem, 1)

            def front_keys(S, n, s):
                act.wait_ge(S["qkT"].sem, S["qkT"].done(n))
                act.wait_ge(S["s2"].sem, S["s2"].freed(n))
                nc.scalar.copy(QT[s][:, 8:, :].rearrange("p a b -> p (a b)"), bank(2).bitcast(F16)).then_inc(S["kTs"].sem, 1)

            def exps(S, chunks, n, s, ks):
                for k in ks:
                    kt, h0, nh, w = chunks[k]
                    act.wait_ge(S["s2"].sem, S["s2"].done(n, k + 1))
                    if k == 0:
                        act.wait_ge(S["o"].sem, S["o"].freed(n))
                    dst = PT[s][:, h0:h0 + nh, kt * TOKENS:kt * TOKENS + w].rearrange("p (i b) w -> p b i w", b=2)
                    nc.scalar.activation(dst, pair_view(6 - 2 * (k % 2), nh // 2, w), ACT.Exp, scale=SCALE).then_inc(S["exp"].sem, 1)

            def raw_heads(S, n, s):
                act.wait_ge(S["o"].sem, S["o"].done(n))
                act.wait_ge(S["ot"].sem, S["ot"].freed(n))
                nc.scalar.copy(OR[s][:].rearrange("p a b -> p (a b)"), bank(4, 2)[:, 0:GROUPS * TOKENS]).then_inc(S["or"].sem, 1)

            def heads_T(S, n, s, used):
                evac(OT[s][:].rearrange("p a b -> p (a b)"), bank(6)[0:CH, :], S["o2"], used, S["o2s"], n)

            def causal_step(new, mid, back):
                S = B_
                if new:
                    front_x(S, *new, CH)
                if mid:
                    exps(S, CAUSAL2, *mid, (0, 1))
                if new:
                    front_qk(S, *new)
                if mid:
                    exps(S, CAUSAL2, *mid, (2,))
                if new:
                    front_v(S, *new)
                if mid:
                    exps(S, CAUSAL2, *mid, (3,))
                if new:
                    front_keys(S, *new)
                if mid:
                    exps(S, CAUSAL2, *mid, (4,))
                if back:
                    n, s = back
                    evac(x3T[s][:].rearrange("p a b -> p (a b)"), bank(6)[0:CH, :], S["x3T"], S["lg"], S["x3Ts"], n)
                if mid:
                    raw_heads(S, *mid)
                    heads_T(S, *mid, S["pj"])

            pipeline(act, causal_step)

            act.wait_ge(t_sig, 2)
            nc.scalar.activation(lexp[:], lsub[:], ACT.Exp).then_inc(t_act, 1)

            def ffn_step(new, mid, back):
                S = C_
                if new:
                    front_x(S, *new, CH + 1)
                if mid:
                    exps(S, FULL, *mid, (0, 1))
                if new:
                    front_qk(S, *new)
                if mid:
                    exps(S, FULL, *mid, (2,))
                if new:
                    front_v(S, *new)
                if mid:
                    exps(S, FULL, *mid, (3,))
                if new:
                    front_keys(S, *new)
                if mid:
                    exps(S, FULL, *mid, (4, 5))
                if mid:
                    n, s = mid
                    for k in range(3):
                        act.wait_ge(S["hm"].sem, S["hm"].done(n, k + 1))
                        if k == 0:
                            act.wait_ge(S["z"].sem, S["z"].freed(n))
                        nc.scalar.activation(hid[s][:, 2 * k:2 * k + 2, :].rearrange("p a b -> p (a b)"), bank(6 + k % 2), ACT.Gelu).then_inc(S["hg"].sem, 1)
                    raw_heads(S, n, s)
                    heads_T(S, n, s, S["z"])

            pipeline(act, ffn_step)

        @block.vector
        def _(dve):
            dve.wait_ge(ld_const, 32)
            nc.vector.tensor_copy(ident16[:], ident[:]).then_inc(dve_consts, 1)
            nc.vector.tensor_copy(identb[:], ident[:]).then_inc(dve_consts, 1)
            for i in range(4):
                nc.vector.tensor_copy(maskb[:, i], maskf[:]).then_inc(dve_consts, 1)
            dve.wait_ge(ld_pos, 16)
            dve.wait_ge(rows_in, 16 * SEQS * HALVES)
            dve.wait_ge(consts_set, 12)

            def whole_norm_stats(x, BS, MV, ready, bn, ag, sq, n):
                dve.wait_ge(ready.sem, ready.done(n))
                dve.wait_ge(sq.sem, sq.freed(n))
                nc.vector.bn_stats(BS[:, 0, :], x.rearrange("p a b -> p (a b)")).then_inc(bn.sem, 1)
                settle(dve)
                dve.wait_ge(bn.sem, bn.done(n))
                nc.vector.bn_aggr(MV[:], BS[:, 0:1, :]).then_inc(ag.sem, 1)
                dve.wait_ge(ag.sem, ag.done(n))
                nc.vector.scalar_tensor_tensor(MV[:, 1:2], MV[:, 0:1], MV[:, 0:1], MV[:, 1:2], ALU.mult, ALU.add).then_inc(sq.sem, 1)

            def whole_norm(x, ST, src, mm, ss, nv, ve, rs_, out_sig, n):
                dve.wait_ge(mm.sem, mm.done(n))
                nc.vector.tensor_copy(ST[:, 0:2], src).then_inc(ss.sem, 1)
                dve.wait_ge(ss.sem, ss.done(n))
                nc.vector.scalar_tensor_tensor(ST[:, 2:3], ST[:, 0:1], ST[:, 0:1], ST[:, 1:2], ALU.mult, ALU.subtract).then_inc(nv.sem, 1)
                dve.wait_ge(nv.sem, nv.done(n))
                nc.vector.tensor_scalar(ST[:, 2:3], ST[:, 2:3], -1.0, EPS_TOK, ALU.mult, ALU.add).then_inc(ve.sem, 1)
                dve.wait_ge(rs_.sem, rs_.done(n))
                nc.vector.tensor_scalar(x, x, ST[:, 0:1], ST[:, 3:4], ALU.subtract, ALU.mult).then_inc(out_sig.sem, 1)

            def row_stats(src, BS, RV, eps, bn, ag, ve, rs_, n):
                dve.wait_ge(ag.sem, ag.freed(n))
                for h in range(HALVES):
                    i = nc.vector.bn_stats(BS[:, h, :], src(h))
                i.then_inc(bn.sem, 1)
                settle(dve)
                dve.wait_ge(bn.sem, bn.done(n))
                dve.wait_ge(rs_.sem, rs_.freed(n))
                for h in range(HALVES):
                    i = nc.vector.bn_aggr(RV[:, h, :], BS[:, h:h + 1, :])
                i.then_inc(ag.sem, 1)
                dve.wait_ge(ag.sem, ag.done(n))
                nc.vector.tensor_scalar(RV[:, :, 1], RV[:, :, 1], eps, None, ALU.add).then_inc(ve.sem, 1)

            def row_apply(src, dst, RV, RSTD, rs_, out_sig, freed, n):
                dve.wait_ge(rs_.sem, rs_.done(n))
                for f in freed:
                    dve.wait_ge(f.sem, f.freed(n))
                for h in range(HALVES):
                    i = nc.vector.tensor_scalar(dst(h), src(h), RV[:, h, 0:1], RSTD[:, h:h + 1], ALU.subtract, ALU.mult)
                i.then_inc(out_sig.sem, 1)

            def tile_of(T, n):
                def tile(h):
                    if isinstance(n, int):
                        return T[:, 2 * n + h, 0:DIM]
                    return T[:, bass.ds(2 * n + h, 1), 0:DIM].rearrange("p a b -> p (a b)")
                return tile

            def tok_step(new, mid, back, last):
                if last:
                    n, s = last
                    S = B_
                    dve.wait_ge(a_h.sem, a_h.done(n))
                    row_stats(tile_of(H, n), bsr[s], rv[s], EPS_ROW, S["bn"], S["ag"], S["ve"], S["rs"], n)
                if new:
                    n, s = new
                    dve.wait_ge(a_yT.sem, a_yT.freed(n))
                    dve.wait_ge(a_res.sem, a_res.freed(n))
                    nc.vector.tensor_tensor(ys[s][:, :, 0:DIM], tiles(X, n)[:, :, 0:DIM], pos[:], ALU.add).then_inc(a_y.sem, 1)
                if mid:
                    n, s = mid
                    dve.wait_ge(a_pT.sem, a_pT.done(n))
                    dve.wait_ge(a_o.sem, a_o.freed(n))
                    nc.vector.tensor_copy(pT[s][:].rearrange("p a b -> p (a b)"), bank(4 * s + 1)).then_inc(a_pTs.sem, 1)
                    dve.wait_ge(a_exp.sem, a_exp.done(n))
                    nc.vector.reciprocal(ri[s][:], rs[s][:]).then_inc(a_ri.sem, 1)
                    dve.wait_ge(a_ri.sem, a_ri.done(n))
                    dve.wait_ge(a_o.sem, a_o.done(n))
                    dve.wait_ge(a_y1.sem, a_y1.freed(n))
                    for h in range(HALVES):
                        i = nc.vector.scalar_tensor_tensor(r1[s][:, h], bank(4 * s + 2)[:, h * DIM:(h + 1) * DIM], ri[s][:, h:h + 1],
                                                           ys[s][:, h, 0:DIM], ALU.mult, ALU.add)
                    i.then_inc(a_res.sem, 1)
                    whole_norm_stats(r1[s][:], bs[s], mv[s], a_res, a_bn, a_ag, a_sq, n)
                if new:
                    n, s = new
                    dve.wait_ge(a_vp.sem, a_vp.done(n))
                    dve.wait_ge(a_o.sem, a_o.freed(n))
                    nc.vector.tensor_copy(vp[s][:].rearrange("p a b -> p (a b)"), bank(4 * s + 2)[:, 0:2 * DIM]).then_inc(a_vps.sem, 1)
                if back:
                    n, s = back
                    dve.wait_ge(a_g.sem, a_g.done(n))
                    dve.wait_ge(a_h.sem, a_h.freed(n))
                    nc.vector.tensor_tensor(r2[s][:], y1[s][:, :, 0:DIM], g1[s][:], ALU.add).then_inc(a_r2.sem, 1)
                    whole_norm_stats(r2[s][:], bs2[s], mv2[s], a_r2, a_bn2, a_ag2, a_sq2, n)
                if mid:
                    n, s = mid
                    whole_norm(r1[s][:], st[s], bank(4 * s + 1)[:, 0:2], a_st, a_ss, a_nv, a_ve, a_rs, a_n, n)
                if new:
                    n, s = new
                    dve.wait_ge(a_sc.sem, a_sc.done(n))
                    dve.wait_ge(a_exp.sem, a_exp.freed(n))
                    nc.vector.tensor_reduce(nm[s][:], bank(4 * s).rearrange("p (h t) -> p h t", h=HALVES), AX.X, ALU.max,
                                            negate=True).then_inc(a_max.sem, 1)
                if mid:
                    n, s = mid
                    dve.wait_ge(a_w.sem, a_w.done(n))
                    dve.wait_ge(a_r2.sem, a_r2.freed(n))
                    dve.wait_ge(a_y1T.sem, a_y1T.freed(n))
                    nc.vector.tensor_tensor(y1[s][:, :, 0:DIM], r1[s][:], ln1b[:], ALU.add).then_inc(a_y1.sem, 1)
                if back:
                    n, s = back
                    whole_norm(r2[s][:], st2[s], bank(4 * s + 3)[:, 0:2], a_st2, a_ss2, a_nv2, a_ve2, a_rs2, a_n2, n)
                if last:
                    n, s = last
                    S = B_
                    row_apply(tile_of(H, n), tile_of(X, n), rv[s], rstd[s], S["rs"], S["x"], [], n)

            pipeline(dve, tok_step, 4)

            def split(S, n, s):
                dve.wait_ge(S["qq"].sem, S["qq"].done(n))
                dve.wait_ge(S["rT"].sem, S["rT"].freed(n))
                for h in range(HALVES):
                    dst = QS[s][:, h, 0:HEADS, 0:2 * HD].rearrange("p h (a e) -> p h a e", e=HD)
                    src = bank(1)[:, h * DIM:(h + 1) * DIM].rearrange("p (h o e) -> p h o e", o=1, e=HD)
                    i = nc.vector.tensor_copy(dst, src.to_broadcast([P, HEADS, 2, HD]))
                i.then_inc(S["hq"].sem, 1)
                for b, (hi, at_, hd0) in enumerate((("hq", 2, 0), ("hi", 1, HEADS))):
                    dve.wait_ge(S[hi].sem, S[hi].done(n))
                    v = bank(1 + b)[:, 0:2 * DIM].rearrange("p (b h e) -> p b h e", b=2, e=HD)
                    i = nc.vector.tensor_tensor(QS[s][:, :, hd0:hd0 + HEADS, at_ * HD:(at_ + 1) * HD], v,
                                                QS[s][:, :, hd0:hd0 + HEADS, 0:HD], ALU.subtract)
                i.then_inc(S["lo"].sem, 1)

            def queries(S, n, s):
                dve.wait_ge(S["qkT"].sem, S["qkT"].done(n))
                dve.wait_ge(S["s2"].sem, S["s2"].freed(n))
                nc.vector.tensor_copy(QT[s][:, 0:8, :].rearrange("p a b -> p (a b)"),
                                      bank(0, 2).bitcast(F16)).then_inc(S["qTs"].sem, 1)

            def maxima(S, chunks, n, s, ks):
                for k in ks:
                    h, h0, nh, w = chunks[k]
                    dve.wait_ge(S["s1"].sem, S["s1"].done(n, k + 1))
                    dst = QS[s][:, h, h0:h0 + nh, 3 * HD].rearrange("p (i b) -> p b i", b=2)
                    nc.vector.tensor_reduce(dst, pair_view(2 * (k % 2), nh // 2, w), AX.X, ALU.max, negate=True).then_inc(S["max"].sem, 1)

            def requeries(S, n, s):
                dve.wait_ge(S["rT"].sem, S["rT"].done(n))
                nc.vector.tensor_copy(QT[s][:, 0:HEADS // 2, :].rearrange("p a b -> p (a b)"),
                                      bank(4, 2).bitcast(F16)[:, 0:HEADS // 2 * TOKENS]).then_inc(S["rTs"].sem, 1)

            def normalise(S, n, s):
                dve.wait_ge(S["ot"].sem, S["ot"].done(n))
                o = bank(4, 2).rearrange("p (a b) -> p a b", a=HALVES)[:, :, 0:HEADS * 2 * HD].rearrange("p a (h e) -> p a h e", e=2 * HD)
                nc.vector.reciprocal(rsum[s][:], o[:, :, :, HD]).then_inc(S["rec"].sem, 1)
                dve.wait_ge(S["rec"].sem, S["rec"].done(n))
                dve.wait_ge(S["o2"].sem, S["o2"].freed(n))
                nc.vector.tensor_tensor(ON[s][:].rearrange("p a (h e) -> p a h e", e=HD), o[:, :, :, 0:HD],
                                        rsum[s][:].unsqueeze(3).to_broadcast([P, HALVES, HEADS, HD]), ALU.mult).then_inc(S["on"].sem, 1)

            def causal_step(new, mid, back):
                S = B_
                if mid:
                    requeries(S, *mid)
                if back:
                    n, s = back
                    dve.wait_ge(S["pj"].sem, S["pj"].done(n))
                    dve.wait_ge(S["base"].sem, S["base"].freed(n))
                    nc.vector.tensor_tensor(h2[s][:], bank(3)[:, 0:2 * DIM].rearrange("p (a b) -> p a b", a=2), tiles(H, n), ALU.add).then_inc(S["h2"].sem, 1)
                    dve.wait_ge(S["h2"].sem, S["h2"].done(n))
                    row_stats(lambda h: h2[s][:, h], bsr3[s], rv3[s], EPS_ROW, S["bn3"], S["ag3"], S["ve3"], S["rs3"], n)
                if new:
                    split(S, *new)
                if back:
                    n, s = back
                    row_apply(lambda h: h2[s][:, h], lambda h: x3[s][:, h], rv3[s], rstd3[s], S["rs3"], S["x3"], [S["x3T"], C_["x"]], n)
                if new:
                    queries(S, *new)
                if back:
                    n, s = back
                    dve.wait_ge(S["x3"].sem, S["x3"].done(n))
                    row_stats(lambda h: x3[s][:, h], bsr4[s], rv4[s], EPS_FFN, C_["bn"], C_["ag"], C_["ve"], C_["rs"], n)
                if new:
                    maxima(S, CAUSAL1, *new, (0, 1))
                if back:
                    n, s = back
                    dve.wait_ge(S["xc"].sem, S["xc"].done(n))
                    row_apply(lambda h: x3[s][:, h], tile_of(X, n), rv4[s], rstd4[s], C_["rs"], C_["x"], [], n)
                if new:
                    maxima(S, CAUSAL1, *new, (2, 3, 4))
                if mid:
                    normalise(S, *mid)
                if back:
                    n, s = back
                    dve.wait_ge(S["lg"].sem, S["lg"].done(n))
                    dst = LG[:, :, bass.ds(n, 1), :] if not isinstance(n, int) else LG[:, :, n:n + 1, :]
                    nc.vector.tensor_copy(dst, bank(7)[:, 0:2 * EXPERTS].rearrange("p (a o b) -> p a o b", a=2, o=1)).then_inc(S["lgs"].sem, 1)

            pipeline(dve, causal_step)

            count = [0]

            def link(i):
                count[0] += 1
                i.then_inc(t_sig, 1)
                dve.wait_ge(t_sig, count[0])

            dve.wait_ge(B_["lgs"].sem, B_["lgs"].done(SEQS - 1))
            wide = [P, HALVES, SEQS, EXPERTS]
            link(nc.vector.tensor_reduce(lmax[:], LG[:], AX.X, ALU.max))
            link(nc.vector.tensor_tensor(lsub[:], LG[:], lmax[:].unsqueeze(3).to_broadcast(wide), ALU.subtract))
            dve.wait_ge(t_act, 1)
            link(nc.vector.tensor_reduce(lsum[:], lexp[:], AX.X, ALU.add))
            link(nc.vector.reciprocal(lsum[:], lsum[:]))
            link(nc.vector.tensor_tensor(PR[:], lexp[:], lsum[:].unsqueeze(3).to_broadcast(wide), ALU.mult))
            dve.wait_ge(t_pe, 1)
            link(nc.vector.tensor_copy(tops[0], bank(0)[0:SEQS * EXPERTS, 0:TOKENS]))
            for r in range(CAP // 8):
                link(nc.vector.max(top8[r % 2][:], tops[r % 2]))
                link(nc.vector.match_replace(tops[1 - r % 2], top8[r % 2][:], tops[r % 2], -1.0))
            link(nc.vector.tensor_scalar(chosen, tops[CAP // 8 % 2], -1.0, None, ALU.is_equal))
            dve.wait_ge(t_pe, 2)
            link(nc.vector.tensor_copy(MS[:].rearrange("p a b c -> p (a b c)"), bank(1)[:, 0:HALVES * SEQS * EXPERTS]))
            link(nc.vector.tensor_tensor(GS[:], MS[:], PR[:], ALU.mult))
            for e in range(EXPERTS - 2, -1, -1):
                nc.vector.tensor_tensor(MS[:, :, :, e], MS[:, :, :, e], MS[:, :, :, e + 1], ALU.add)
                link(nc.vector.tensor_tensor(GS[:, :, :, e], GS[:, :, :, e], GS[:, :, :, e + 1], ALU.add))

            def ffn_step(new, mid, back):
                S = C_
                if mid:
                    requeries(S, *mid)
                if new:
                    n, s = new
                    split(S, n, s)
                    queries(S, n, s)
                    maxima(S, FULL, n, s, range(len(FULL)))
                if mid:
                    normalise(S, *mid)
                if back:
                    n, s = back
                    dve.wait_ge(S["z"].sem, S["z"].done(n))
                    dve.wait_ge(stored[s].sem, stored[s].freed(n - s, 16))
                    nc.vector.tensor_tensor(z[s][:], bank(7)[:, 0:2 * DIM].rearrange("p (a b) -> p a b", a=2), b2[:], ALU.add).then_inc(S["zb"].sem, 1)

            dve.wait_ge(pre_ffn, 3)
            pipeline(dve, ffn_step)

        @block.tensor
        def _(pe):
            def mm(out, l, r, start=True, stop=True, free=False):
                return nc.tensor.matmul(out, l, r, start=start, stop=stop, skip_group_check=free)

            def rows(c):
                return CH + c

            pe.wait_ge(ld_fold, 80)
            pe.wait_ge(ld_const, 32)
            pe.wait_ge(consts_set, 12)
            pe.wait_ge(dve_consts, 6)
            for b, (left, right, width, bias) in enumerate((((0), None, DIM + 1, None), (2, 0, DIM, 0), (3, 1, DIM, 1))):
                for c in range(2):
                    lo = c * CH
                    out = bank(b)[0:CH + 1, c * width:(c + 1) * width]
                    for k in range(HT):
                        r = fold_l[:, 1, k, :] if right is None else fold_r[:, right, k, :]
                        i = mm(out, fold_l[:, left, k, lo:lo + CH + 1], r, start=(k == 0), stop=(k == HT - 1 and bias is None))
                    if bias is not None:
                        i = mm(out, e_last[0:1, lo:lo + CH + 1], bias_r[0:1, bias, :], start=False, stop=True)
                i.then_inc(fold_mm, 1)
            pe.wait_ge(fold_set, 3)

            def transposes(dst, src, width, ready, n, made):
                pe.wait_ge(ready.sem, ready.done(n))
                for c in range(2):
                    for h in range(HALVES):
                        i = nc.tensor.transpose(dst[0:width, c * TOKENS + h * P:c * TOKENS + (h + 1) * P],
                                                src[:, h, c * CH:c * CH + width], ident[:])
                i.then_inc(made.sem, 1)

            def tok_front1(n, s):
                pe.wait_ge(a_exp.sem, a_exp.freed(n))
                transposes(bank(4 * s), ys[s], CH + 1, a_y, n, a_yT)

            def tok_front2(n, s):
                pe.wait_ge(a_yTs.sem, a_yTs.done(n))
                pe.wait_ge(a_ss.sem, a_ss.freed(n))
                for m in range(2):
                    for c in range(2):
                        i = mm(bank(4 * s + 1)[0:CH + 1, m * TOKENS:(m + 1) * TOKENS], Aw[0:rows(c), c, m * CH:m * CH + CH + 1],
                               yT[s][0:rows(c), c, :], start=(c == 0), stop=(c == 1))
                i.then_inc(a_q2.sem, 1)
                pe.wait_ge(a_res.sem, a_res.freed(n))
                for h in range(HALVES):
                    for c in range(2):
                        i = mm(bank(4 * s + 2)[:, h * DIM:(h + 1) * DIM], yT[s][0:rows(c), c, h * P:(h + 1) * P], VO[0:rows(c), c, :],
                               start=(c == 0), stop=(c == 1))
                i.then_inc(a_vp.sem, 1)

            def tok_scores(n, s):
                pe.wait_ge(a_q2s.sem, a_q2s.done(n))
                for h in range(HALVES):
                    for c in range(2):
                        i = mm(bank(4 * s)[:, h * TOKENS:(h + 1) * TOKENS], q2[s][0:rows(c), c, h * P:(h + 1) * P], yT[s][0:rows(c), c, :],
                               start=(c == 0), stop=(c == 1))
                i.then_inc(a_sc.sem, 1)

            def tok_pT(n, s):
                pe.wait_ge(a_exp.sem, a_exp.done(n))
                for k in range(HALVES):
                    for h in range(HALVES):
                        i = nc.tensor.transpose(bank(4 * s + 1)[:, k * TOKENS + h * P:k * TOKENS + (h + 1) * P],
                                                pr[s][:, h, k * P:(k + 1) * P], ident[:])
                i.then_inc(a_pT.sem, 1)

            def tok_out(n, s):
                pe.wait_ge(a_pTs.sem, a_pTs.done(n))
                pe.wait_ge(a_vps.sem, a_vps.done(n))
                for h in range(HALVES):
                    for k in range(HALVES):
                        i = mm(bank(4 * s + 2)[:, h * DIM:(h + 1) * DIM], pT[s][:, k, h * P:(h + 1) * P], vp[s][:, k, :],
                               start=(k == 0), stop=(k == 1))
                i.then_inc(a_o.sem, 1)

            def tok_step(new, mid, back):
                if mid:
                    tok_pT(*mid)
                if new:
                    tok_front1(*new)
                if back:
                    n, s = back
                    pe.wait_ge(a_ss2.sem, a_ss2.freed(n))
                    transposes(bank(4 * s + 3), y1[s], CH + 1, a_y1, n, a_y1T)
                if mid:
                    tok_out(*mid)
                if new:
                    tok_front2(*new)
                if back:
                    n, s = back
                    pe.wait_ge(a_y1Ts.sem, a_y1Ts.done(n))
                    for h in range(HALVES):
                        for c in range(2):
                            i = mm(bank(4 * s + 3)[:, h * DIM:(h + 1) * DIM], y1T[s][0:rows(c), c, h * P:(h + 1) * P], W12[0:rows(c), c, :],
                                   start=(c == 0), stop=(c == 1))
                    i.then_inc(a_f.sem, 1)
                if mid:
                    n, s = mid
                    pe.wait_ge(a_sq.sem, a_sq.done(n))
                    mm(bank(4 * s + 1)[:, 0:2], mean_of[:], mv[s][:]).then_inc(a_st.sem, 1)
                if new:
                    tok_scores(*new)
                if back:
                    n, s = back
                    pe.wait_ge(a_sq2.sem, a_sq2.done(n))
                    mm(bank(4 * s + 3)[:, 0:2], mean_of[:], mv2[s][:]).then_inc(a_st2.sem, 1)

            pipeline(pe, tok_step)

            def front_qk(S, n, s, W, col, K):
                pe.wait_ge(S["xTs"].sem, S["xTs"].done(n))
                for m in range(2):
                    for h in range(HALVES):
                        for c in range(2):
                            i = mm(bank(1 + m)[:, h * DIM:(h + 1) * DIM], xT[s][0:K[c], c, h * P:(h + 1) * P],
                                   W[0:K[c], c, col + m * DIM:col + (m + 1) * DIM], start=(c == 0), stop=(c == 1))
                    i.then_inc(S["qq" if m == 0 else "qk"].sem, 1)

            def front_v(S, n, s, W, col, K):
                for h in range(HALVES):
                    for c in range(2):
                        i = mm(bank(3)[:, h * DIM:(h + 1) * DIM], xT[s][0:K[c], c, h * P:(h + 1) * P], W[0:K[c], c, col + 2 * DIM:col + 3 * DIM],
                               start=(c == 0), stop=(c == 1))
                i.then_inc(S["v"].sem, 1)

            def slots_T(dst, s, blocks):
                for j, b in enumerate(blocks):
                    for h in range(HALVES):
                        i = nc.tensor.transpose(dst[:, j * TOKENS + h * P:j * TOKENS + (h + 1) * P],
                                                QS[s][:, h, 2 * b:2 * b + 2, :].rearrange("p a b -> p (a b)"), ident16[:])
                return i

            def front_T(S, n, s):
                pe.wait_ge(S["hi"].sem, S["hi"].done(n))
                pe.wait_ge(S["lo"].sem, S["lo"].done(n))
                slots_T(bank(0, 3).bitcast(F16), s, range(HEADS)).then_inc(S["qkT"].sem, 1)

            def head_rows(t, h):
                return t[SLOT * (h % 2):SLOT * (h % 2) + SLOT]

            def front_s1(S, chunks, n, s, ks, causal):
                for k in ks:
                    half, h0, nh, w = chunks[k]
                    if k == 0:
                        pe.wait_ge(S["qTs"].sem, S["qTs"].done(n))
                        pe.wait_ge(S["kTs"].sem, S["kTs"].done(n))
                    if k == 1:
                        pe.wait_ge(S["vs"].sem, S["vs"].done(n))
                    if k >= 2:
                        pe.wait_ge(S["max"].sem, S["max"].done(n, k - 1))
                    pair = 2 * (k % 2)
                    if causal:
                        for b in range(2):
                            v = bank(pair + b)[:, 0:nh // 2 * w].rearrange("p (i w) -> p i w", w=w)[:, :, w - P:w]
                            mm(v, identb[:], maskb[:, 0:nh // 2, :], start=True, stop=False, free=True)
                    for j in range(nh):
                        h = h0 + j
                        i = mm(bank(pair + j % 2)[:, j // 2 * w:(j // 2 + 1) * w], head_rows(QT[s], h)[:, h // 2, half * P:(half + 1) * P],
                               head_rows(QT[s], h)[:, HEADS // 2 + h // 2, 0:w], start=(not causal and j < 2), stop=(j >= nh - 2), free=True)
                    i.then_inc(S["s1"].sem, 1)

            def mid_rT(S, n, s):
                pe.wait_ge(S["max"].sem, S["max"].done(n))
                pe.wait_ge(S["on"].sem, S["on"].done(n - 1))
                slots_T(bank(4, 2).bitcast(F16), s, range(HEADS // 2)).then_inc(S["rT"].sem, 1)

            def mid_s2(S, chunks, n, s, ks):
                for k in ks:
                    kt, h0, nh, w = chunks[k]
                    if k == 0:
                        pe.wait_ge(S["rTs"].sem, S["rTs"].done(n))
                    if k >= 2:
                        pe.wait_ge(S["exp"].sem, S["exp"].done(n, k - 1))
                    pair = 6 - 2 * (k % 2)
                    for j in range(nh):
                        h = h0 + j
                        i = mm(bank(pair + j % 2)[:, j // 2 * w:(j // 2 + 1) * w], head_rows(QT[s], h)[:, HEADS // 2 + h // 2, kt * P:(kt + 1) * P],
                               head_rows(QT[s], h)[:, h // 2, TOKENS - w:TOKENS], start=(j < 2), stop=(j >= nh - 2), free=True)
                    i.then_inc(S["s2"].sem, 1)

            def mid_pv(S, n, s, w1_, g):
                if g == 0:
                    pe.wait_ge(S["exp"].sem, S["exp"].done(n))
                for kt, w in ((0, TOKENS), (1, w1_)):
                    for j in range(4):
                        i = mm(bank(4, 2)[32 * j:32 * j + 32, g * TOKENS + TOKENS - w:(g + 1) * TOKENS], VA[s][:, kt, 4 * g + j, :],
                               PT[s][:, 4 * g + j, kt * TOKENS:kt * TOKENS + w], start=(kt == 0), stop=(kt == 1), free=True)
                if g == GROUPS - 1:
                    i.then_inc(S["o"].sem, 1)

            def mid_tokens(S, n, s):
                pe.wait_ge(S["or"].sem, S["or"].done(n))
                for h in range(HALVES):
                    for g in range(GROUPS):
                        i = nc.tensor.transpose(bank(4 + h)[:, g * P:(g + 1) * P], OR[s][:, g, h * P:(h + 1) * P], ident[:])
                i.then_inc(S["ot"].sem, 1)

            def causal_step(new, mid, back):
                S = B_
                W = (wqkv, 0, (CH, CH))
                if mid:
                    mid_rT(S, *mid)
                if back:
                    n, s = back
                    pe.wait_ge(S["o2s"].sem, S["o2s"].done(n))
                    for h in range(HALVES):
                        for c in range(2):
                            i = mm(bank(3)[:, h * DIM:(h + 1) * DIM], OT[s][:, c, h * P:(h + 1) * P], wproj[:, c, :],
                                   start=(c == 0), stop=(c == 1))
                    i.then_inc(S["pj"].sem, 1)
                if new:
                    transposes(bank(0), xs[new[1]], CH, S["xc"], new[0], S["xT"])
                if mid:
                    n, s = mid
                    pe.wait_ge(S["lgs"].sem, S["lgs"].freed(n))
                    mid_s2(S, CAUSAL2, n, s, (0,))
                if new:
                    front_qk(S, *new, *W)
                if mid:
                    mid_s2(S, CAUSAL2, *mid, (1,))
                if mid:
                    mid_s2(S, CAUSAL2, *mid, (2,))
                if back:
                    n, s = back
                    pe.wait_ge(S["h2"].sem, S["h2"].done(n))
                if new:
                    front_v(S, *new, *W)
                if mid:
                    mid_s2(S, CAUSAL2, *mid, (3,))
                if new:
                    front_T(S, *new)
                if mid:
                    mid_s2(S, CAUSAL2, *mid, (4,))
                if new:
                    front_s1(S, CAUSAL1, *new, (0, 1), True)
                if back:
                    n, s = back
                    if mid:
                        pe.wait_ge(S["exp"].sem, S["exp"].done(n + 1))
                    transposes(bank(6), x3[s], CH, S["x3"], n, S["x3T"])
                if mid:
                    n, s = mid
                    pe.wait_ge(S["cut"].sem, S["cut"].done(n))
                for g in range(GROUPS):
                    if mid:
                        mid_pv(S, *mid, P, g)
                    if new:
                        front_s1(S, CAUSAL1, *new, (2 + g,), True)
                if back:
                    n, s = back
                    pe.wait_ge(S["x3Ts"].sem, S["x3Ts"].done(n))
                    pe.wait_ge(S["lgs"].sem, S["lgs"].done(n - 1))
                    for h in range(HALVES):
                        for c in range(2):
                            i = mm(bank(7)[:, h * EXPERTS:(h + 1) * EXPERTS], x3T[s][:, c, h * P:(h + 1) * P], wrout[:, c, :],
                                   start=(c == 0), stop=(c == 1))
                    i.then_inc(S["lg"].sem, 1)
                if mid:
                    mid_tokens(S, *mid)
                    n, s = mid
                    transposes(bank(6), ON[s], CH, S["on"], n, S["o2"])

            pe.wait_ge(ld_attn, 48)
            pipeline(pe, causal_step)

            pe.wait_ge(t_sig, 5)
            for h in range(HALVES):
                i = nc.tensor.transpose(bank(0)[0:SEQS * EXPERTS, h * P:(h + 1) * P], PR[:, h].rearrange("p a b -> p (a b)"), ident[:])
            i.then_inc(t_pe, 1)
            pe.wait_ge(t_sig, 6 + 2 * (CAP // 8) + 1)
            for h in range(HALVES):
                i = nc.tensor.transpose(bank(1)[:, h * SEQS * EXPERTS:(h + 1) * SEQS * EXPERTS], chosen[:, h * P:(h + 1) * P],
                                        ident[0:SEQS * EXPERTS, 0:SEQS * EXPERTS])
            i.then_inc(t_pe, 1)
            pe.wait_ge(t_sig, 6 + 2 * (CAP // 8) + 2)

            def mid_hidden(S, n, s, k):
                if k == 0:
                    pe.wait_ge(S["exp"].sem, S["exp"].done(n, 5))
                if k == 2:
                    pe.wait_ge(S["hg"].sem, S["hg"].done(n, 1))
                for m in (2 * k, 2 * k + 1):
                    for c in range(2):
                        i = mm(bank(6 + k % 2)[:, m % 2 * TOKENS:(m % 2 + 1) * TOKENS], w1[0:rows(c), c, m * P:(m + 1) * P],
                               xT[s][0:rows(c), c, :], start=(c == 0), stop=(c == 1))
                i.then_inc(S["hm"].sem, 1)

            def back_fc2(S, n, s, h):
                for k in range(HT + 2):
                    l = hid[s][:, k, h * P:(h + 1) * P] if k < HT else OT[s][:, k - HT, h * P:(h + 1) * P]
                    i = mm(bank(7)[:, h * DIM:(h + 1) * DIM], l, w2[0:l.shape[0], k, :], start=(k == 0), stop=(k == HT + 1))
                return i

            def ffn_step(new, mid, back):
                S = C_
                W = (w1, HIDDEN, (CH, CH + 1))
                if mid:
                    mid_rT(S, *mid)
                if new:
                    transposes(bank(0), xs[new[1]], CH + 1, S["xc"], new[0], S["xT"])
                if mid:
                    n, s = mid
                    pe.wait_ge(S["zb"].sem, S["zb"].freed(n))
                    pe.wait_ge(S["o2s"].sem, S["o2s"].done(n - 1))
                    mid_s2(S, FULL, n, s, (0,))
                if new:
                    front_qk(S, *new, *W)
                if mid:
                    mid_s2(S, FULL, *mid, (1,))
                if mid:
                    mid_s2(S, FULL, *mid, (2,))
                if new:
                    front_v(S, *new, *W)
                if mid:
                    mid_s2(S, FULL, *mid, (3,))
                if new:
                    front_T(S, *new)
                if mid:
                    mid_s2(S, FULL, *mid, (4, 5))
                rest = [lambda: mid_hidden(S, *mid, 0), lambda: mid_hidden(S, *mid, 1), lambda: mid_pv(S, *mid, TOKENS, 0),
                        lambda: mid_hidden(S, *mid, 2), lambda: mid_pv(S, *mid, TOKENS, 1), lambda: mid_pv(S, *mid, TOKENS, 2)]
                for k, part in enumerate(rest):
                    if mid:
                        part()
                    if new:
                        front_s1(S, FULL, *new, (k,), False)
                if back:
                    n, s = back
                    if mid:
                        pe.wait_ge(S["hg"].sem, S["hg"].done(n + 1, 2))
                    pe.wait_ge(S["o2s"].sem, S["o2s"].done(n))
                    pe.wait_ge(S["zb"].sem, S["zb"].done(n - 1))
                    back_fc2(S, n, s, 0)
                if mid:
                    mid_tokens(S, *mid)
                if back:
                    back_fc2(S, *back, 1).then_inc(S["z"].sem, 1)
                if mid:
                    n, s = mid
                    pe.wait_ge(S["hg"].sem, S["hg"].done(n))
                    transposes(bank(6), ON[s], CH, S["on"], n, S["o2"])

            pe.wait_ge(ld_ffn, 4 * 16)
            pe.wait_ge(pre_ffn, 3)
            pipeline(pe, ffn_step)


def kernel(**inputs):
    import numpy as np
    import concourse.bacc as bacc
    from concourse.bass_utils import run_bass_kernel_spmd

    a = {k: np.asarray(v) for k, v in inputs.items()}
    tok = lambda k: a["L0_tok_" + k]

    def rows(w):
        return np.ascontiguousarray(w.reshape(-1, P, w.shape[-1]).transpose(1, 0, 2))

    def aug(w, b):
        return rows(np.concatenate([w, b[None]], 0).T)

    def halves(w):
        out = np.zeros((w.shape[0] - CH, 2, w.shape[1]), w.dtype)
        out[:CH, 0] = w[:CH]
        out[:, 1] = w[CH:]
        return out

    def second(w):
        out = np.zeros((P, HT + 2, w.shape[1]), w.dtype)
        out[:, :HT] = rows(w[:HIDDEN])
        out[:CH, HT:] = halves(w[HIDDEN:])
        return out

    f = np.float32
    ang = np.arange(TOKENS, dtype=f)[:, None] / np.power(f(10000.0), np.arange(DIM, dtype=f)[None] / f(DIM)).astype(f)
    pos = np.where((np.arange(DIM) % 2 == 0)[None], np.sin(ang), np.cos(ang)).astype(f)
    causal = np.where(np.arange(P)[None, :] <= np.arange(P)[:, None], f(0), f(MASKED)).astype(f)
    w2 = a["L0_ffn_w2"]
    split2 = [second(w.T) for w in (w2[:DIM], w2[DIM:])]
    arrays = {
        "idx": np.ascontiguousarray(a["x"].reshape(SEQS * HALVES, P).T),
        "emb": tok("emb"),
        "pos": np.ascontiguousarray(pos.reshape(HALVES, P, DIM).transpose(1, 0, 2)),
        "ident": np.eye(P, dtype=f),
        "mask": causal,
        "fold_l": np.stack([aug(tok("W" + k), tok("b" + k)) for k in ("q", "k", "v", "1")], 1),
        "fold_r": np.stack([rows(tok("Wo")), rows(tok("W2"))], 1),
        "bias_r": np.stack([tok("bo"), tok("b2")])[None],
        "e_last": np.eye(DIM + 1, dtype=f)[DIM:],
        "ln1_w": tok("ln1_w"), "ln1_b": tok("ln1_b"), "ln2_w": tok("ln2_w"), "ln2_b": tok("ln2_b"),
        "wqkv": halves(a["L0_attn_W_qkv"].T),
        "wproj": halves(a["L0_attn_W_proj"].T),
        "wrout": halves(a["L0_ffn_w_router"].T),
        "w1": halves(np.concatenate([a["L0_ffn_w1"].T, a["L0_ffn_b1"][None]], 0)),
        "w2": np.stack(split2, 1),
        "b2": a["L0_ffn_b2"].reshape(2, DIM),
        "gamma": a["L0_ffn_gamma1"], "beta": a["L0_ffn_beta1"],
    }
    arrays = {k: np.ascontiguousarray(v) for k, v in arrays.items()}
    nc = bacc.Bacc("TRN2", target_bir_lowering=False, num_devices=1)
    d = {k: nc.dram_tensor("in_" + k, v.shape, mybir.dt.from_np(v.dtype), kind="ExternalInput").ap() for k, v in arrays.items()}
    d["out"] = nc.dram_tensor("out", (SEQS, TOKENS, DIM), F32, kind="ExternalOutput").ap()
    build(nc, d)
    r = run_bass_kernel_spmd(nc, [{"in_" + k: v for k, v in arrays.items()}], core_ids=[0])
    return r.results[0]["out"]
```

```python
from contextlib import ExitStack

import concourse.bass as bass
from concourse import mybir

F32 = mybir.dt.float32
F16 = mybir.dt.float16
BF16 = mybir.dt.bfloat16
U32 = mybir.dt.uint32
I32 = mybir.dt.int32
ALU = mybir.AluOpType
ACT = mybir.ActivationFunctionType
AX = mybir.AxisListType

P = 128
SEQS, TOKENS, DIM, HIDDEN = 8, 256, 192, 768
HALVES = TOKENS // P
VOCAB = 8000
CH = DIM // 2
HT = HIDDEN // P
HEADS, HD = 12, 16
GROUPS = HEADS // 4
SLOT = 64
EXPERTS = 4
CAP = TOKENS // 2
REGIONS = [(0, DIM // 8), (DIM // 8, DIM // 4), (DIM // 4, DIM // 2), (DIM // 2, DIM)]
BANK = 512
QKV = 3 * DIM
FC1 = HIDDEN + QKV
SCALE = HD ** -0.5
TAIL = DIM - P
PASSES = [(0, 0, P), (0, 2, P), (2, 0, P), (1, 1, P), (3, 3, TAIL)]
BIASED = PASSES[:-1] + [(3, 3, TAIL + 2)]
WS = 64.0
EPS_TOK, EPS_ROW, EPS_FFN = 1e-5, 1e-5, 1e-6
MASKED = -1e30
AHEAD = 2


class Signal:

    def __init__(self, sem, per_seq):
        self.sem, self.per_seq = sem, per_seq

    def done(self, seq, count=None):
        return seq * self.per_seq + (AHEAD * self.per_seq + (self.per_seq if count is None else count))

    def freed(self, seq, count=None):
        return seq * self.per_seq + (self.per_seq if count is None else count)


def build(nc, d):
    with ExitStack() as ctx:
        def sb(name, shape, dt=F32):
            return ctx.enter_context(nc.sbuf_tensor(name, shape, dt))

        signals = []

        def sig(name, per_seq=1):
            s = Signal(ctx.enter_context(nc.semaphore(name)), per_seq)
            signals.append(s)
            return s

        def sem(name):
            return ctx.enter_context(nc.semaphore(name))

        PS = ctx.enter_context(nc.psum_tensor("PS", [P, 8 * BANK], F32))

        def bank(b, n=1):
            return PS[:, b * BANK:(b + n) * BANK]

        idx = sb("idx", [P, SEQS * HALVES], I32)
        pos = sb("pos", [P, HALVES, DIM])
        ident = sb("ident", [P, P])
        ident16 = sb("ident16", [P, P], F16)
        identb = sb("identb", [P, P], BF16)
        maskf = sb("maskf", [P, P])
        maskb = sb("maskb", [P, 4, P], BF16)
        mean_of = sb("mean_of", [P, P])
        half_neg = sb("half_neg", [P, 3])
        fold = sb("fold", [P, 4 * HT * (DIM + 1) + 2 * HT * DIM])
        fold_l = fold[:, 0:4 * HT * (DIM + 1)].rearrange("p (a k c) -> p a k c", a=4, k=HT)
        fold_r = fold[:, 4 * HT * (DIM + 1):].rearrange("p (a k c) -> p a k c", a=2, k=HT)
        bias_r = sb("bias_r", [1, 2, DIM])
        e_last = sb("e_last", [1, DIM + 1])
        Aw = sb("Aw", [CH + 1, 2, DIM + 1])
        VO = sb("VO", [CH + 1, 2, DIM])
        W12 = sb("W12", [CH + 1, 2, DIM])
        ln1w = sb("ln1w", [P, HALVES, DIM])
        ln1b = sb("ln1b", [P, HALVES, DIM])
        ln2w = sb("ln2w", [P, HALVES, DIM])
        ln2b = sb("ln2b", [P, HALVES, DIM])
        wqkv = sb("wqkv", [P, 4, QKV], F16)
        wproj = sb("wproj", [CH, 2, DIM])
        wrout = sb("wrout", [CH, 2, EXPERTS])
        w1 = sb("w1", [P, 4, FC1], F16)
        free_at = SEQS * HALVES * DIM
        w2ab = fold[:, free_at:free_at + 2 * (HT + 2) * DIM].rearrange("p (a k c) -> p a k c", a=2, k=HT + 2)
        w2h = sb("w2h", [P, HT, DIM], F16)
        w2l = sb("w2l", [P, HT, DIM], F16)
        w2o = sb("w2o", [CH, 2, DIM])
        b2ab = sb("b2ab", [P, 2, DIM])
        b2 = sb("b2", [P, HALVES, DIM])
        gamma = sb("gamma", [P, 1, DIM])
        beta = sb("beta", [P, 1, DIM])

        X = sb("X", [P, SEQS * HALVES, DIM])
        H = sb("H", [P, SEQS * HALVES, DIM])
        BASE = fold[:, 0:SEQS * HALVES * DIM].rearrange("p (t c) -> p t c", c=DIM)
        LG = sb("LG", [P, HALVES, SEQS, EXPERTS])

        def two(name, shape, dt=F32):
            return [sb(f"{name}{s}", shape, dt) for s in range(2)]

        PTf = two("PT", [P, HEADS * 2 * TOKENS])
        at = [0, 0]

        def carve(shape):
            size = shape[1] * shape[2]
            out = []
            for s in range(2):
                out.append(PTf[s][0:shape[0], at[s]:at[s] + size].rearrange("p (a b) -> p a b", a=shape[1]))
                at[s] += size
            return out

        ys = carve([P, HALVES, DIM + 1])
        yT = carve([CH + 1, 2, TOKENS])
        q2 = carve([CH + 1, 2, TOKENS])
        vp = carve([P, HALVES, DIM])
        nm = two("nm", [P, HALVES])
        pr = carve([P, HALVES, TOKENS])
        rs = two("rs", [P, HALVES])
        ri = two("ri", [P, HALVES])
        pT = carve([P, HALVES, TOKENS])
        r1 = carve([P, HALVES, DIM])
        y1 = carve([P, HALVES, DIM + 1])
        y1T = carve([CH + 1, 2, TOKENS])
        g1 = carve([P, HALVES, DIM])
        r2 = carve([P, HALVES, DIM])
        wqkv_raw = PTf[0][:, at[0]:at[0] + 2 * QKV].rearrange("p (k c) -> p k c", k=2)
        w1_raw = PTf[0][:, 0:3 * FC1].rearrange("p (k c) -> p k c", k=3)
        bs = two("bs", [P, 2, 6])
        mv = two("mv", [P, 2])
        st = two("st", [P, 4])
        bs2 = two("bs2", [P, 2, 6])
        mv2 = two("mv2", [P, 2])
        st2 = two("st2", [P, 4])

        rv = two("rv", [P, HALVES, 2])
        rstd = two("rstd", [P, HALVES])
        bsr = two("bsr", [P, HALVES, 6])
        XS = two("XS", [P, HALVES, 4 * P], F16)
        xT = two("xT", [P, 4, TOKENS], F16)
        QS = two("QS", [P, HALVES, 2 * HEADS, SLOT], F16)
        VA = two("VA", [P, HALVES, HEADS, 2 * HD])
        QT = two("QT", [P, HEADS, TOKENS], F16)
        PT = [t[:].rearrange("p (h c) -> p h c", h=HEADS) for t in PTf]
        OR = two("OR", [P, GROUPS, TOKENS])
        ON = two("ON", [P, HALVES, DIM])
        rsum = two("rsum", [P, HALVES, HEADS])
        OT = two("OT", [CH, 2, TOKENS])
        h2 = two("h2", [P, HALVES, DIM])
        xs = two("x3", [P, HALVES, DIM])
        w3_hi = QT[0][:].rearrange("p a b -> p (a b)")[:, 0:FC1]
        x3 = xs
        x3T = two("x3T", [CH, 2, TOKENS])
        rv3 = two("rv3", [P, HALVES, 2])
        rstd3 = two("rstd3", [P, HALVES])
        rv4 = two("rv4", [P, HALVES, 2])
        rstd4 = two("rstd4", [P, HALVES])
        bsr4 = two("bsr4", [P, HALVES, 6])
        bsr3 = two("bsr3", [P, HALVES, 6])
        hidden = [fold[:, free_at + i * HT * P:free_at + (i + 1) * HT * P].bitcast(F16).rearrange("p (k t) -> p k t", k=HT) for i in range(4)]
        hidh, hidl = hidden[0:2], hidden[2:4]
        hidf = H[:].rearrange("p a b -> p (a b)")[:, 0:HT * TOKENS].rearrange("p (k t) -> p k t", k=HT)
        z = h2

        lmax = sb("lmax", [P, HALVES, SEQS])
        lsum = sb("lsum", [P, HALVES, SEQS])
        lsub = sb("lsub", [P, HALVES, SEQS, EXPERTS])
        lexp = sb("lexp", [P, HALVES, SEQS, EXPERTS])
        PR = sb("PR", [P, HALVES, SEQS, EXPERTS])
        GROUP_SEQS = ((0, SEQS - 2), (SEQS - 2, SEQS))
        flat = lambda c: c[:].rearrange("p a b -> p (a b)")[0:(SEQS - 2) * EXPERTS, 0:TOKENS]
        tops, chosen = [flat(pos), flat(ln1w)], flat(ln1b)
        top8 = [sb(f"top8{i}", [(SEQS - 2) * EXPERTS, 8]) for i in range(2)]
        MS = sb("MS", [P, HALVES, SEQS, EXPERTS])
        GS = sb("GS", [P, HALVES, SEQS, EXPERTS])

        ld_idx, ld_pos, ld_const, ld_fold = sem("ld_idx"), sem("ld_pos"), sem("ld_const"), sem("ld_fold")
        ld_ln, ld_attn, ld_ffn, ld_w2 = sem("ld_ln"), sem("ld_attn"), sem("ld_ffn"), sem("ld_w2")
        ld_fold_a, ld_wqkv, ld_w1 = sem("ld_fold_a"), sem("ld_wqkv"), sem("ld_w1")
        weights_hi = sem("weights_hi")
        rows_first, rows_in = sem("rows_first"), sem("rows_in")
        slots_set, dve_consts = sem("slots_set"), sem("dve_consts")
        fold_mm, fold_set = sem("fold_mm"), sem("fold_set")
        pre_ffn = sem("pre_ffn")

        a_y, a_yT, a_yTs = sig("a_y"), sig("a_yT"), sig("a_yTs")
        a_q2, a_q2s, a_vp, a_vps = sig("a_q2"), sig("a_q2s"), sig("a_vp"), sig("a_vps")
        a_sc, a_max, a_exp, a_pT, a_pTs = sig("a_sc"), sig("a_max"), sig("a_exp", 2), sig("a_pT"), sig("a_pTs")
        a_ri, a_o, a_res, a_bn, a_ag, a_sq = sig("a_ri"), sig("a_o"), sig("a_res"), sig("a_bn"), sig("a_ag"), sig("a_sq")
        a_st, a_ss, a_nv, a_ve, a_rs, a_n, a_w, a_y1 = (sig(f"a_{x}") for x in ("st", "ss", "nv", "ve", "rs", "n", "w", "y1"))
        a_y1T, a_y1Ts, a_f, a_g, a_r2 = sig("a_y1T"), sig("a_y1Ts"), sig("a_f"), sig("a_g"), sig("a_r2")
        a_bn2, a_ag2, a_sq2, a_st2, a_ss2 = (sig(f"a_{x}") for x in ("bn2", "ag2", "sq2", "st2", "ss2"))
        a_nv2, a_ve2, a_rs2, a_n2, a_w2, a_h = (sig(f"a_{x}") for x in ("nv2", "ve2", "rs2", "n2", "w2", "h"))

        def head_signals(loop, chunks1, chunks2, own):
            names = {
                "bn": 1, "ag": 1, "ve": 1, "rs": 1, "x": 1, "xh": 1, "xc": 1, "xT": 1, "xTs": 1,
                "qq": 1, "hq": 1, "qk": 1, "v": 1, "hi": 1, "lo": 1, "vs": 1,
                "qkT": 1, "qTs": 1, "kTs": 1, "s1": chunks1, "max": chunks1,
                "rT": 1, "rTs": 1, "s2": chunks2, "exp": chunks2,
                "o": 1, "or": 1, "ot": 1, "rec": 1, "on": 1, "o2": 1, "o2s": 1,
            } | own
            return {name: sig(f"{loop}_{name}", per) for name, per in names.items()}

        CAUSAL1 = [(1, 0, 4, 256), (1, 4, 4, 256), (1, 8, 4, 256), (0, 0, 8, 128), (0, 8, 4, 128)]
        CAUSAL2 = [(0, 0, 4, 256), (0, 4, 4, 256), (0, 8, 4, 256), (1, 0, 8, 128), (1, 8, 4, 128)]
        FULL = [(k, h, 4, 256) for k in (0, 1) for h in (0, 4, 8)]
        B_ = head_signals("b", len(CAUSAL1), len(CAUSAL2), {
            "cut": 2, "pj": 1, "h2": 1, "bn3": 1, "ag3": 1, "ve3": 1, "rs3": 1, "x3": 1, "base": 1,
            "x3T": 1, "x3Ts": 1, "lg": 1, "lgs": 1})
        C_ = head_signals("c", len(FULL), len(FULL), {
            "gm": 1, "bt": 1, "xm": 1, "hm": 3, "hf": 3, "hl": 3, "z": 1, "zb": 1, "zg": 1, "za": 1})
        stored = [sig(f"stored{s}", 8) for s in range(2)]
        carriers = sem("carriers")
        t_sig = sem("t_sig")
        ROUNDS = CAP // 8
        CHOICE_BANK = (1, 3)
        ROUNDS_AT = (0, 5, 6, 8, 12)
        EXPERT_ROUNDS_AT = (0, 1, 2, 2, 4, 6, 10, 11, 14, ROUNDS)
        probs_made, rows_chosen, routed = 5, 6 + 2 * ROUNDS + 1, 6 + 2 * ROUNDS + 3 + EXPERTS - 1
        t_pe, t_act = sem("t_pe"), sem("t_act")

        def pipeline(eng, step, stages=3, late=None):
            def peeled(i):
                if late and i in late:
                    late[i]()
                step(*[(i - k, (i - k) % 2) if 0 <= i - k < SEQS else None for k in range(stages)])

            first = stages // 2 * 2
            for i in range(first):
                peeled(i)
            with eng.Fori(first // 2, SEQS // 2) as pair:
                for i in range(2):
                    step(*[(2 * pair + (i - k), (i - k) % 2) for k in range(stages)])
            for i in range(SEQS, SEQS + stages - 2):
                peeled(i)
            return lambda: peeled(SEQS + stages - 2)

        def first(stage):
            return isinstance(stage[0], int) and stage[0] == 0

        def stage_halves(eng, on, S, n, s, src):
            x, v = XS[s], XS[s][:].rearrange("p a (t c) -> p a t c", t=4)
            on.tensor_copy(x[:, :, 0:P], src[:, :, 0:P])
            on.tensor_copy(v[:, :, 1::2, 0:TAIL], src[:, :, P:DIM].unsqueeze(2).to_broadcast([P, HALVES, 2, TAIL])).then_inc(S["xh"].sem, 1)
            settle(eng)
            eng.wait_ge(S["xh"].sem, S["xh"].done(n))
            on.tensor_tensor(x[:, :, 2 * P:3 * P], src[:, :, 0:P], x[:, :, 0:P], ALU.subtract)
            on.tensor_tensor(x[:, :, P + TAIL:2 * P], src[:, :, P:DIM], x[:, :, P:P + TAIL], ALU.subtract).then_inc(S["xc"].sem, 1)

        def region(on, dst, src, W, n):
            for e, (lo, hi) in enumerate(REGIONS):
                w = (W[:, :, bass.ds(n, 1), e:e + 1] if not isinstance(n, int) else W[:, :, n:n + 1, e:e + 1])
                w = w.rearrange("p a b c -> p a (b c)").to_broadcast([P, HALVES, hi - lo])
                i = on.tensor_tensor(dst[:, :, lo:hi], src[:, :, lo:hi], w, ALU.mult)
            return i

        def stage_masked(eng, on, n, s):
            S = C_
            w = MS[:, :, bass.ds(n, 1), 0:1] if not isinstance(n, int) else MS[:, :, n:n + 1, 0:1]
            settle(eng)
            eng.wait_ge(S["xT"].sem, S["xT"].freed(n))
            on.tensor_copy(XS[s][:, :, 3 * P + TAIL:3 * P + TAIL + 2], w.rearrange("p a b c -> p a (b c)").to_broadcast([P, HALVES, 2]))
            region(on, xs[s], tiles(X, n), MS, n).then_inc(S["xm"].sem, 1)
            eng.wait_ge(S["xm"].sem, S["xm"].done(n))
            eng.sem_inc(carriers, 1)
            stage_halves(eng, on, S, n, s, xs[s])

        def settle(eng):
            eng.wait_ge(ld_const, 32)

        def tiles(T, n):
            return T[:, bass.ds(2 * n, 2), :] if not isinstance(n, int) else T[:, 2 * n:2 * n + 2, :]

        def pair_view(pair, slots, width, lo=0, hi=None):
            v = bank(pair, 2).rearrange("p (b c) -> p b c", b=2)[:, :, 0:slots * width]
            return v.rearrange("p b (i w) -> p b i w", w=width)

        with nc.Block() as start:
            def start_values(share):
                def program(eng):
                    for s in signals[share::5]:
                        eng.sem_inc(s.sem, AHEAD * s.per_seq)
                return program

            for share, on in enumerate((start.sync, start.gpsimd, start.scalar, start.vector, start.tensor)):
                on(start_values(share))

        block = ctx.enter_context(nc.Block())

        @block.sync
        def _(sp):
            sp.dma_start(idx[:], d["idx"]).then_inc(ld_idx, 16)
            sp.dma_start(ident[:], d["ident"]).then_inc(ld_const, 16)
            sp.dma_start(maskf[:], d["mask"]).then_inc(ld_const, 16)
            sp.dma_start(fold_l[:, 0:2], d["fold_l"][:, 0:2]).then_inc(ld_fold_a, 16)
            sp.dma_start(pos[:], d["pos"]).then_inc(ld_pos, 16)
            sp.dma_start(fold_l[:, 2:4], d["fold_l"][:, 2:4]).then_inc(ld_fold, 16)
            sp.dma_start(fold_r[:], d["fold_r"]).then_inc(ld_fold, 16)
            sp.dma_start(bias_r[:], d["bias_r"]).then_inc(ld_fold, 16)
            sp.dma_start(e_last[:], d["e_last"]).then_inc(ld_fold, 16)
            for t, name in ((ln1w, "ln1_w"), (ln1b, "ln1_b"), (ln2w, "ln2_w"), (ln2b, "ln2_b")):
                sp.dma_start(t[:], d[name].rearrange("(h p) c -> p h c", p=P)).then_inc(ld_ln, 16)
            sp.dma_start(wqkv_raw, d["wqkv"]).then_inc(ld_wqkv, 16)
            sp.dma_start(wproj[:], d["wproj"]).then_inc(ld_attn, 16)
            sp.dma_start(wrout[:], d["wrout"]).then_inc(ld_attn, 16)
            sp.dma_start(b2ab[:], d["b2"].partition_broadcast(P)).then_inc(ld_ffn, 16)
            sp.dma_start(gamma[:, 0, :], d["gamma"].partition_broadcast(P)).then_inc(ld_ffn, 16)
            sp.dma_start(beta[:, 0, :], d["beta"].partition_broadcast(P)).then_inc(ld_ffn, 16)
            sp.wait_ge(fold_mm, 3)
            sp.dma_start(w2ab[:], d["w2"]).then_inc(ld_w2, 16)
            sp.wait_ge(B_["o"].sem, B_["o"].done(SEQS - 2))
            sp.dma_start(w1_raw, d["w1"]).then_inc(ld_w1, 16)

            def store(n, s):
                sp.wait_ge(C_["za"].sem, C_["za"].done(n))
                dst = d["out"][bass.ds(n, 1)] if not isinstance(n, int) else d["out"][n:n + 1]
                sp.dma_start(dst.rearrange("a (h p) c -> p (a h) c", p=P), z[s][:]).then_inc(stored[s].sem, 16)

            with sp.Fori(0, SEQS // 2) as pair:
                store(2 * pair, 0)
                store(2 * pair + 1, 1)
            for s in range(2):
                sp.wait_ge(stored[s].sem, stored[s].done(SEQS - 2, 16))

        @block.gpsimd
        def _(pool):
            pool.wait_ge(ld_idx, 16)
            for t in range(SEQS * HALVES):
                pool.indirect_dma_start(X[:, t, :], None, d["emb"],
                                        bass.IndirectOffsetOnAxis(ap=idx[:, t:t + 1], axis=0)).then_inc(rows_first if t < 2 * HALVES else rows_in, 16)
            pool.wait_ge(dve_consts, 6)

            def power(out, var, s, have, freed, sig_out, n):
                pool.wait_ge(have.sem, have.done(n))
                pool.wait_ge(freed.sem, freed.freed(n))
                nc.gpsimd.tensor_tensor(out, var, half_neg[:, 0:var.shape[1]], ALU.pow).then_inc(sig_out.sem, 1)

            pool.wait_ge(ld_pos, 16)
            pool.wait_ge(rows_first, 16 * 2 * HALVES)

            def stage(n, s):
                S = B_
                settle(pool)
                pool.wait_ge(S["x"].sem, S["x"].done(n))
                pool.wait_ge(S["xT"].sem, S["xT"].freed(n))
                stage_halves(pool, nc.gpsimd, S, n, s, tiles(X, n))

            def tok_step(new, heads, norm1, mlp, norm2):
                if new:
                    n, s = new
                    if isinstance(n, int) and n == 2:
                        pool.wait_ge(rows_in, 16 * (SEQS - 2) * HALVES)
                    settle(pool)
                    pool.wait_ge(a_yT.sem, a_yT.freed(n))
                    pool.wait_ge(a_res.sem, a_res.freed(n))
                    nc.gpsimd.tensor_tensor(ys[s][:, :, 0:DIM], tiles(X, n), pos[:], ALU.add).then_inc(a_y.sem, 1)
                if norm1:
                    n, s = norm1
                    power(st[s][:, 3:4], st[s][:, 2:3], s, a_ve, a_n, a_rs, n)
                if norm2:
                    n, s = norm2
                    power(st2[s][:, 3:4], st2[s][:, 2:3], s, a_ve2, a_n2, a_rs2, n)
                if norm1:
                    n, s = norm1
                    pool.wait_ge(a_n.sem, a_n.done(n))
                    pool.wait_ge(ld_ln, 64)
                    nc.gpsimd.tensor_tensor(r1[s][:], r1[s][:], ln1w[:], ALU.mult).then_inc(a_w.sem, 1)
                if norm2:
                    n, s = norm2
                    pool.wait_ge(a_n2.sem, a_n2.done(n))
                    nc.gpsimd.tensor_tensor(r2[s][:], r2[s][:], ln2w[:], ALU.mult).then_inc(a_w2.sem, 1)
                    pool.wait_ge(a_w2.sem, a_w2.done(n))
                    nc.gpsimd.tensor_tensor(tiles(H, n), r2[s][:], ln2b[:], ALU.add).then_inc(a_h.sem, 1)
                    S = B_
                    power(rstd[s][:], rv[s][:, :, 1], s, S["ve"], S["x"], S["rs"], n)

            tok_end = pipeline(pool, tok_step, 5, late={SEQS: lambda: stage(0, 0), SEQS + 2: lambda: stage(1, 1)})

            zero = pool.to_reg(0.0)

            def causal_step(soon, new, mid, back, last):
                S = B_
                if last:
                    n, s = last
                    power(rstd4[s][:], rv4[s][:, :, 1], s, C_["ve"], C_["x"], C_["rs"], n)
                def cut(n, s, k):
                    col, last = ((0, 3), (TOKENS, 5))[k]
                    pool.wait_ge(S["exp"].sem, S["exp"].done(n, last))
                    pool.sem_inc(carriers, 1)
                    v = PT[s][:, :, col:col + P]
                    nc.gpsimd.affine_select(out=v, in_=v, compare_op=ALU.is_ge, fill=zero, base=0,
                                            pattern=[[0, HEADS], [1, P]], channel_multiplier=-1).then_inc(S["cut"].sem, 1)

                if mid:
                    cut(*mid, 0)
                if back:
                    n, s = back
                    power(rstd3[s][:], rv3[s][:, :, 1], s, S["ve3"], S["x3"], S["rs3"], n)
                if mid:
                    cut(*mid, 1)
                if soon and not (isinstance(soon[0], int) and soon[0] < 2):
                    stage(*soon)
                if back:
                    n, s = back
                    settle(pool)
                    pool.wait_ge(S["x3"].sem, S["x3"].done(n))
                    nc.gpsimd.tensor_tensor(tiles(BASE, n), h2[s][:], x3[s][:], ALU.add).then_inc(S["base"].sem, 1)
                if last:
                    n, s = last
                    xn = tiles(X, n)[:, :, 0:DIM]
                    settle(pool)
                    pool.wait_ge(C_["x"].sem, C_["x"].done(n))
                    nc.gpsimd.tensor_tensor(xn, xn, gamma[:].to_broadcast([P, HALVES, DIM]), ALU.mult).then_inc(C_["gm"].sem, 1)
                    settle(pool)
                    pool.wait_ge(C_["gm"].sem, C_["gm"].done(n))
                    nc.gpsimd.tensor_tensor(xn, xn, beta[:].to_broadcast([P, HALVES, DIM]), ALU.add).then_inc(C_["bt"].sem, 1)

            def second_weights():
                pool.wait_ge(ld_w2, 16)
                nc.gpsimd.tensor_tensor(w2ab[:, 0], w2ab[:, 0], w2ab[:, 1], ALU.add).then_inc(pre_ffn, 1)
                for h in range(HALVES):
                    nc.gpsimd.tensor_tensor(b2[:, h], b2ab[:, 0], b2ab[:, 1], ALU.add).then_inc(pre_ffn, 1)
                tok_end()

            def second_weights_low():
                pool.wait_ge(weights_hi, 5)
                nc.gpsimd.tensor_tensor(w2l[:], w2ab[:, 0, 0:HT], w2h[:], ALU.subtract).then_inc(pre_ffn, 1)

            pool.wait_ge(ld_ffn, 3 * 16)
            causal_end = pipeline(pool, causal_step, 5, late={1: second_weights, 2: second_weights_low})

            pool.wait_ge(weights_hi, 9)
            nc.gpsimd.tensor_tensor(w1[:, 2], w1_raw[:, 0], w1[:, 0], ALU.subtract).then_inc(pre_ffn, 1)
            nc.gpsimd.tensor_tensor(w1[0:TAIL + 2, 3], w1_raw[0:TAIL + 2, 2], w3_hi[0:TAIL + 2], ALU.subtract).then_inc(pre_ffn, 1)
            pool.wait_ge(t_sig, routed)
            pool.wait_ge(C_["xc"].sem, C_["xc"].done(0))
            causal_end()

            def ffn_step(soon, new, mid, back, last):
                S = C_
                if soon and (not isinstance(soon[0], int) or soon[0] >= 4):
                    pool.wait_ge(t_sig, 2 * routed)
                if soon and not (isinstance(soon[0], int) and soon[0] == 0):
                    stage_masked(pool, nc.gpsimd, *soon)
                if last:
                    n, s = last
                    settle(pool)
                    pool.wait_ge(S["zb"].sem, S["zb"].done(n))
                    region(nc.gpsimd, z[s], z[s], GS, n).then_inc(S["zg"].sem, 1)
                    pool.wait_ge(S["zg"].sem, S["zg"].done(n))
                    nc.gpsimd.tensor_tensor(z[s][:], z[s][:], tiles(BASE, n), ALU.add).then_inc(S["za"].sem, 1)
                if mid:
                    n, s = mid
                    for k in range(3):
                        ks = slice(2 * k, 2 * k + 2)
                        pool.wait_ge(S["hf"].sem, S["hf"].done(n, k + 1))
                        if k == 0:
                            pool.wait_ge(S["z"].sem, S["z"].freed(n))
                        nc.gpsimd.tensor_tensor(hidl[s][:, ks], hidf[:, ks], hidh[s][:, ks], ALU.subtract).then_inc(S["hl"].sem, 1)

            pipeline(pool, ffn_step, 5)()

        @block.scalar
        def _(act):
            def evac(dst, src, ready, freed, made, n, extra=()):
                act.wait_ge(ready.sem, ready.done(n))
                act.wait_ge(freed.sem, freed.freed(n))
                nc.scalar.copy(dst, src).then_inc(made.sem, 1)

            def folded(k, w, b, width):
                act.wait_ge(fold_mm, k + 1)
                nc.scalar.copy(w[:].rearrange("p a b -> p (a b)"), bank(b)[0:CH + 1, 0:2 * width]).then_inc(fold_set, 1)

            folded(0, Aw, 0, DIM + 1)
            folded(1, VO, 2, DIM)

            def high_halves():
                act.wait_ge(ld_wqkv, 16)
                for k in range(2):
                    nc.scalar.activation(wqkv[:, k], wqkv_raw[:, k], ACT.Copy, scale=WS).then_inc(weights_hi, 1)

            def tok_step(new, heads, norm1, mlp):
                if new:
                    n, s = new
                    evac(yT[s][:].rearrange("p a b -> p (a b)"), bank(4 * s)[0:CH + 1, :], a_yT, a_sc, a_yTs, n)
                if mlp:
                    n, s = mlp
                    act.wait_ge(a_f.sem, a_f.done(n))
                    act.wait_ge(a_r2.sem, a_r2.freed(n))
                    nc.scalar.activation(g1[s][:].rearrange("p a b -> p (a b)"), bank(4 * s + 3)[:, 0:2 * DIM], ACT.Gelu).then_inc(a_g.sem, 1)
                if new:
                    n, s = new
                    evac(q2[s][:].rearrange("p a b -> p (a b)"), bank(4 * s + 1)[0:CH + 1, :], a_q2, a_sc, a_q2s, n)
                if norm1:
                    n, s = norm1
                    evac(y1T[s][:].rearrange("p a b -> p (a b)"), bank(4 * s + 3)[0:CH + 1, :], a_y1T, a_f, a_y1Ts, n)
                if new:
                    n, s = new
                    act.wait_ge(a_max.sem, a_max.done(n))
                    act.wait_ge(a_pT.sem, a_pT.freed(n))
                    act.wait_ge(a_ri.sem, a_ri.freed(n))
                    for h in range(HALVES):
                        nc.scalar.activation(pr[s][:, h, :], bank(4 * s)[:, h * TOKENS:(h + 1) * TOKENS], ACT.Exp,
                                             bias=nm[s][:, h:h + 1], accum_out=rs[s][:, h:h + 1]).then_inc(a_exp.sem, 1)

            def soon_x(S, n, s, used):
                evac(xT[s][:].rearrange("p a b -> p (a b)"), bank(0).bitcast(F16), S["xT"], used, S["xTs"], n)

            pipeline(act, tok_step, 4, late={2: high_halves, 3: lambda: folded(2, W12, 7, DIM),
                                             SEQS + 2: lambda: soon_x(B_, 0, 0, B_["v"])})()
            act.wait_ge(slots_set, 8)

            def front_qk(S, n, s):
                act.wait_ge(S["qk"].sem, S["qk"].done(n))
                act.wait_ge(S["qkT"].sem, S["qkT"].freed(n))
                for h in range(HALVES):
                    dst = QS[s][:, h, HEADS:, :].rearrange("p h (a b e) -> p h a b e", a=2, e=HD)[:, :, :, 0, :]
                    src = bank(2)[:, h * DIM:(h + 1) * DIM].rearrange("p (h o e) -> p h o e", o=1, e=HD)
                    i = nc.scalar.activation(dst, src.to_broadcast([P, HEADS, 2, HD]), ACT.Copy, scale=1 / WS)
                i.then_inc(S["hi"].sem, 1)

            def front_v(S, n, s):
                act.wait_ge(S["v"].sem, S["v"].done(n))
                act.wait_ge(S["o"].sem, S["o"].freed(n))
                v = bank(3)[:, 0:2 * DIM].rearrange("p (b h e) -> p b h e", b=2, e=HD)
                nc.scalar.activation(VA[s][:, :, :, 0:HD], v, ACT.Copy, scale=1 / WS).then_inc(S["vs"].sem, 1)

            def front_keys(S, n, s):
                act.wait_ge(S["qkT"].sem, S["qkT"].done(n))
                act.wait_ge(S["s2"].sem, S["s2"].freed(n))
                nc.scalar.copy(QT[s][:, 8:, :].rearrange("p a b -> p (a b)"), bank(2).bitcast(F16)).then_inc(S["kTs"].sem, 1)

            def exps(S, chunks, n, s, ks):
                for k in ks:
                    kt, h0, nh, w = chunks[k]
                    act.wait_ge(S["s2"].sem, S["s2"].done(n, k + 1))
                    if k == 0:
                        act.wait_ge(S["o"].sem, S["o"].freed(n))
                    dst = PT[s][:, h0:h0 + nh, kt * TOKENS:kt * TOKENS + w].rearrange("p (i b) w -> p b i w", b=2)
                    nc.scalar.activation(dst, pair_view(6 - 2 * (k % 2), nh // 2, w), ACT.Exp, scale=SCALE).then_inc(S["exp"].sem, 1)

            def raw_heads(S, n, s):
                act.wait_ge(S["o"].sem, S["o"].done(n))
                act.wait_ge(S["ot"].sem, S["ot"].freed(n))
                nc.scalar.copy(OR[s][:].rearrange("p a b -> p (a b)"), bank(4, 2)[:, 0:GROUPS * TOKENS]).then_inc(S["or"].sem, 1)

            def heads_T(S, n, s, used):
                evac(OT[s][:].rearrange("p a b -> p (a b)"), bank(6)[0:CH, :], S["o2"], used, S["o2s"], n)

            def causal_step(soon, new, mid, back):
                S = B_
                if mid:
                    exps(S, CAUSAL2, *mid, (0, 1))
                if new:
                    front_qk(S, *new)
                if mid and isinstance(mid[0], int) and mid[0] == SEQS - 1:
                    choice_exp(0)
                if mid:
                    exps(S, CAUSAL2, *mid, (2,))
                if new:
                    front_v(S, *new)
                if mid:
                    exps(S, CAUSAL2, *mid, (3,))
                if new:
                    front_keys(S, *new)
                if mid:
                    exps(S, CAUSAL2, *mid, (4,))
                if mid:
                    raw_heads(S, *mid)
                if back:
                    n, s = back
                    evac(x3T[s][:].rearrange("p a b -> p (a b)"), bank(6)[0:CH, :], S["x3T"], S["lg"], S["x3Ts"], n)
                if soon and not first(soon):
                    soon_x(S, *soon, S["v"])
                if mid:
                    heads_T(S, *mid, S["pj"])

            def choice_exp(g):
                a, b = GROUP_SEQS[g]
                act.wait_ge(t_sig, g * routed + 2)
                nc.scalar.activation(lexp[:, :, a:b], lsub[:, :, a:b], ACT.Exp).then_inc(t_act, 1)

            def first_layer():
                act.wait_ge(ld_w1, 16)
                for dst, k in ((w1[:, 0], 0), (w1[:, 1], 1), (w3_hi[:], 2)):
                    nc.scalar.activation(dst, w1_raw[:, k], ACT.Copy, scale=WS).then_inc(weights_hi, 1)
                act.wait_ge(weights_hi, 8)
                nc.scalar.activation(w1_raw, w1_raw, ACT.Copy, scale=WS).then_inc(weights_hi, 1)

            def second_layer():
                act.wait_ge(pre_ffn, 1)
                nc.scalar.activation(w2ab[:, 0], w2ab[:, 0], ACT.Copy, scale=WS).then_inc(weights_hi, 1)
                act.wait_ge(weights_hi, 3)
                nc.scalar.copy(w2h[:], w2ab[:, 0, 0:HT]).then_inc(weights_hi, 1)
                nc.scalar.copy(w2o[:], w2ab[0:CH, 0, HT:]).then_inc(weights_hi, 1)

            pipeline(act, causal_step, 4, late={2: second_layer, SEQS + 2: first_layer})()

            act.wait_ge(pre_ffn, 6)
            nc.scalar.copy(w1[TAIL:TAIL + 1, 3], w3_hi[TAIL:TAIL + 1]).then_inc(weights_hi, 1)
            choice_exp(1)

            def ffn_step(soon, new, mid):
                S = C_
                if mid:
                    exps(S, FULL, *mid, (0,))
                if new:
                    front_qk(S, *new)
                if mid:
                    exps(S, FULL, *mid, (1,))
                if new:
                    front_v(S, *new)
                if mid:
                    exps(S, FULL, *mid, (2,))
                if new:
                    front_keys(S, *new)
                if mid:
                    exps(S, FULL, *mid, (3, 4, 5))
                if mid:
                    n, s = mid
                    for k in range(3):
                        act.wait_ge(S["hm"].sem, S["hm"].done(n, k + 1))
                        if k == 0:
                            act.wait_ge(S["z"].sem, S["z"].freed(n))
                            act.wait_ge(pre_ffn, 4)
                            act.wait_ge(S["hl"].sem, S["hl"].done(n - 1))
                        src = bank((3, 6, 7)[k]).rearrange("p (a b) -> p a b", a=2)
                        nc.scalar.activation(hidh[s][:, 2 * k:2 * k + 2], src, ACT.Gelu, scale=1 / WS)
                        nc.scalar.activation(hidf[:, 2 * k:2 * k + 2], src, ACT.Gelu, scale=1 / WS).then_inc(S["hf"].sem, 1)
                    nc.scalar.activation(half_neg[:, 2:3], half_neg[:, 0:1], ACT.Exp)
                    raw_heads(S, n, s)
                if soon:
                    soon_x(S, *soon, S["hm"])
                if mid:
                    heads_T(S, *mid, S["z"])

            pipeline(act, ffn_step)()

        @block.vector
        def _(dve):
            nc.vector.memset(half_neg[:, 0:2], -0.5).then_inc(dve_consts, 1)
            nc.vector.memset(mean_of[:], 1.0 / P).then_inc(dve_consts, 1)
            for s in range(2):
                nc.vector.memset(ys[s][:, :, DIM:DIM + 1], 1.0).then_inc(dve_consts, 1)
                nc.vector.memset(y1[s][:, :, DIM:DIM + 1], 1.0).then_inc(dve_consts, 1)
            for s in range(2):
                nc.vector.memset(QS[s][:], 0.0).then_inc(slots_set, 1)
                nc.vector.memset(VA[s][:], 1.0).then_inc(slots_set, 1)
                nc.vector.memset(XS[s][:], 0.0).then_inc(slots_set, 1)
            dve.wait_ge(slots_set, 6)
            for s in range(2):
                nc.vector.memset(QS[s][:, :, HEADS:, 3 * HD:3 * HD + 1], 1.0).then_inc(slots_set, 1)
            dve.wait_ge(ld_const, 32)
            nc.vector.tensor_copy(ident16[:], ident[:]).then_inc(dve_consts, 1)
            nc.vector.tensor_copy(identb[:], ident[:]).then_inc(dve_consts, 1)
            for i in range(4):
                nc.vector.tensor_copy(maskb[:, i], maskf[:]).then_inc(dve_consts, 1)
            dve.wait_ge(slots_set, 8)

            def low_halves():
                dve.wait_ge(weights_hi, 2)
                for k, n_rows in ((0, P), (1, TAIL)):
                    nc.vector.scalar_tensor_tensor(wqkv[0:n_rows, 2 + k], wqkv_raw[0:n_rows, k], WS, wqkv[0:n_rows, k], ALU.mult, ALU.subtract).then_inc(dve_consts, 1)

            def whole_norm_stats(x, BS, MV, ready, bn, ag, sq, n):
                dve.wait_ge(ready.sem, ready.done(n))
                dve.wait_ge(sq.sem, sq.freed(n))
                nc.vector.bn_stats(BS[:, 0, :], x.rearrange("p a b -> p (a b)")).then_inc(bn.sem, 1)
                settle(dve)
                dve.wait_ge(bn.sem, bn.done(n))
                nc.vector.bn_aggr(MV[:], BS[:, 0:1, :]).then_inc(ag.sem, 1)
                dve.wait_ge(ag.sem, ag.done(n))
                nc.vector.scalar_tensor_tensor(MV[:, 1:2], MV[:, 0:1], MV[:, 0:1], MV[:, 1:2], ALU.mult, ALU.add).then_inc(sq.sem, 1)

            def whole_norm_var(ST, src, mm, ss, nv, ve, n):
                dve.wait_ge(mm.sem, mm.done(n))
                nc.vector.tensor_copy(ST[:, 0:2], src).then_inc(ss.sem, 1)
                dve.wait_ge(ss.sem, ss.done(n))
                nc.vector.scalar_tensor_tensor(ST[:, 2:3], ST[:, 0:1], ST[:, 0:1], ST[:, 1:2], ALU.mult, ALU.subtract).then_inc(nv.sem, 1)
                dve.wait_ge(nv.sem, nv.done(n))
                nc.vector.tensor_scalar(ST[:, 2:3], ST[:, 2:3], -1.0, EPS_TOK, ALU.mult, ALU.add).then_inc(ve.sem, 1)

            def whole_norm(x, ST, rs_, out_sig, n):
                dve.wait_ge(rs_.sem, rs_.done(n))
                nc.vector.tensor_scalar(x, x, ST[:, 0:1], ST[:, 3:4], ALU.subtract, ALU.mult).then_inc(out_sig.sem, 1)

            def row_stats(src, BS, RV, eps, bn, ag, ve, rs_, n):
                dve.wait_ge(ag.sem, ag.freed(n))
                for h in range(HALVES):
                    i = nc.vector.bn_stats(BS[:, h, :], src(h))
                i.then_inc(bn.sem, 1)
                settle(dve)
                dve.wait_ge(bn.sem, bn.done(n))
                dve.wait_ge(rs_.sem, rs_.freed(n))
                for h in range(HALVES):
                    i = nc.vector.bn_aggr(RV[:, h, :], BS[:, h:h + 1, :])
                i.then_inc(ag.sem, 1)
                dve.wait_ge(ag.sem, ag.done(n))
                nc.vector.tensor_scalar(RV[:, :, 1], RV[:, :, 1], eps, None, ALU.add).then_inc(ve.sem, 1)

            def row_apply(src, dst, RV, RSTD, rs_, out_sig, freed, n):
                dve.wait_ge(rs_.sem, rs_.done(n))
                for f in freed:
                    dve.wait_ge(f.sem, f.freed(n))
                for h in range(HALVES):
                    i = nc.vector.tensor_scalar(dst(h), src(h), RV[:, h, 0:1], RSTD[:, h:h + 1], ALU.subtract, ALU.mult)
                i.then_inc(out_sig.sem, 1)

            def tile_of(T, n):
                def tile(h):
                    if isinstance(n, int):
                        return T[:, 2 * n + h, 0:DIM]
                    return T[:, bass.ds(2 * n + h, 1), 0:DIM].rearrange("p a b -> p (a b)")
                return tile

            def tok_step(new, heads, norm1, mlp, norm2):
                S = B_
                if norm1:
                    n, s = norm1
                    whole_norm_var(st[s], bank(4 * s + 2)[:, 0:2], a_st, a_ss, a_nv, a_ve, n)
                if norm2:
                    n, s = norm2
                    whole_norm_var(st2[s], bank(4 * s + 3)[:, 0:2], a_st2, a_ss2, a_nv2, a_ve2, n)
                if norm1:
                    n, s = norm1
                    whole_norm(r1[s][:], st[s], a_rs, a_n, n)
                if norm2:
                    n, s = norm2
                    whole_norm(r2[s][:], st2[s], a_rs2, a_n2, n)
                if mlp:
                    n, s = mlp
                    dve.wait_ge(a_g.sem, a_g.done(n))
                    dve.wait_ge(a_h.sem, a_h.freed(n))
                    nc.vector.tensor_tensor(r2[s][:], y1[s][:, :, 0:DIM], g1[s][:], ALU.add).then_inc(a_r2.sem, 1)
                if heads:
                    n, s = heads
                    dve.wait_ge(a_pT.sem, a_pT.done(n))
                    dve.wait_ge(a_o.sem, a_o.freed(n))
                    nc.vector.tensor_copy(pT[s][:].rearrange("p a b -> p (a b)"), bank(4 * s + 1)).then_inc(a_pTs.sem, 1)
                    dve.wait_ge(a_exp.sem, a_exp.done(n))
                    nc.vector.reciprocal(ri[s][:], rs[s][:]).then_inc(a_ri.sem, 1)
                if mlp:
                    n, s = mlp
                    whole_norm_stats(r2[s][:], bs2[s], mv2[s], a_r2, a_bn2, a_ag2, a_sq2, n)
                if norm1:
                    n, s = norm1
                    dve.wait_ge(a_w.sem, a_w.done(n))
                    dve.wait_ge(a_r2.sem, a_r2.freed(n))
                    dve.wait_ge(a_y1T.sem, a_y1T.freed(n))
                    nc.vector.tensor_tensor(y1[s][:, :, 0:DIM], r1[s][:], ln1b[:], ALU.add).then_inc(a_y1.sem, 1)
                if new:
                    n, s = new
                    dve.wait_ge(a_vp.sem, a_vp.done(n))
                    dve.wait_ge(a_o.sem, a_o.freed(n))
                    nc.vector.tensor_copy(vp[s][:].rearrange("p a b -> p (a b)"), bank(4 * s + 2)[:, 0:2 * DIM]).then_inc(a_vps.sem, 1)
                if norm2:
                    n, s = norm2
                    dve.wait_ge(a_h.sem, a_h.done(n))
                    row_stats(tile_of(H, n), bsr[s], rv[s], EPS_ROW, S["bn"], S["ag"], S["ve"], S["rs"], n)
                if heads:
                    n, s = heads
                    dve.wait_ge(a_ri.sem, a_ri.done(n))
                    dve.wait_ge(a_o.sem, a_o.done(n))
                    dve.wait_ge(a_y1.sem, a_y1.freed(n))
                    for h in range(HALVES):
                        i = nc.vector.scalar_tensor_tensor(r1[s][:, h], bank(4 * s + 2)[:, h * DIM:(h + 1) * DIM], ri[s][:, h:h + 1],
                                                           ys[s][:, h, 0:DIM], ALU.mult, ALU.add)
                    i.then_inc(a_res.sem, 1)
                    whole_norm_stats(r1[s][:], bs[s], mv[s], a_res, a_bn, a_ag, a_sq, n)
                if norm2:
                    n, s = norm2
                    row_apply(tile_of(H, n), tile_of(X, n), rv[s], rstd[s], S["rs"], S["x"], [], n)
                if new:
                    n, s = new
                    dve.wait_ge(a_sc.sem, a_sc.done(n))
                    dve.wait_ge(a_exp.sem, a_exp.freed(n))
                    nc.vector.tensor_reduce(nm[s][:], bank(4 * s).rearrange("p (h t) -> p h t", h=HALVES), AX.X, ALU.max,
                                            negate=True).then_inc(a_max.sem, 1)

            tok_end = pipeline(dve, tok_step, 5, late={3: low_halves})

            def low_half(src, s, h, first, slot):
                v = src[:, h * DIM:(h + 1) * DIM].rearrange("p (h e) -> p h e", e=HD)
                q = QS[s][:, h, first:first + HEADS, :]
                return nc.vector.scalar_tensor_tensor(q[:, :, slot * HD:(slot + 1) * HD], v, 1 / WS, q[:, :, 0:HD], ALU.mult, ALU.subtract)

            def split_queries(S, n, s):
                dve.wait_ge(S["qq"].sem, S["qq"].done(n))
                dve.wait_ge(S["rT"].sem, S["rT"].freed(n))
                for h in range(HALVES):
                    dst = QS[s][:, h, 0:HEADS, 0:2 * HD].rearrange("p h (a e) -> p h a e", e=HD)
                    src = bank(1)[:, h * DIM:(h + 1) * DIM].rearrange("p (h o e) -> p h o e", o=1, e=HD)
                    i = nc.vector.tensor_scalar(dst, src.to_broadcast([P, HEADS, 2, HD]), 1 / WS, None, ALU.mult)
                i.then_inc(S["hq"].sem, 1)
                dve.wait_ge(S["hq"].sem, S["hq"].done(n))
                for h in range(HALVES):
                    low_half(bank(1), s, h, 0, 2)

            def split_keys(S, n, s):
                dve.wait_ge(S["hi"].sem, S["hi"].done(n))
                for h in range(HALVES):
                    i = low_half(bank(2), s, h, HEADS, 1)
                i.then_inc(S["lo"].sem, 1)

            def queries(S, n, s):
                dve.wait_ge(S["qkT"].sem, S["qkT"].done(n))
                dve.wait_ge(S["s2"].sem, S["s2"].freed(n))
                nc.vector.tensor_copy(QT[s][:, 0:8, :].rearrange("p a b -> p (a b)"),
                                      bank(0, 2).bitcast(F16)).then_inc(S["qTs"].sem, 1)

            def maxima(S, chunks, n, s, ks):
                for k in ks:
                    h, h0, nh, w = chunks[k]
                    dve.wait_ge(S["s1"].sem, S["s1"].done(n, k + 1))
                    dst = QS[s][:, h, h0:h0 + nh, 3 * HD].rearrange("p (i b) -> p b i", b=2)
                    nc.vector.tensor_reduce(dst, pair_view(2 * (k % 2), nh // 2, w), AX.X, ALU.max, negate=True).then_inc(S["max"].sem, 1)

            def requeries(S, n, s):
                dve.wait_ge(S["rT"].sem, S["rT"].done(n))
                nc.vector.tensor_copy(QT[s][:, 0:HEADS // 2, :].rearrange("p a b -> p (a b)"),
                                      bank(1, 2).bitcast(F16)[:, 0:HEADS // 2 * TOKENS]).then_inc(S["rTs"].sem, 1)

            def normalise(S, n, s):
                dve.wait_ge(S["ot"].sem, S["ot"].done(n))
                o = bank(4, 2).rearrange("p (a b) -> p a b", a=HALVES)[:, :, 0:HEADS * 2 * HD].rearrange("p a (h e) -> p a h e", e=2 * HD)
                nc.vector.reciprocal(rsum[s][:], o[:, :, :, HD]).then_inc(S["rec"].sem, 1)
                dve.wait_ge(S["rec"].sem, S["rec"].done(n))
                dve.wait_ge(S["o2"].sem, S["o2"].freed(n))
                nc.vector.tensor_tensor(ON[s][:].rearrange("p a (h e) -> p a h e", e=HD), o[:, :, :, 0:HD],
                                        rsum[s][:].unsqueeze(3).to_broadcast([P, HALVES, HEADS, HD]), ALU.mult).then_inc(S["on"].sem, 1)

            count = [0]

            def link(i):
                count[0] += 1
                i.then_inc(t_sig, 1)
                dve.wait_ge(t_sig, count[0])

            def choice_probs(g):
                a, b = GROUP_SEQS[g]
                G = slice(a, b)
                wide = [P, HALVES, b - a, EXPERTS]
                dve.wait_ge(B_["lgs"].sem, B_["lgs"].done(b - 1))
                link(nc.vector.tensor_reduce(lmax[:, :, G], LG[:, :, G], AX.X, ALU.max))
                link(nc.vector.tensor_tensor(lsub[:, :, G], LG[:, :, G], lmax[:, :, G].unsqueeze(3).to_broadcast(wide), ALU.subtract))
                dve.wait_ge(t_act, g + 1)
                link(nc.vector.tensor_reduce(lsum[:, :, G], lexp[:, :, G], AX.X, ALU.add))
                link(nc.vector.reciprocal(lsum[:, :, G], lsum[:, :, G]))
                link(nc.vector.tensor_tensor(PR[:, :, G], lexp[:, :, G], lsum[:, :, G].unsqueeze(3).to_broadcast(wide), ALU.mult))

            def choice_rounds(g, rounds):
                a, b = GROUP_SEQS[g]
                n_rows = (b - a) * EXPERTS
                tp = [x[0:n_rows] for x in tops]
                for k in rounds:
                    if k == 0:
                        dve.wait_ge(t_pe, 2 * g + 1)
                        link(nc.vector.tensor_copy(tp[0], bank(0)[0:n_rows, 0:TOKENS]))
                    link(nc.vector.max(top8[k % 2][0:n_rows], tp[k % 2]))
                    link(nc.vector.match_replace(tp[1 - k % 2], top8[k % 2][0:n_rows], tp[k % 2], -1.0))
                    if k == ROUNDS - 1:
                        link(nc.vector.tensor_scalar(chosen[0:n_rows], tp[ROUNDS % 2], -1.0, None, ALU.is_equal))

            def choice_back(g):
                a, b = GROUP_SEQS[g]
                G = slice(a, b)
                dve.wait_ge(t_pe, 2 * g + 2)
                src = bank(CHOICE_BANK[g])[:, 0:HALVES * (b - a) * EXPERTS].rearrange("p (a b c) -> p a b c", a=HALVES, c=EXPERTS)
                link(nc.vector.tensor_copy(MS[:, :, G], src))
                link(nc.vector.tensor_tensor(GS[:, :, G], MS[:, :, G], PR[:, :, G], ALU.mult))
                for e in range(EXPERTS - 2, -1, -1):
                    nc.vector.tensor_tensor(MS[:, :, G, e], MS[:, :, G, e], MS[:, :, G, e + 1], ALU.add)
                    link(nc.vector.tensor_tensor(GS[:, :, G, e], GS[:, :, G, e], GS[:, :, G, e + 1], ALU.add))

            def causal_step(new, mid, back, last):
                S = B_

                def first_choice(stage, n, k):
                    if stage and isinstance(stage[0], int) and stage[0] == n:
                        choice_rounds(0, range(ROUNDS_AT[k], ROUNDS_AT[k + 1]))

                if last:
                    n, s = last
                    dve.wait_ge(S["x3"].sem, S["x3"].done(n))
                    row_stats(lambda h: x3[s][:, h], bsr4[s], rv4[s], EPS_FFN, C_["bn"], C_["ag"], C_["ve"], C_["rs"], n)
                first_choice(back, SEQS - 1, 2)
                if back:
                    n, s = back
                    dve.wait_ge(S["pj"].sem, S["pj"].done(n))
                    dve.wait_ge(S["base"].sem, S["base"].freed(n))
                    nc.vector.tensor_tensor(h2[s][:], bank(3)[:, 0:2 * DIM].rearrange("p (a b) -> p a b", a=2), tiles(H, n), ALU.add).then_inc(S["h2"].sem, 1)
                if new:
                    split_queries(S, *new)
                if new:
                    split_keys(S, *new)
                if back:
                    n, s = back
                    dve.wait_ge(S["h2"].sem, S["h2"].done(n))
                    row_stats(lambda h: h2[s][:, h], bsr3[s], rv3[s], EPS_ROW, S["bn3"], S["ag3"], S["ve3"], S["rs3"], n)
                if last:
                    n, s = last
                    row_apply(lambda h: x3[s][:, h], tile_of(X, n), rv4[s], rstd4[s], C_["rs"], C_["x"], [], n)
                if mid and isinstance(mid[0], int) and mid[0] == SEQS - 1:
                    choice_probs(0)
                if new:
                    queries(S, *new)
                if back:
                    n, s = back
                    row_apply(lambda h: h2[s][:, h], lambda h: x3[s][:, h], rv3[s], rstd3[s], S["rs3"], S["x3"], [S["x3T"], C_["x"]], n)
                if new:
                    maxima(S, CAUSAL1, *new, range(len(CAUSAL1)))
                first_choice(mid, SEQS - 1, 0)
                if mid:
                    normalise(S, *mid)
                first_choice(mid, SEQS - 1, 1)
                if new:
                    requeries(S, *new)
                first_choice(back, SEQS - 1, 3)
                if back:
                    n, s = back
                    dve.wait_ge(S["lg"].sem, S["lg"].done(n))
                    dst = LG[:, :, bass.ds(n, 1), :] if not isinstance(n, int) else LG[:, :, n:n + 1, :]
                    nc.vector.tensor_copy(dst, bank(7)[:, 0:2 * EXPERTS].rearrange("p (a o b) -> p a o b", a=2, o=1)).then_inc(S["lgs"].sem, 1)

            causal_end = pipeline(dve, causal_step, 4, late={1: tok_end})

            choice_rounds(0, range(ROUNDS_AT[4], ROUNDS))
            choice_back(0)
            dve.wait_ge(C_["bt"].sem, C_["bt"].done(0))
            dve.wait_ge(B_["xT"].sem, B_["xT"].done(SEQS - 1))
            stage_masked(dve, nc.vector, 0, 0)
            choice_probs(1)
            causal_end()

            def ffn_step(new, mid, back):
                S = C_

                def second_choice(k):
                    if new and isinstance(new[0], int) and new[0] < 3:
                        at = 3 * new[0] + k
                        choice_rounds(1, range(EXPERT_ROUNDS_AT[at], EXPERT_ROUNDS_AT[at + 1]))

                second_choice(0)
                if new:
                    n, s = new
                    split_queries(S, n, s)
                    split_keys(S, n, s)
                    second_choice(1)
                    queries(S, n, s)
                    maxima(S, FULL, n, s, (0,))
                    second_choice(2)
                    maxima(S, FULL, n, s, range(1, len(FULL)))
                if mid:
                    normalise(S, *mid)
                if new:
                    requeries(S, *new)
                if back and isinstance(back[0], int) and back[0] == 0:
                    choice_back(1)
                if back:
                    n, s = back
                    dve.wait_ge(S["z"].sem, S["z"].done(n))
                    dve.wait_ge(stored[s].sem, stored[s].freed(n - s, 16))
                    nc.vector.scalar_tensor_tensor(z[s][:], bank(7)[:, 0:2 * DIM].rearrange("p (a b) -> p a b", a=2), 1 / WS, b2[:], ALU.mult, ALU.add).then_inc(S["zb"].sem, 1)

            dve.wait_ge(pre_ffn, 3)
            pipeline(dve, lambda new, mid, back, _: ffn_step(new, mid, back), 4)

        @block.tensor
        def _(pe):
            def mm(out, l, r, start=True, stop=True, free=False):
                return nc.tensor.matmul(out, l, r, start=start, stop=stop, skip_group_check=free)

            def rows(c):
                return CH + c

            def fold_weights(b, left, right, width, chunks=(0, 1)):
                for c in chunks:
                    lo = c * CH
                    out = bank(b)[0:CH + 1, c * width:(c + 1) * width]
                    for k in range(HT):
                        factor = fold_l[:, 1, k, :] if right is None else fold_r[:, right, k, :]
                        i = mm(out, fold_l[:, left, k, lo:lo + CH + 1], factor, start=(k == 0), stop=(k == HT - 1 and right is None))
                    if right is not None:
                        i = mm(out, e_last[0:1, lo:lo + CH + 1], bias_r[0:1, right, :], start=False, stop=True)
                if chunks[-1] == 1:
                    i.then_inc(fold_mm, 1)

            pe.wait_ge(ld_fold_a, 16)
            fold_weights(0, 0, None, DIM + 1)
            pe.wait_ge(ld_fold, 64)
            fold_weights(2, 2, 0, DIM)
            pe.wait_ge(fold_set, 2)
            pe.wait_ge(ld_const, 32)
            pe.wait_ge(dve_consts, 12)
            pe.wait_ge(slots_set, 8)

            def transposes(dst, src, width, ready, n, made):
                pe.wait_ge(ready.sem, ready.done(n))
                for c in range(2):
                    for h in range(HALVES):
                        i = nc.tensor.transpose(dst[0:width, c * TOKENS + h * P:c * TOKENS + (h + 1) * P],
                                                src[:, h, c * CH:c * CH + width], ident[:])
                i.then_inc(made.sem, 1)

            def tok_front1(n, s):
                pe.wait_ge(a_exp.sem, a_exp.freed(n))
                transposes(bank(4 * s), ys[s], CH + 1, a_y, n, a_yT)

            def tok_queries(n, s):
                pe.wait_ge(a_yTs.sem, a_yTs.done(n))
                for m in range(2):
                    for c in range(2):
                        i = mm(bank(4 * s + 1)[0:CH + 1, m * TOKENS:(m + 1) * TOKENS], Aw[0:rows(c), c, m * CH:m * CH + CH + 1],
                               yT[s][0:rows(c), c, :], start=(c == 0), stop=(c == 1))
                i.then_inc(a_q2.sem, 1)

            def tok_values(n, s):
                pe.wait_ge(a_ss.sem, a_ss.freed(n))
                for h in range(HALVES):
                    for c in range(2):
                        i = mm(bank(4 * s + 2)[:, h * DIM:(h + 1) * DIM], yT[s][0:rows(c), c, h * P:(h + 1) * P], VO[0:rows(c), c, :],
                               start=(c == 0), stop=(c == 1))
                i.then_inc(a_vp.sem, 1)

            def tok_scores(n, s):
                pe.wait_ge(a_q2s.sem, a_q2s.done(n))
                for h in range(HALVES):
                    for c in range(2):
                        i = mm(bank(4 * s)[:, h * TOKENS:(h + 1) * TOKENS], q2[s][0:rows(c), c, h * P:(h + 1) * P], yT[s][0:rows(c), c, :],
                               start=(c == 0), stop=(c == 1))
                i.then_inc(a_sc.sem, 1)

            def tok_pT(n, s):
                pe.wait_ge(a_exp.sem, a_exp.done(n))
                for k in range(HALVES):
                    for h in range(HALVES):
                        i = nc.tensor.transpose(bank(4 * s + 1)[:, k * TOKENS + h * P:k * TOKENS + (h + 1) * P],
                                                pr[s][:, h, k * P:(k + 1) * P], ident[:])
                i.then_inc(a_pT.sem, 1)

            def tok_out(n, s):
                pe.wait_ge(a_pTs.sem, a_pTs.done(n))
                pe.wait_ge(a_vps.sem, a_vps.done(n))
                for h in range(HALVES):
                    for k in range(HALVES):
                        i = mm(bank(4 * s + 2)[:, h * DIM:(h + 1) * DIM], pT[s][:, k, h * P:(h + 1) * P], vp[s][:, k, :],
                               start=(k == 0), stop=(k == 1))
                i.then_inc(a_o.sem, 1)

            def tok_step(new, heads, norm1, mlp):
                if new:
                    tok_front1(*new)
                if mlp:
                    n, s = mlp
                    pe.wait_ge(a_y1Ts.sem, a_y1Ts.done(n))
                    for h in range(HALVES):
                        for c in range(2):
                            i = mm(bank(4 * s + 3)[:, h * DIM:(h + 1) * DIM], y1T[s][0:rows(c), c, h * P:(h + 1) * P], W12[0:rows(c), c, :],
                                   start=(c == 0), stop=(c == 1))
                    i.then_inc(a_f.sem, 1)
                if new:
                    tok_queries(*new)
                if heads:
                    tok_pT(*heads)
                if new:
                    tok_values(*new)
                if heads:
                    tok_out(*heads)
                if norm1:
                    n, s = norm1
                    pe.wait_ge(a_ss2.sem, a_ss2.freed(n))
                    transposes(bank(4 * s + 3), y1[s], CH + 1, a_y1, n, a_y1T)
                if new:
                    tok_scores(*new)
                if mlp:
                    n, s = mlp
                    pe.wait_ge(a_sq2.sem, a_sq2.done(n))
                    mm(bank(4 * s + 3)[:, 0:2], mean_of[:], mv2[s][:]).then_inc(a_st2.sem, 1)
                if heads:
                    n, s = heads
                    pe.wait_ge(a_sq.sem, a_sq.done(n))
                    mm(bank(4 * s + 2)[:, 0:2], mean_of[:], mv[s][:]).then_inc(a_st.sem, 1)

            def x_transposes(S, n, s, last_even):
                pe.wait_ge(S["max"].sem, S["max"].done(n - 1, last_even + 1))
                pe.wait_ge(S["xc"].sem, S["xc"].done(n))
                for k in range(4):
                    for h in range(HALVES):
                        i = nc.tensor.transpose(bank(0).bitcast(F16)[:, k * TOKENS + h * P:k * TOKENS + (h + 1) * P],
                                                XS[s][:, h, k * P:(k + 1) * P], ident16[:])
                i.then_inc(S["xT"].sem, 1)

            def front_product(S, n, s, W, col, passes, m):
                if m == 0:
                    pe.wait_ge(S["xTs"].sem, S["xTs"].done(n))
                    pe.wait_ge(S["rTs"].sem, S["rTs"].done(n - 1))
                for h in range(HALVES):
                    for i_, (kx, kw, K) in enumerate(passes):
                        i = mm(bank(1 + m)[:, h * DIM:(h + 1) * DIM], xT[s][0:K, kx, h * P:(h + 1) * P],
                               W[0:K, kw, col + m * DIM:col + (m + 1) * DIM], start=(i_ == 0), stop=(i_ == len(passes) - 1))
                i.then_inc(S[("qq", "qk", "v")[m]].sem, 1)

            W_B = (wqkv, 0, PASSES)

            def first_products():
                pe.wait_ge(ld_attn, 32)
                pe.wait_ge(dve_consts, 14)
                pe.wait_ge(a_ss.sem, a_ss.done(SEQS - 2))
                for m in range(2):
                    front_product(B_, 0, 0, *W_B, m)

            pipeline(pe, tok_step, 4, late={1: lambda: fold_weights(7, 3, 1, DIM, (0,)), 2: lambda: fold_weights(7, 3, 1, DIM, (1,)),
                                            3: lambda: pe.wait_ge(fold_set, 3),
                                            SEQS + 1: lambda: x_transposes(B_, 0, 0, 4), SEQS + 2: first_products})()
            pe.wait_ge(a_ss2.sem, a_ss2.done(SEQS - 2))

            def slots_T(dst, s, blocks):
                for j, b in enumerate(blocks):
                    for h in range(HALVES):
                        i = nc.tensor.transpose(dst[:, j * TOKENS + h * P:j * TOKENS + (h + 1) * P],
                                                QS[s][:, h, 2 * b:2 * b + 2, :].rearrange("p a b -> p (a b)"), ident16[:])
                return i

            def front_T(S, n, s):
                pe.wait_ge(S["hi"].sem, S["hi"].done(n))
                pe.wait_ge(S["lo"].sem, S["lo"].done(n))
                slots_T(bank(0, 3).bitcast(F16), s, range(HEADS)).then_inc(S["qkT"].sem, 1)

            def head_rows(t, h):
                return t[SLOT * (h % 2):SLOT * (h % 2) + SLOT]

            def front_s1(S, chunks, n, s, ks, causal):
                for k in ks:
                    half, h0, nh, w = chunks[k]
                    if k == 0:
                        pe.wait_ge(S["qTs"].sem, S["qTs"].done(n))
                        pe.wait_ge(S["kTs"].sem, S["kTs"].done(n))
                    if k == 1:
                        pe.wait_ge(S["vs"].sem, S["vs"].done(n))
                    if k >= 2:
                        pe.wait_ge(S["max"].sem, S["max"].done(n, k - 1))
                    pair = 2 * (k % 2)
                    if causal:
                        for b in range(2):
                            v = bank(pair + b)[:, 0:nh // 2 * w].rearrange("p (i w) -> p i w", w=w)[:, :, w - P:w]
                            mm(v, identb[:], maskb[:, 0:nh // 2, :], start=True, stop=False, free=True)
                    for j in range(nh):
                        h = h0 + j
                        i = mm(bank(pair + j % 2)[:, j // 2 * w:(j // 2 + 1) * w], head_rows(QT[s], h)[:, h // 2, half * P:(half + 1) * P],
                               head_rows(QT[s], h)[:, HEADS // 2 + h // 2, 0:w], start=(not causal and j < 2), stop=(j >= nh - 2), free=True)
                    i.then_inc(S["s1"].sem, 1)

            def front_rT(S, n, s):
                pe.wait_ge(S["max"].sem, S["max"].done(n))
                slots_T(bank(1, 2).bitcast(F16), s, range(HEADS // 2)).then_inc(S["rT"].sem, 1)

            def mid_s2(S, chunks, n, s, ks):
                for k in ks:
                    kt, h0, nh, w = chunks[k]
                    if k == 0:
                        pe.wait_ge(S["rTs"].sem, S["rTs"].done(n))
                    if k >= 2:
                        pe.wait_ge(S["exp"].sem, S["exp"].done(n, k - 1))
                    pair = 6 - 2 * (k % 2)
                    for j in range(nh):
                        h = h0 + j
                        i = mm(bank(pair + j % 2)[:, j // 2 * w:(j // 2 + 1) * w], head_rows(QT[s], h)[:, HEADS // 2 + h // 2, kt * P:(kt + 1) * P],
                               head_rows(QT[s], h)[:, h // 2, TOKENS - w:TOKENS], start=(j < 2), stop=(j >= nh - 2), free=True)
                    i.then_inc(S["s2"].sem, 1)

            def mid_pv(S, n, s, w1_, g, kts=(0, 1)):
                for kt in kts:
                    w = w1_ if kt else TOKENS
                    for j in range(4):
                        i = mm(bank(4, 2)[32 * j:32 * j + 32, g * TOKENS + TOKENS - w:(g + 1) * TOKENS], VA[s][:, kt, 4 * g + j, :],
                               PT[s][:, 4 * g + j, kt * TOKENS:kt * TOKENS + w], start=(kt == 0 and g != 1), stop=(kt == 1), free=True)
                if g == GROUPS - 1 and kts[-1] == 1:
                    i.then_inc(S["o"].sem, 1)

            def mid_tokens(S, n, s):
                pe.wait_ge(S["or"].sem, S["or"].done(n))
                for h in range(HALVES):
                    for g in range(GROUPS):
                        i = nc.tensor.transpose(bank(4 + h)[:, g * P:(g + 1) * P], OR[s][:, g, h * P:(h + 1) * P], ident[:])
                i.then_inc(S["ot"].sem, 1)

            def router(S, n, s):
                pe.wait_ge(S["x3Ts"].sem, S["x3Ts"].done(n))
                pe.wait_ge(S["lgs"].sem, S["lgs"].done(n - 1))
                for h in range(HALVES):
                    for c in range(2):
                        i = mm(bank(7)[:, h * EXPERTS:(h + 1) * EXPERTS], x3T[s][:, c, h * P:(h + 1) * P], wrout[:, c, :],
                               start=(c == 0), stop=(c == 1))
                i.then_inc(S["lg"].sem, 1)

            def choice_rows(g):
                a, b = GROUP_SEQS[g]
                pe.wait_ge(t_sig, g * routed + probs_made)
                for h in range(HALVES):
                    i = nc.tensor.transpose(bank(0)[0:(b - a) * EXPERTS, h * P:(h + 1) * P], PR[:, h, a:b].rearrange("p a b -> p (a b)"), ident[:])
                i.then_inc(t_pe, 1)

            def choice_tokens(g):
                n_rows = (GROUP_SEQS[g][1] - GROUP_SEQS[g][0]) * EXPERTS
                pe.wait_ge(t_sig, g * routed + rows_chosen)
                for h in range(HALVES):
                    i = nc.tensor.transpose(bank(CHOICE_BANK[g])[:, h * n_rows:(h + 1) * n_rows], chosen[0:n_rows, h * P:(h + 1) * P],
                                            ident[0:n_rows, 0:n_rows])
                i.then_inc(t_pe, 1)

            def causal_step(soon, new, mid, back):
                S = B_
                W = W_B
                if back:
                    n, s = back
                    pe.wait_ge(S["o2s"].sem, S["o2s"].done(n))
                    for h in range(HALVES):
                        for c in range(2):
                            i = mm(bank(3)[:, h * DIM:(h + 1) * DIM], OT[s][:, c, h * P:(h + 1) * P], wproj[:, c, :],
                                   start=(c == 0), stop=(c == 1))
                    i.then_inc(S["pj"].sem, 1)
                if mid:
                    n, s = mid
                    pe.wait_ge(S["lgs"].sem, S["lgs"].freed(n))
                    mid_s2(S, CAUSAL2, n, s, (0,))
                if new and not first(new):
                    front_product(S, *new, *W, 0)
                if mid:
                    mid_s2(S, CAUSAL2, *mid, (1,))
                if new and not first(new):
                    front_product(S, *new, *W, 1)
                if mid:
                    mid_s2(S, CAUSAL2, *mid, (2,))
                if back:
                    n, s = back
                    pe.wait_ge(S["h2"].sem, S["h2"].done(n))
                if new:
                    front_product(S, *new, *W, 2)
                if mid:
                    mid_s2(S, CAUSAL2, *mid, (3,))
                if new:
                    front_T(S, *new)
                if mid:
                    mid_s2(S, CAUSAL2, *mid, (4,))
                    n, s = mid
                    if isinstance(n, int) and n == SEQS - 1:
                        choice_rows(0)
                    pe.wait_ge(S["exp"].sem, S["exp"].done(n, 4))
                    pe.wait_ge(S["cut"].sem, S["cut"].done(n, 1))
                    for g in (0, 1):
                        mid_pv(S, n, s, P, g, (0,))
                if new:
                    front_s1(S, CAUSAL1, *new, (0,), True)
                if mid:
                    mid_pv(S, *mid, P, 2, (0,))
                if new:
                    front_s1(S, CAUSAL1, *new, (1,), True)
                if mid:
                    n, s = mid
                    pe.wait_ge(S["exp"].sem, S["exp"].done(n))
                if mid:
                    n, s = mid
                    pe.wait_ge(S["cut"].sem, S["cut"].done(n))
                for g in range(GROUPS):
                    if mid:
                        mid_pv(S, *mid, P, g, (1,))
                    if new:
                        front_s1(S, CAUSAL1, *new, (2 + g,), True)
                if back:
                    n, s = back
                    transposes(bank(6), x3[s], CH, S["x3"], n, S["x3T"])
                if mid:
                    mid_tokens(S, *mid)
                if soon and not first(soon):
                    x_transposes(S, *soon, 4)
                if new:
                    front_rT(S, *new)
                if back:
                    n, s = back
                    pe.wait_ge(S["x3Ts"].sem, S["x3Ts"].done(n))
                if mid:
                    n, s = mid
                    transposes(bank(6), ON[s], CH, S["on"], n, S["o2"])
                if back:
                    router(S, *back)

            pipeline(pe, causal_step, 4, late={2: lambda: pe.wait_ge(a_ss2.sem, a_ss2.done(SEQS - 1))})()

            choice_tokens(0)

            def mid_hidden(S, n, s, k, follows):
                if k == 0:
                    pe.wait_ge(S["vs"].sem, S["vs"].done(n + 1) if follows else S["vs"].done(n))
                if k == 1:
                    pe.wait_ge(S["exp"].sem, S["exp"].done(n, 5))
                for m in (2 * k, 2 * k + 1):
                    for i_, (kx, kw, K) in enumerate(BIASED):
                        i = mm(bank((3, 6, 7)[k])[:, m % 2 * TOKENS:(m % 2 + 1) * TOKENS], w1[0:K, kw, m * P:(m + 1) * P],
                               xT[s][0:K, kx, :], start=(i_ == 0), stop=(i_ == len(BIASED) - 1))
                i.then_inc(S["hm"].sem, 1)

            def back_fc2(S, n, s, h, parts=(0, 1)):
                tok, out = slice(h * P, (h + 1) * P), bank(7)[:, h * DIM:(h + 1) * DIM]
                if 0 in parts:
                    for k in range(HT):
                        mm(out, hidh[s][:, k, tok], w2h[:, k, :], start=(k == 0), stop=False)
                        i = mm(out, hidl[s][:, k, tok], w2h[:, k, :], start=False, stop=False)
                if 1 in parts:
                    for k in range(HT):
                        mm(out, hidh[s][:, k, tok], w2l[:, k, :], start=False, stop=False)
                    for c in range(2):
                        i = mm(out, OT[s][:, c, tok], w2o[:, c, :], start=False, stop=(c == 1))
                return i

            def ffn_step(soon, new, mid, back):
                S = C_
                W = (w1, HIDDEN, BIASED)
                if new:
                    front_product(S, *new, *W, 0)
                if mid:
                    n, s = mid
                    pe.wait_ge(S["zb"].sem, S["zb"].freed(n))
                    pe.wait_ge(S["o2s"].sem, S["o2s"].done(n - 1))
                    mid_s2(S, FULL, n, s, (0,))
                if new:
                    front_product(S, *new, *W, 1)
                if mid:
                    mid_s2(S, FULL, *mid, (1,))
                if new:
                    front_product(S, *new, *W, 2)
                if mid:
                    mid_s2(S, FULL, *mid, (2,))
                if new:
                    front_T(S, *new)
                if mid:
                    mid_s2(S, FULL, *mid, (3, 4))
                    mid_hidden(S, *mid, 0, bool(new))
                    mid_s2(S, FULL, *mid, (5,))
                if new:
                    front_s1(S, FULL, *new, (0,), False)
                if mid:
                    mid_hidden(S, *mid, 1, bool(new))
                    mid_hidden(S, *mid, 2, bool(new))
                    n, s = mid
                    pe.wait_ge(S["exp"].sem, S["exp"].done(n))
                    mid_pv(S, n, s, TOKENS, 0)
                    pe.wait_ge(S["hf"].sem, S["hf"].done(n, 1))
                for g in range(GROUPS):
                    if new:
                        front_s1(S, FULL, *new, (1 + g,), False)
                    if mid and g < 2:
                        mid_pv(S, *mid, TOKENS, 1 + g)
                if new:
                    front_s1(S, FULL, *new, (4,), False)
                if back:
                    n, s = back
                    if mid:
                        pe.wait_ge(S["hf"].sem, S["hf"].done(n + 1))
                    pe.wait_ge(S["hl"].sem, S["hl"].done(n))
                    pe.wait_ge(S["o2s"].sem, S["o2s"].done(n))
                    pe.wait_ge(S["zb"].sem, S["zb"].done(n - 1))
                    back_fc2(S, n, s, 0)
                if new:
                    front_s1(S, FULL, *new, (5,), False)
                if mid:
                    mid_tokens(S, *mid)
                if back:
                    back_fc2(S, *back, 1, (0,))
                if soon:
                    x_transposes(S, *soon, 4)
                if new:
                    front_rT(S, *new)
                if new and isinstance(new[0], int) and new[0] == 2:
                    choice_tokens(1)
                if back:
                    back_fc2(S, *back, 1, (1,)).then_inc(S["z"].sem, 1)
                if mid:
                    n, s = mid
                    pe.wait_ge(S["hf"].sem, S["hf"].done(n))
                    transposes(bank(6), ON[s], CH, S["on"], n, S["o2"])

            def second_choice_rows():
                pe.wait_ge(C_["xTs"].sem, C_["xTs"].done(0))
                choice_rows(1)

            pe.wait_ge(ld_ffn, 3 * 16)
            pe.wait_ge(pre_ffn, 6)
            pe.wait_ge(weights_hi, 10)
            pipeline(pe, ffn_step, 4, late={1: second_choice_rows})()


def kernel(**inputs):
    import numpy as np
    import concourse.bacc as bacc
    from concourse.bass_utils import run_bass_kernel_spmd

    a = {k: np.asarray(v) for k, v in inputs.items()}
    tok = lambda k: a["L0_tok_" + k]

    def rows(w):
        return np.ascontiguousarray(w.reshape(-1, P, w.shape[-1]).transpose(1, 0, 2))

    def aug(w, b):
        return rows(np.concatenate([w, b[None]], 0).T)

    def halves(w):
        out = np.zeros((w.shape[0] - CH, 2, w.shape[1]), w.dtype)
        out[:CH, 0] = w[:CH]
        out[:, 1] = w[CH:]
        return out

    def second(w):
        out = np.zeros((P, HT + 2, w.shape[1]), w.dtype)
        out[:, :HT] = rows(w[:HIDDEN])
        out[:CH, HT:] = halves(w[HIDDEN:])
        return out

    def tiled(w, bias=None):
        a, b = w[:P], w[P:]
        tiles = [a, np.concatenate([b, b], 0)]
        if bias is not None:
            tiles.append(np.concatenate([b, bias[None], bias[None], np.zeros((P - TAIL - 2, w.shape[1]), w.dtype)], 0))
        return np.stack(tiles, 1)

    f = np.float32
    ang = np.arange(TOKENS, dtype=f)[:, None] / np.power(f(10000.0), np.arange(DIM, dtype=f)[None] / f(DIM)).astype(f)
    pos = np.where((np.arange(DIM) % 2 == 0)[None], np.sin(ang), np.cos(ang)).astype(f)
    causal = np.where(np.arange(P)[None, :] <= np.arange(P)[:, None], f(0), f(MASKED)).astype(f)
    w2 = a["L0_ffn_w2"]
    split2 = [second(w.T) for w in (w2[:DIM], w2[DIM:])]
    arrays = {
        "idx": np.ascontiguousarray(a["x"].reshape(SEQS * HALVES, P).T),
        "emb": tok("emb"),
        "pos": np.ascontiguousarray(pos.reshape(HALVES, P, DIM).transpose(1, 0, 2)),
        "ident": np.eye(P, dtype=f),
        "mask": causal,
        "fold_l": np.stack([aug(tok("W" + k), tok("b" + k)) for k in ("q", "k", "v", "1")], 1),
        "fold_r": np.stack([rows(tok("Wo")), rows(tok("W2"))], 1),
        "bias_r": np.stack([tok("bo"), tok("b2")])[None],
        "e_last": np.eye(DIM + 1, dtype=f)[DIM:],
        "ln1_w": tok("ln1_w"), "ln1_b": tok("ln1_b"), "ln2_w": tok("ln2_w"), "ln2_b": tok("ln2_b"),
        "wqkv": tiled(a["L0_attn_W_qkv"].T),
        "wproj": halves(a["L0_attn_W_proj"].T),
        "wrout": halves(a["L0_ffn_w_router"].T),
        "w1": tiled(a["L0_ffn_w1"].T, a["L0_ffn_b1"]),
        "w2": np.stack(split2, 1),
        "b2": a["L0_ffn_b2"].reshape(2, DIM),
        "gamma": a["L0_ffn_gamma1"], "beta": a["L0_ffn_beta1"],
    }
    arrays = {k: np.ascontiguousarray(v) for k, v in arrays.items()}
    nc = bacc.Bacc("TRN2", target_bir_lowering=False, num_devices=1)
    d = {k: nc.dram_tensor("in_" + k, v.shape, mybir.dt.from_np(v.dtype), kind="ExternalInput").ap() for k, v in arrays.items()}
    d["out"] = nc.dram_tensor("out", (SEQS, TOKENS, DIM), F32, kind="ExternalOutput").ap()
    build(nc, d)
    r = run_bass_kernel_spmd(nc, [{"in_" + k: v for k, v in arrays.items()}], core_ids=[0])
    return r.results[0]["out"]
```
